# Optimizing a Trainium2 kernel written in Bass

```python
import numpy as np
import jax
import jax.numpy as jnp

def _softmax(x, axis=-1):
    return jax.nn.softmax(x, axis=axis)

def _gelu(x):
    return jax.nn.gelu(x, approximate=True)

def _silu(x):
    return jax.nn.silu(x)

def _sigmoid(x):
    return jax.nn.sigmoid(x)

def _layernorm(x, axis=-1, eps=1e-05):
    m = jnp.mean(x, axis=axis, keepdims=True)
    v = jnp.var(x, axis=axis, keepdims=True)
    return (x - m) / jnp.sqrt(v + eps)

def _scatter_add(tgt, idx, src, axis=0):
    return tgt.at[idx].add(src)

def _segment_sum(src, seg, n):
    return jax.ops.segment_sum(src, seg, n)
kernel_name = 'mk_xattn_seq_d4_seqx_r8_687a22'

def setup_inputs(seed: int=0):
    np.random.seed(seed)
    _w = jnp.asarray

    def _rec_inputs():
        import jax
        import jax.numpy as jnp
        _rk = jax.random.key(seed)
        x = -0.0005146 + 1 * jax.random.normal(jax.random.fold_in(_rk, 1), (4, 256, 256), jnp.float32)
        _lenS = 256 - jax.random.randint(jax.random.fold_in(_rk, 7), (4,), 0, max(1, 256 // 4) + 1, jnp.int32)
        _lenS2 = 64 - jax.random.randint(jax.random.fold_in(_rk, 8), (4,), 0, max(1, 64 // 4) + 1, jnp.int32)
        _ctx_2048P = jax.random.normal(jax.random.fold_in(_rk, 11), (4, 16, 256), jnp.float32)
        _ctx_2048c = jax.random.dirichlet(jax.random.fold_in(_rk, 511), 0.3 * jnp.ones((16,), jnp.float32), (4, 64))
        _ctx_2048t = jnp.einsum('bsk,bkd->bsd', _ctx_2048c, _ctx_2048P)
        _ctx_2048t = _ctx_2048t * jax.lax.rsqrt(jnp.mean(jnp.square(_ctx_2048t)) + 1e-12) * 0.953939
        ctx_2048 = -0.000392918 + 0.999932 * (_ctx_2048t + 0.3 * jax.random.normal(jax.random.fold_in(_rk, 611), (4, 64, 256), jnp.float32))
        _validS = jnp.arange(256)[None, :] < _lenS[:, None]
        _validS2 = jnp.arange(64)[None, :] < _lenS2[:, None]
        _causal = jnp.tril(jnp.ones((256, 256), dtype=bool))
        mask_BxS2_ik0 = jnp.where(jnp.broadcast_to(_validS2[:, :], (4, 64)), 0, 1).astype(jnp.int32)
        mask_BxS2_bf1 = jnp.ones((4, 64), dtype=bool)
        return (x, ctx_2048, mask_BxS2_ik0, mask_BxS2_bf1)
    x, ctx_2048, mask_BxS2_ik0, mask_BxS2_bf1 = _rec_inputs()

    def _L0_xattn_setup():
        import jax, jax.numpy as jnp
        import numpy as np
        B, P, K, H, NH = (4, 256, 32, 256, 16)
        DH = H // NH
        EPS = 1e-06

        def rmsnorm(x, w):
            var = jnp.mean(jnp.square(x), axis=-1, keepdims=True)
            return x * jax.lax.rsqrt(var + EPS) * w
        key = jax.random.key(seed)
        ks = jax.random.split(key, 12)
        s = 0.02
        return {'x': jax.random.normal(ks[0], (B, P, H), jnp.float32), 'latents': jax.random.normal(ks[1], (B, K, H), jnp.float32), 'attention_mask': jax.random.randint(ks[2], (B, P), 0, 2, jnp.int32), 'q_w': s * jax.random.normal(ks[3], (H, H), jnp.float32), 'q_b': jnp.zeros((H,), jnp.float32), 'kv_w': s * jax.random.normal(ks[4], (H, 2 * H), jnp.float32), 'kv_b': jnp.zeros((2 * H,), jnp.float32), 'out_w': s * jax.random.normal(ks[5], (H, H), jnp.float32), 'out_b': jnp.zeros((H,), jnp.float32), 'postnorm_w': jnp.ones((H,), jnp.float32), 'mlp_w1': s * jax.random.normal(ks[6], (H, 4 * H), jnp.float32), 'mlp_b1': jnp.zeros((4 * H,), jnp.float32), 'mlp_w2': s * jax.random.normal(ks[7], (4 * H, H), jnp.float32), 'mlp_b2': jnp.zeros((H,), jnp.float32)}
    _L0_xattn_all = _L0_xattn_setup()
    _L0_xattn_in = {k: v for k, v in _L0_xattn_all.items() if k in ('q_w', 'q_b', 'kv_w', 'kv_b', 'out_w', 'out_b', 'postnorm_w', 'mlp_w1', 'mlp_b1', 'mlp_w2', 'mlp_b2')}
    del _L0_xattn_all

    def _L1_xattn_setup():
        import jax, jax.numpy as jnp
        import numpy as np
        B, Q, S1, S2 = (4, 32, 256, 256)
        D, H, K, F = (256, 16, 128, 1024)
        LN_EPS = 1e-05

        def _layer_norm(x, scale, offset):
            mu = jnp.mean(x, axis=-1, keepdims=True)
            var = jnp.var(x, axis=-1, keepdims=True)
            return (x - mu) * jax.lax.rsqrt(var + LN_EPS) * scale + offset

        def _cross_attention(q_in, kv_in, wq, bq, wk, bk, wv, bv, wo, bo, bias_k, bias_v):
            b, q_len, _ = q_in.shape
            t = kv_in.shape[1]
            qh = (q_in @ wq + bq).reshape(b, q_len, H, K)
            kh = (kv_in @ wk + bk).reshape(b, t, H, K)
            vh = (kv_in @ wv + bv).reshape(b, t, H, K)
            kh = jnp.concatenate([kh, jnp.broadcast_to(bias_k, (b, 1, H, K))], axis=1)
            vh = jnp.concatenate([vh, jnp.broadcast_to(bias_v, (b, 1, H, K))], axis=1)
            scale = jnp.sqrt(jnp.asarray(K, q_in.dtype))
            logits = jnp.einsum('bqhk,bthk->bhqt', qh, kh) / scale
            weights = jax.nn.softmax(logits, axis=-1)
            ctx = jnp.einsum('bhqt,bthk->bqhk', weights, vh).reshape(b, q_len, H * K)
            return ctx @ wo + bo

        def _forward(x, xf_1, xf_2, ln1_scale, ln1_offset, wq1, bq1, wk1, bk1, wv1, bv1, wo1, bo1, bias_k1, bias_v1, ln2_scale, ln2_offset, wq2, bq2, wk2, bk2, wv2, bv2, wo2, bo2, bias_k2, bias_v2, ln_mlp_scale, ln_mlp_offset, w_fc1, b_fc1, w_fc2, b_fc2):
            res = x
            h = _layer_norm(x, ln1_scale, ln1_offset)
            x = res + _cross_attention(h, xf_1, wq1, bq1, wk1, bk1, wv1, bv1, wo1, bo1, bias_k1, bias_v1)
            res = x
            h = _layer_norm(x, ln2_scale, ln2_offset)
            x = res + _cross_attention(h, xf_2, wq2, bq2, wk2, bk2, wv2, bv2, wo2, bo2, bias_k2, bias_v2)
            h = _layer_norm(x, ln_mlp_scale, ln_mlp_offset)
            h = jax.nn.gelu(h @ w_fc1 + b_fc1, approximate=False) @ w_fc2 + b_fc2
            return x + h
        key = jax.random.key(seed)
        ks = iter(jax.random.split(key, 64))

        def rn(shape, s=0.02):
            return jax.random.normal(next(ks), shape, jnp.float32) * s
        inp = {'x': rn((B, Q, D), 1.0), 'xf_1': rn((B, S1, D), 1.0), 'xf_2': rn((B, S2, D), 1.0)}
        for i in (1, 2):
            inp[f'ln{i}_scale'] = jnp.ones((D,), jnp.float32)
            inp[f'ln{i}_offset'] = jnp.zeros((D,), jnp.float32)
            inp[f'wq{i}'] = rn((D, H * K))
            inp[f'bq{i}'] = jnp.zeros((H * K,), jnp.float32)
            inp[f'wk{i}'] = rn((D, H * K))
            inp[f'bk{i}'] = jnp.zeros((H * K,), jnp.float32)
            inp[f'wv{i}'] = rn((D, H * K))
            inp[f'bv{i}'] = jnp.zeros((H * K,), jnp.float32)
            inp[f'wo{i}'] = rn((H * K, D))
            inp[f'bo{i}'] = jnp.zeros((D,), jnp.float32)
            inp[f'bias_k{i}'] = rn((1, 1, H, K))
            inp[f'bias_v{i}'] = rn((1, 1, H, K))
        inp['ln_mlp_scale'] = jnp.ones((D,), jnp.float32)
        inp['ln_mlp_offset'] = jnp.zeros((D,), jnp.float32)
        inp['w_fc1'] = rn((D, F))
        inp['b_fc1'] = jnp.zeros((F,), jnp.float32)
        inp['w_fc2'] = rn((F, D))
        inp['b_fc2'] = jnp.zeros((D,), jnp.float32)
        return inp
    _L1_xattn_all = _L1_xattn_setup()
    _L1_xattn_in = {k: v for k, v in _L1_xattn_all.items() if k in ('ln1_scale', 'ln1_offset', 'wq1', 'bq1', 'wk1', 'bk1', 'wv1', 'bv1', 'wo1', 'bo1', 'bias_k1', 'bias_v1', 'ln2_scale', 'ln2_offset', 'wq2', 'bq2', 'wk2', 'bk2', 'wv2', 'bv2', 'wo2', 'bo2', 'bias_k2', 'bias_v2', 'ln_mlp_scale', 'ln_mlp_offset', 'w_fc1', 'b_fc1', 'w_fc2', 'b_fc2')}
    del _L1_xattn_all

    def _L2_xattn_setup():
        import jax, jax.numpy as jnp
        import numpy as np
        D = 256
        H = 16
        HD = D // H
        INNER = 4 * D
        EPS = 1e-05

        def layer_norm(x, w, b):
            mu = jnp.mean(x, axis=-1, keepdims=True)
            var = jnp.mean(jnp.square(x - mu), axis=-1, keepdims=True)
            return (x - mu) * jax.lax.rsqrt(var + EPS) * w + b
        key = jax.random.key(seed)
        ks = jax.random.split(key, 12)
        B, LQ, LK = (4, 128, 256)
        std = 0.02
        inp = {'hidden_states': jax.random.normal(ks[0], (B, LQ, D), jnp.float32), 'encoder_hidden_states': jax.random.normal(ks[1], (B, LK, D), jnp.float32), 'encoder_attention_mask': jnp.ones((B, LK), dtype=bool), 'ln1_w': jnp.ones((D,), jnp.float32), 'ln1_b': jnp.zeros((D,), jnp.float32), 'q_w': jax.random.normal(ks[2], (D, D), jnp.float32) * std, 'q_b': jnp.zeros((D,), jnp.float32), 'k_w': jax.random.normal(ks[3], (D, D), jnp.float32) * std, 'k_b': jnp.zeros((D,), jnp.float32), 'v_w': jax.random.normal(ks[4], (D, D), jnp.float32) * std, 'v_b': jnp.zeros((D,), jnp.float32), 'cproj_w': jax.random.normal(ks[5], (D, D), jnp.float32) * std, 'cproj_b': jnp.zeros((D,), jnp.float32), 'ln2_w': jnp.ones((D,), jnp.float32), 'ln2_b': jnp.zeros((D,), jnp.float32), 'fc_w': jax.random.normal(ks[6], (D, INNER), jnp.float32) * std, 'fc_b': jnp.zeros((INNER,), jnp.float32), 'proj_w': jax.random.normal(ks[7], (INNER, D), jnp.float32) * std, 'proj_b': jnp.zeros((D,), jnp.float32)}
        return inp
    _L2_xattn_all = _L2_xattn_setup()
    _L2_xattn_in = {k: v for k, v in _L2_xattn_all.items() if k in ('ln1_w', 'ln1_b', 'q_w', 'q_b', 'k_w', 'k_b', 'v_w', 'v_b', 'cproj_w', 'cproj_b', 'ln2_w', 'ln2_b', 'fc_w', 'fc_b', 'proj_w', 'proj_b')}
    del _L2_xattn_all

    def _L3_xattn_setup():
        import jax, jax.numpy as jnp
        import numpy as np
        B, Q, S1, S2 = (4, 32, 256, 256)
        D, H, K, F = (256, 16, 128, 1024)
        LN_EPS = 1e-05

        def _layer_norm(x, scale, offset):
            mu = jnp.mean(x, axis=-1, keepdims=True)
            var = jnp.var(x, axis=-1, keepdims=True)
            return (x - mu) * jax.lax.rsqrt(var + LN_EPS) * scale + offset

        def _cross_attention(q_in, kv_in, wq, bq, wk, bk, wv, bv, wo, bo, bias_k, bias_v):
            b, q_len, _ = q_in.shape
            t = kv_in.shape[1]
            qh = (q_in @ wq + bq).reshape(b, q_len, H, K)
            kh = (kv_in @ wk + bk).reshape(b, t, H, K)
            vh = (kv_in @ wv + bv).reshape(b, t, H, K)
            kh = jnp.concatenate([kh, jnp.broadcast_to(bias_k, (b, 1, H, K))], axis=1)
            vh = jnp.concatenate([vh, jnp.broadcast_to(bias_v, (b, 1, H, K))], axis=1)
            scale = jnp.sqrt(jnp.asarray(K, q_in.dtype))
            logits = jnp.einsum('bqhk,bthk->bhqt', qh, kh) / scale
            weights = jax.nn.softmax(logits, axis=-1)
            ctx = jnp.einsum('bhqt,bthk->bqhk', weights, vh).reshape(b, q_len, H * K)
            return ctx @ wo + bo

        def _forward(x, xf_1, xf_2, ln1_scale, ln1_offset, wq1, bq1, wk1, bk1, wv1, bv1, wo1, bo1, bias_k1, bias_v1, ln2_scale, ln2_offset, wq2, bq2, wk2, bk2, wv2, bv2, wo2, bo2, bias_k2, bias_v2, ln_mlp_scale, ln_mlp_offset, w_fc1, b_fc1, w_fc2, b_fc2):
            res = x
            h = _layer_norm(x, ln1_scale, ln1_offset)
            x = res + _cross_attention(h, xf_1, wq1, bq1, wk1, bk1, wv1, bv1, wo1, bo1, bias_k1, bias_v1)
            res = x
            h = _layer_norm(x, ln2_scale, ln2_offset)
            x = res + _cross_attention(h, xf_2, wq2, bq2, wk2, bk2, wv2, bv2, wo2, bo2, bias_k2, bias_v2)
            h = _layer_norm(x, ln_mlp_scale, ln_mlp_offset)
            h = jax.nn.gelu(h @ w_fc1 + b_fc1, approximate=False) @ w_fc2 + b_fc2
            return x + h
        key = jax.random.key(seed)
        ks = iter(jax.random.split(key, 64))

        def rn(shape, s=0.02):
            return jax.random.normal(next(ks), shape, jnp.float32) * s
        inp = {'x': rn((B, Q, D), 1.0), 'xf_1': rn((B, S1, D), 1.0), 'xf_2': rn((B, S2, D), 1.0)}
        for i in (1, 2):
            inp[f'ln{i}_scale'] = jnp.ones((D,), jnp.float32)
            inp[f'ln{i}_offset'] = jnp.zeros((D,), jnp.float32)
            inp[f'wq{i}'] = rn((D, H * K))
            inp[f'bq{i}'] = jnp.zeros((H * K,), jnp.float32)
            inp[f'wk{i}'] = rn((D, H * K))
            inp[f'bk{i}'] = jnp.zeros((H * K,), jnp.float32)
            inp[f'wv{i}'] = rn((D, H * K))
            inp[f'bv{i}'] = jnp.zeros((H * K,), jnp.float32)
            inp[f'wo{i}'] = rn((H * K, D))
            inp[f'bo{i}'] = jnp.zeros((D,), jnp.float32)
            inp[f'bias_k{i}'] = rn((1, 1, H, K))
            inp[f'bias_v{i}'] = rn((1, 1, H, K))
        inp['ln_mlp_scale'] = jnp.ones((D,), jnp.float32)
        inp['ln_mlp_offset'] = jnp.zeros((D,), jnp.float32)
        inp['w_fc1'] = rn((D, F))
        inp['b_fc1'] = jnp.zeros((F,), jnp.float32)
        inp['w_fc2'] = rn((F, D))
        inp['b_fc2'] = jnp.zeros((D,), jnp.float32)
        return inp
    _L3_xattn_all = _L3_xattn_setup()
    _L3_xattn_in = {k: v for k, v in _L3_xattn_all.items() if k in ('ln1_scale', 'ln1_offset', 'wq1', 'bq1', 'wk1', 'bk1', 'wv1', 'bv1', 'wo1', 'bo1', 'bias_k1', 'bias_v1', 'ln2_scale', 'ln2_offset', 'wq2', 'bq2', 'wk2', 'bk2', 'wv2', 'bv2', 'wo2', 'bo2', 'bias_k2', 'bias_v2', 'ln_mlp_scale', 'ln_mlp_offset', 'w_fc1', 'b_fc1', 'w_fc2', 'b_fc2')}
    del _L3_xattn_all
    return {'x': x, 'ctx_2048': ctx_2048, 'mask_BxS2_ik0': mask_BxS2_ik0, 'mask_BxS2_bf1': mask_BxS2_bf1, 'L0_xattn_q_w': _L0_xattn_in['q_w'], 'L0_xattn_q_b': _L0_xattn_in['q_b'], 'L0_xattn_kv_w': _L0_xattn_in['kv_w'], 'L0_xattn_kv_b': _L0_xattn_in['kv_b'], 'L0_xattn_out_w': _L0_xattn_in['out_w'], 'L0_xattn_out_b': _L0_xattn_in['out_b'], 'L0_xattn_postnorm_w': _L0_xattn_in['postnorm_w'], 'L0_xattn_mlp_w1': _L0_xattn_in['mlp_w1'], 'L0_xattn_mlp_b1': _L0_xattn_in['mlp_b1'], 'L0_xattn_mlp_w2': _L0_xattn_in['mlp_w2'], 'L0_xattn_mlp_b2': _L0_xattn_in['mlp_b2'], 'L1_xattn_ln1_scale': _L1_xattn_in['ln1_scale'], 'L1_xattn_ln1_offset': _L1_xattn_in['ln1_offset'], 'L1_xattn_wq1': _L1_xattn_in['wq1'], 'L1_xattn_bq1': _L1_xattn_in['bq1'], 'L1_xattn_wk1': _L1_xattn_in['wk1'], 'L1_xattn_bk1': _L1_xattn_in['bk1'], 'L1_xattn_wv1': _L1_xattn_in['wv1'], 'L1_xattn_bv1': _L1_xattn_in['bv1'], 'L1_xattn_wo1': _L1_xattn_in['wo1'], 'L1_xattn_bo1': _L1_xattn_in['bo1'], 'L1_xattn_bias_k1': _L1_xattn_in['bias_k1'], 'L1_xattn_bias_v1': _L1_xattn_in['bias_v1'], 'L1_xattn_ln2_scale': _L1_xattn_in['ln2_scale'], 'L1_xattn_ln2_offset': _L1_xattn_in['ln2_offset'], 'L1_xattn_wq2': _L1_xattn_in['wq2'], 'L1_xattn_bq2': _L1_xattn_in['bq2'], 'L1_xattn_wk2': _L1_xattn_in['wk2'], 'L1_xattn_bk2': _L1_xattn_in['bk2'], 'L1_xattn_wv2': _L1_xattn_in['wv2'], 'L1_xattn_bv2': _L1_xattn_in['bv2'], 'L1_xattn_wo2': _L1_xattn_in['wo2'], 'L1_xattn_bo2': _L1_xattn_in['bo2'], 'L1_xattn_bias_k2': _L1_xattn_in['bias_k2'], 'L1_xattn_bias_v2': _L1_xattn_in['bias_v2'], 'L1_xattn_ln_mlp_scale': _L1_xattn_in['ln_mlp_scale'], 'L1_xattn_ln_mlp_offset': _L1_xattn_in['ln_mlp_offset'], 'L1_xattn_w_fc1': _L1_xattn_in['w_fc1'], 'L1_xattn_b_fc1': _L1_xattn_in['b_fc1'], 'L1_xattn_w_fc2': _L1_xattn_in['w_fc2'], 'L1_xattn_b_fc2': _L1_xattn_in['b_fc2'], 'L2_xattn_ln1_w': _L2_xattn_in['ln1_w'], 'L2_xattn_ln1_b': _L2_xattn_in['ln1_b'], 'L2_xattn_q_w': _L2_xattn_in['q_w'], 'L2_xattn_q_b': _L2_xattn_in['q_b'], 'L2_xattn_k_w': _L2_xattn_in['k_w'], 'L2_xattn_k_b': _L2_xattn_in['k_b'], 'L2_xattn_v_w': _L2_xattn_in['v_w'], 'L2_xattn_v_b': _L2_xattn_in['v_b'], 'L2_xattn_cproj_w': _L2_xattn_in['cproj_w'], 'L2_xattn_cproj_b': _L2_xattn_in['cproj_b'], 'L2_xattn_ln2_w': _L2_xattn_in['ln2_w'], 'L2_xattn_ln2_b': _L2_xattn_in['ln2_b'], 'L2_xattn_fc_w': _L2_xattn_in['fc_w'], 'L2_xattn_fc_b': _L2_xattn_in['fc_b'], 'L2_xattn_proj_w': _L2_xattn_in['proj_w'], 'L2_xattn_proj_b': _L2_xattn_in['proj_b'], 'L3_xattn_ln1_scale': _L3_xattn_in['ln1_scale'], 'L3_xattn_ln1_offset': _L3_xattn_in['ln1_offset'], 'L3_xattn_wq1': _L3_xattn_in['wq1'], 'L3_xattn_bq1': _L3_xattn_in['bq1'], 'L3_xattn_wk1': _L3_xattn_in['wk1'], 'L3_xattn_bk1': _L3_xattn_in['bk1'], 'L3_xattn_wv1': _L3_xattn_in['wv1'], 'L3_xattn_bv1': _L3_xattn_in['bv1'], 'L3_xattn_wo1': _L3_xattn_in['wo1'], 'L3_xattn_bo1': _L3_xattn_in['bo1'], 'L3_xattn_bias_k1': _L3_xattn_in['bias_k1'], 'L3_xattn_bias_v1': _L3_xattn_in['bias_v1'], 'L3_xattn_ln2_scale': _L3_xattn_in['ln2_scale'], 'L3_xattn_ln2_offset': _L3_xattn_in['ln2_offset'], 'L3_xattn_wq2': _L3_xattn_in['wq2'], 'L3_xattn_bq2': _L3_xattn_in['bq2'], 'L3_xattn_wk2': _L3_xattn_in['wk2'], 'L3_xattn_bk2': _L3_xattn_in['bk2'], 'L3_xattn_wv2': _L3_xattn_in['wv2'], 'L3_xattn_bv2': _L3_xattn_in['bv2'], 'L3_xattn_wo2': _L3_xattn_in['wo2'], 'L3_xattn_bo2': _L3_xattn_in['bo2'], 'L3_xattn_bias_k2': _L3_xattn_in['bias_k2'], 'L3_xattn_bias_v2': _L3_xattn_in['bias_v2'], 'L3_xattn_ln_mlp_scale': _L3_xattn_in['ln_mlp_scale'], 'L3_xattn_ln_mlp_offset': _L3_xattn_in['ln_mlp_offset'], 'L3_xattn_w_fc1': _L3_xattn_in['w_fc1'], 'L3_xattn_b_fc1': _L3_xattn_in['b_fc1'], 'L3_xattn_w_fc2': _L3_xattn_in['w_fc2'], 'L3_xattn_b_fc2': _L3_xattn_in['b_fc2']}

def reference(x, ctx_2048, mask_BxS2_ik0, mask_BxS2_bf1, L0_xattn_q_w, L0_xattn_q_b, L0_xattn_kv_w, L0_xattn_kv_b, L0_xattn_out_w, L0_xattn_out_b, L0_xattn_postnorm_w, L0_xattn_mlp_w1, L0_xattn_mlp_b1, L0_xattn_mlp_w2, L0_xattn_mlp_b2, L1_xattn_ln1_scale, L1_xattn_ln1_offset, L1_xattn_wq1, L1_xattn_bq1, L1_xattn_wk1, L1_xattn_bk1, L1_xattn_wv1, L1_xattn_bv1, L1_xattn_wo1, L1_xattn_bo1, L1_xattn_bias_k1, L1_xattn_bias_v1, L1_xattn_ln2_scale, L1_xattn_ln2_offset, L1_xattn_wq2, L1_xattn_bq2, L1_xattn_wk2, L1_xattn_bk2, L1_xattn_wv2, L1_xattn_bv2, L1_xattn_wo2, L1_xattn_bo2, L1_xattn_bias_k2, L1_xattn_bias_v2, L1_xattn_ln_mlp_scale, L1_xattn_ln_mlp_offset, L1_xattn_w_fc1, L1_xattn_b_fc1, L1_xattn_w_fc2, L1_xattn_b_fc2, L2_xattn_ln1_w, L2_xattn_ln1_b, L2_xattn_q_w, L2_xattn_q_b, L2_xattn_k_w, L2_xattn_k_b, L2_xattn_v_w, L2_xattn_v_b, L2_xattn_cproj_w, L2_xattn_cproj_b, L2_xattn_ln2_w, L2_xattn_ln2_b, L2_xattn_fc_w, L2_xattn_fc_b, L2_xattn_proj_w, L2_xattn_proj_b, L3_xattn_ln1_scale, L3_xattn_ln1_offset, L3_xattn_wq1, L3_xattn_bq1, L3_xattn_wk1, L3_xattn_bk1, L3_xattn_wv1, L3_xattn_bv1, L3_xattn_wo1, L3_xattn_bo1, L3_xattn_bias_k1, L3_xattn_bias_v1, L3_xattn_ln2_scale, L3_xattn_ln2_offset, L3_xattn_wq2, L3_xattn_bq2, L3_xattn_wk2, L3_xattn_bk2, L3_xattn_wv2, L3_xattn_bv2, L3_xattn_wo2, L3_xattn_bo2, L3_xattn_bias_k2, L3_xattn_bias_v2, L3_xattn_ln_mlp_scale, L3_xattn_ln_mlp_offset, L3_xattn_w_fc1, L3_xattn_b_fc1, L3_xattn_w_fc2, L3_xattn_b_fc2):
    import jax
    import jax.numpy as jnp

    def _L0_xattn_ref(x, latents, attention_mask, q_w, q_b, kv_w, kv_b, out_w, out_b, postnorm_w, mlp_w1, mlp_b1, mlp_w2, mlp_b2):
        import jax, jax.numpy as jnp
        import numpy as np
        B, P, K, H, NH = (4, 256, 32, 256, 16)
        DH = H // NH
        EPS = 1e-06

        def rmsnorm(x, w):
            var = jnp.mean(jnp.square(x), axis=-1, keepdims=True)
            return x * jax.lax.rsqrt(var + EPS) * w
        b, p, _ = x.shape
        k_len = latents.shape[1]
        residual = latents
        h = jnp.concatenate([x, latents], axis=1)
        q = (latents @ q_w + q_b).reshape(b, k_len, NH, DH)
        kv = (h @ kv_w + kv_b).reshape(b, p + k_len, NH, DH, 2)
        kmat, v = (kv[..., 0], kv[..., 1])
        attn = jnp.einsum('bkhd,bnhd->bhkn', q, kmat) / DH
        full_mask = jnp.concatenate([attention_mask.astype(bool), jnp.ones((b, k_len), bool)], axis=-1)
        attn = jnp.where(full_mask[:, None, None, :], attn, -jnp.inf)
        attn = jax.nn.softmax(attn.astype(jnp.float32), axis=-1).astype(q.dtype)
        attn_out = jnp.einsum('bhkn,bnhd->bkhd', attn, v).reshape(b, k_len, H)
        attn_out = attn_out @ out_w + out_b + residual
        out = rmsnorm(attn_out, postnorm_w)
        out = jax.nn.gelu(out @ mlp_w1 + mlp_b1) @ mlp_w2 + mlp_b2
        return out + residual

    def _L1_xattn_ref(x, xf_1, xf_2, ln1_scale, ln1_offset, wq1, bq1, wk1, bk1, wv1, bv1, wo1, bo1, bias_k1, bias_v1, ln2_scale, ln2_offset, wq2, bq2, wk2, bk2, wv2, bv2, wo2, bo2, bias_k2, bias_v2, ln_mlp_scale, ln_mlp_offset, w_fc1, b_fc1, w_fc2, b_fc2):
        import jax, jax.numpy as jnp
        import numpy as np
        B, Q, S1, S2 = (4, 32, 256, 256)
        D, H, K, F = (256, 16, 128, 1024)
        LN_EPS = 1e-05

        def _layer_norm(x, scale, offset):
            mu = jnp.mean(x, axis=-1, keepdims=True)
            var = jnp.var(x, axis=-1, keepdims=True)
            return (x - mu) * jax.lax.rsqrt(var + LN_EPS) * scale + offset

        def _cross_attention(q_in, kv_in, wq, bq, wk, bk, wv, bv, wo, bo, bias_k, bias_v):
            b, q_len, _ = q_in.shape
            t = kv_in.shape[1]
            qh = (q_in @ wq + bq).reshape(b, q_len, H, K)
            kh = (kv_in @ wk + bk).reshape(b, t, H, K)
            vh = (kv_in @ wv + bv).reshape(b, t, H, K)
            kh = jnp.concatenate([kh, jnp.broadcast_to(bias_k, (b, 1, H, K))], axis=1)
            vh = jnp.concatenate([vh, jnp.broadcast_to(bias_v, (b, 1, H, K))], axis=1)
            scale = jnp.sqrt(jnp.asarray(K, q_in.dtype))
            logits = jnp.einsum('bqhk,bthk->bhqt', qh, kh) / scale
            weights = jax.nn.softmax(logits, axis=-1)
            ctx = jnp.einsum('bhqt,bthk->bqhk', weights, vh).reshape(b, q_len, H * K)
            return ctx @ wo + bo

        def _forward(x, xf_1, xf_2, ln1_scale, ln1_offset, wq1, bq1, wk1, bk1, wv1, bv1, wo1, bo1, bias_k1, bias_v1, ln2_scale, ln2_offset, wq2, bq2, wk2, bk2, wv2, bv2, wo2, bo2, bias_k2, bias_v2, ln_mlp_scale, ln_mlp_offset, w_fc1, b_fc1, w_fc2, b_fc2):
            res = x
            h = _layer_norm(x, ln1_scale, ln1_offset)
            x = res + _cross_attention(h, xf_1, wq1, bq1, wk1, bk1, wv1, bv1, wo1, bo1, bias_k1, bias_v1)
            res = x
            h = _layer_norm(x, ln2_scale, ln2_offset)
            x = res + _cross_attention(h, xf_2, wq2, bq2, wk2, bk2, wv2, bv2, wo2, bo2, bias_k2, bias_v2)
            h = _layer_norm(x, ln_mlp_scale, ln_mlp_offset)
            h = jax.nn.gelu(h @ w_fc1 + b_fc1, approximate=False) @ w_fc2 + b_fc2
            return x + h
        return _forward(x, xf_1, xf_2, ln1_scale, ln1_offset, wq1, bq1, wk1, bk1, wv1, bv1, wo1, bo1, bias_k1, bias_v1, ln2_scale, ln2_offset, wq2, bq2, wk2, bk2, wv2, bv2, wo2, bo2, bias_k2, bias_v2, ln_mlp_scale, ln_mlp_offset, w_fc1, b_fc1, w_fc2, b_fc2)

    def _L2_xattn_ref(hidden_states, encoder_hidden_states, encoder_attention_mask, ln1_w, ln1_b, q_w, q_b, k_w, k_b, v_w, v_b, cproj_w, cproj_b, ln2_w, ln2_b, fc_w, fc_b, proj_w, proj_b):
        import jax, jax.numpy as jnp
        import numpy as np
        D = 256
        H = 16
        HD = D // H
        INNER = 4 * D
        EPS = 1e-05

        def layer_norm(x, w, b):
            mu = jnp.mean(x, axis=-1, keepdims=True)
            var = jnp.mean(jnp.square(x - mu), axis=-1, keepdims=True)
            return (x - mu) * jax.lax.rsqrt(var + EPS) * w + b
        B, LQ, _ = hidden_states.shape
        LK = encoder_hidden_states.shape[1]
        residual = hidden_states
        x = layer_norm(hidden_states, ln1_w, ln1_b)
        q = (x @ q_w + q_b).reshape(B, LQ, H, HD).transpose(0, 2, 1, 3)
        k = (encoder_hidden_states @ k_w + k_b).reshape(B, LK, H, HD).transpose(0, 2, 1, 3)
        v = (encoder_hidden_states @ v_w + v_b).reshape(B, LK, H, HD).transpose(0, 2, 1, 3)
        scale = 1.0 / np.sqrt(HD).astype(np.float32)
        scores = jnp.einsum('bhqd,bhkd->bhqk', q, k) * scale
        mask = encoder_attention_mask[:, None, None, :]
        mask_value = jnp.finfo(scores.dtype).min
        scores = jnp.where(mask, scores, mask_value)
        attn = jax.nn.softmax(scores, axis=-1)
        out = jnp.einsum('bhqk,bhkd->bhqd', attn, v)
        out = out.transpose(0, 2, 1, 3).reshape(B, LQ, D)
        out = out @ cproj_w + cproj_b
        hidden = out + residual
        residual = hidden
        y = layer_norm(hidden, ln2_w, ln2_b)
        y = jax.nn.gelu(y @ fc_w + fc_b, approximate=True)
        y = y @ proj_w + proj_b
        return residual + y

    def _L3_xattn_ref(x, xf_1, xf_2, ln1_scale, ln1_offset, wq1, bq1, wk1, bk1, wv1, bv1, wo1, bo1, bias_k1, bias_v1, ln2_scale, ln2_offset, wq2, bq2, wk2, bk2, wv2, bv2, wo2, bo2, bias_k2, bias_v2, ln_mlp_scale, ln_mlp_offset, w_fc1, b_fc1, w_fc2, b_fc2):
        import jax, jax.numpy as jnp
        import numpy as np
        B, Q, S1, S2 = (4, 32, 256, 256)
        D, H, K, F = (256, 16, 128, 1024)
        LN_EPS = 1e-05

        def _layer_norm(x, scale, offset):
            mu = jnp.mean(x, axis=-1, keepdims=True)
            var = jnp.var(x, axis=-1, keepdims=True)
            return (x - mu) * jax.lax.rsqrt(var + LN_EPS) * scale + offset

        def _cross_attention(q_in, kv_in, wq, bq, wk, bk, wv, bv, wo, bo, bias_k, bias_v):
            b, q_len, _ = q_in.shape
            t = kv_in.shape[1]
            qh = (q_in @ wq + bq).reshape(b, q_len, H, K)
            kh = (kv_in @ wk + bk).reshape(b, t, H, K)
            vh = (kv_in @ wv + bv).reshape(b, t, H, K)
            kh = jnp.concatenate([kh, jnp.broadcast_to(bias_k, (b, 1, H, K))], axis=1)
            vh = jnp.concatenate([vh, jnp.broadcast_to(bias_v, (b, 1, H, K))], axis=1)
            scale = jnp.sqrt(jnp.asarray(K, q_in.dtype))
            logits = jnp.einsum('bqhk,bthk->bhqt', qh, kh) / scale
            weights = jax.nn.softmax(logits, axis=-1)
            ctx = jnp.einsum('bhqt,bthk->bqhk', weights, vh).reshape(b, q_len, H * K)
            return ctx @ wo + bo

        def _forward(x, xf_1, xf_2, ln1_scale, ln1_offset, wq1, bq1, wk1, bk1, wv1, bv1, wo1, bo1, bias_k1, bias_v1, ln2_scale, ln2_offset, wq2, bq2, wk2, bk2, wv2, bv2, wo2, bo2, bias_k2, bias_v2, ln_mlp_scale, ln_mlp_offset, w_fc1, b_fc1, w_fc2, b_fc2):
            res = x
            h = _layer_norm(x, ln1_scale, ln1_offset)
            x = res + _cross_attention(h, xf_1, wq1, bq1, wk1, bk1, wv1, bv1, wo1, bo1, bias_k1, bias_v1)
            res = x
            h = _layer_norm(x, ln2_scale, ln2_offset)
            x = res + _cross_attention(h, xf_2, wq2, bq2, wk2, bk2, wv2, bv2, wo2, bo2, bias_k2, bias_v2)
            h = _layer_norm(x, ln_mlp_scale, ln_mlp_offset)
            h = jax.nn.gelu(h @ w_fc1 + b_fc1, approximate=False) @ w_fc2 + b_fc2
            return x + h
        return _forward(x, xf_1, xf_2, ln1_scale, ln1_offset, wq1, bq1, wk1, bk1, wv1, bv1, wo1, bo1, bias_k1, bias_v1, ln2_scale, ln2_offset, wq2, bq2, wk2, bk2, wv2, bv2, wo2, bo2, bias_k2, bias_v2, ln_mlp_scale, ln_mlp_offset, w_fc1, b_fc1, w_fc2, b_fc2)
    x = _L0_xattn_ref(ctx_2048, x, mask_BxS2_ik0, L0_xattn_q_w, L0_xattn_q_b, L0_xattn_kv_w, L0_xattn_kv_b, L0_xattn_out_w, L0_xattn_out_b, L0_xattn_postnorm_w, L0_xattn_mlp_w1, L0_xattn_mlp_b1, L0_xattn_mlp_w2, L0_xattn_mlp_b2)
    x = _L1_xattn_ref(x, ctx_2048, ctx_2048, L1_xattn_ln1_scale, L1_xattn_ln1_offset, L1_xattn_wq1, L1_xattn_bq1, L1_xattn_wk1, L1_xattn_bk1, L1_xattn_wv1, L1_xattn_bv1, L1_xattn_wo1, L1_xattn_bo1, L1_xattn_bias_k1, L1_xattn_bias_v1, L1_xattn_ln2_scale, L1_xattn_ln2_offset, L1_xattn_wq2, L1_xattn_bq2, L1_xattn_wk2, L1_xattn_bk2, L1_xattn_wv2, L1_xattn_bv2, L1_xattn_wo2, L1_xattn_bo2, L1_xattn_bias_k2, L1_xattn_bias_v2, L1_xattn_ln_mlp_scale, L1_xattn_ln_mlp_offset, L1_xattn_w_fc1, L1_xattn_b_fc1, L1_xattn_w_fc2, L1_xattn_b_fc2)
    x = _L2_xattn_ref(x, ctx_2048, mask_BxS2_bf1, L2_xattn_ln1_w, L2_xattn_ln1_b, L2_xattn_q_w, L2_xattn_q_b, L2_xattn_k_w, L2_xattn_k_b, L2_xattn_v_w, L2_xattn_v_b, L2_xattn_cproj_w, L2_xattn_cproj_b, L2_xattn_ln2_w, L2_xattn_ln2_b, L2_xattn_fc_w, L2_xattn_fc_b, L2_xattn_proj_w, L2_xattn_proj_b)
    x = _L3_xattn_ref(x, ctx_2048, ctx_2048, L3_xattn_ln1_scale, L3_xattn_ln1_offset, L3_xattn_wq1, L3_xattn_bq1, L3_xattn_wk1, L3_xattn_bk1, L3_xattn_wv1, L3_xattn_bv1, L3_xattn_wo1, L3_xattn_bo1, L3_xattn_bias_k1, L3_xattn_bias_v1, L3_xattn_ln2_scale, L3_xattn_ln2_offset, L3_xattn_wq2, L3_xattn_bq2, L3_xattn_wk2, L3_xattn_bk2, L3_xattn_wv2, L3_xattn_bv2, L3_xattn_wo2, L3_xattn_bo2, L3_xattn_bias_k2, L3_xattn_bias_v2, L3_xattn_ln_mlp_scale, L3_xattn_ln_mlp_offset, L3_xattn_w_fc1, L3_xattn_b_fc1, L3_xattn_w_fc2, L3_xattn_b_fc2)
    return x

_drawn_inputs = setup_inputs


def setup_inputs(seed=0):
    import zlib

    import numpy as np

    out = dict(_drawn_inputs(seed))
    spreads = {'L0_xattn_q_b': (0.0, 0.8),
     'L0_xattn_kv_b': (0.0, 0.8),
     'L0_xattn_out_b': (0.0, 0.756),
     'L0_xattn_postnorm_w': (1.0, 0.6),
     'L0_xattn_mlp_b1': (0.0, 0.272),
     'L0_xattn_mlp_b2': (0.0, 0.1),
     'L1_xattn_ln1_scale': (1.0, 0.6),
     'L1_xattn_ln1_offset': (0.0, 0.8),
     'L1_xattn_bq1': (0.0, 0.8),
     'L1_xattn_bk1': (0.0, 2.0),
     'L1_xattn_bv1': (0.0, 0.1),
     'L1_xattn_bo1': (0.0, 0.1),
     'L1_xattn_ln2_scale': (1.0, 0.6),
     'L1_xattn_ln2_offset': (0.0, 0.8),
     'L1_xattn_bq2': (0.0, 0.8),
     'L1_xattn_bk2': (0.0, 2.0),
     'L1_xattn_bv2': (0.0, 0.1),
     'L1_xattn_bo2': (0.0, 0.1),
     'L1_xattn_ln_mlp_scale': (1.0, 0.6),
     'L1_xattn_ln_mlp_offset': (0.0, 0.754),
     'L1_xattn_b_fc1': (0.0, 0.1),
     'L1_xattn_b_fc2': (0.0, 0.1),
     'L2_xattn_ln1_w': (1.0, 0.6),
     'L2_xattn_ln1_b': (0.0, 0.8),
     'L2_xattn_q_b': (0.0, 0.8),
     'L2_xattn_k_b': (0.0, 2.0),
     'L2_xattn_v_b': (0.0, 0.296),
     'L2_xattn_cproj_b': (0.0, 0.1),
     'L2_xattn_ln2_w': (1.0, 0.6),
     'L2_xattn_ln2_b': (0.0, 0.8),
     'L2_xattn_fc_b': (0.0, 0.1),
     'L2_xattn_proj_b': (0.0, 0.1),
     'L3_xattn_ln1_scale': (1.0, 0.6),
     'L3_xattn_ln1_offset': (0.0, 0.8),
     'L3_xattn_bq1': (0.0, 0.8),
     'L3_xattn_bk1': (0.0, 2.0),
     'L3_xattn_bv1': (0.0, 0.1),
     'L3_xattn_bo1': (0.0, 0.1),
     'L3_xattn_ln2_scale': (1.0, 0.6),
     'L3_xattn_ln2_offset': (0.0, 0.8),
     'L3_xattn_bq2': (0.0, 0.8),
     'L3_xattn_bk2': (0.0, 2.0),
     'L3_xattn_bv2': (0.0, 0.1),
     'L3_xattn_bo2': (0.0, 0.1),
     'L3_xattn_ln_mlp_scale': (1.0, 0.6),
     'L3_xattn_ln_mlp_offset': (0.0, 0.8),
     'L3_xattn_b_fc1': (0.0, 0.281),
     'L3_xattn_b_fc2': (0.0, 0.1)}
    factors = {'L0_xattn_q_w': 8.0,
     'L0_xattn_kv_w': 8.0,
     'L0_xattn_out_w': 8.0,
     'L1_xattn_wq1': 8.0,
     'L1_xattn_wk1': 8.0,
     'L1_xattn_bias_k1': 64.0,
     'L1_xattn_bias_v1': 56.335,
     'L1_xattn_wq2': 8.0,
     'L1_xattn_wk2': 8.0,
     'L1_xattn_bias_k2': 64.0,
     'L1_xattn_bias_v2': 64.0,
     'L2_xattn_q_w': 8.0,
     'L2_xattn_k_w': 8.0,
     'L3_xattn_wq1': 8.0,
     'L3_xattn_wk1': 8.0,
     'L3_xattn_bias_k1': 64.0,
     'L3_xattn_bias_v1': 64.0,
     'L3_xattn_wq2': 8.0,
     'L3_xattn_wk2': 8.0,
     'L3_xattn_bias_k2': 64.0,
     'L3_xattn_bias_v2': 64.0}
    for name, (base, spread) in spreads.items():
        noise = np.random.default_rng([zlib.crc32(name.encode()), seed]).standard_normal(out[name].shape)
        drawn = base * np.exp(spread * noise) if base else spread * noise
        out[name] = jnp.asarray(drawn.astype(out[name].dtype))
    for name, factor in factors.items():
        out[name] = (out[name] * factor).astype(out[name].dtype)
    return out
```

```python
import numpy as np
from contextlib import ExitStack

import concourse.bass as bass
from concourse import mybir

F32 = mybir.dt.float32
I32 = mybir.dt.int32
U8 = mybir.dt.uint8
ACT = mybir.ActivationFunctionType
ALU = mybir.AluOpType
AX = mybir.AxisListType

P = 128
D = 256
DH = D // P
B = 4
S = 256
C = 64
TOK = B * S
TILES = TOK // P
H = 16
PAIRS = H // 2
HD = 16
HK = 128
F = 1024
FT = F // P
KEYS0 = S + C
VO = HD + 1
MASKED = -1.0e30
WIDTH = 4 * D
RING = 3
ATTN = [("L1", 1), ("L1", 2), ("L3", 1), ("L3", 2)]

COLS = {}


def _col(name, n):
    COLS[name] = (sum(w for _, w in COLS.values()), n)


for _l, _i in ATTN:
    for _v in ("bq", "bk", "bv", "bias_k"):
        _col(f"{_l}_{_v}{_i}", H)
    _col(f"{_l}_ln{_i}_scale", DH)
    _col(f"{_l}_ln{_i}_offset", DH)
for _l in ("L1", "L3"):
    _col(f"{_l}_ln_mlp_scale", DH)
    _col(f"{_l}_ln_mlp_offset", DH)
    _col(f"{_l}_b_fc1", FT)
_col("L0_q_b", 4)
_col("L0_k_b", 4)
_col("L0_v_b", DH)
_col("L0_postnorm_w", DH)
_col("L0_mlp_b1", FT)
_col("L2_ln1_w", DH)
_col("L2_ln1_b", DH)
_col("L2_q_b", 4)
_col("L2_k_b", 4)
_col("L2_v_b", DH)
_col("L2_ln2_w", DH)
_col("L2_ln2_b", DH)
_col("L2_fc_b", FT)
_col("zero", DH)
NCOLS = sum(w for _, w in COLS.values())
ROWS = ["L0_out_b", "L0_mlp_b2", "L1_b_fc2", "L2_cproj_b", "L2_proj_b", "L3_b_fc2"]

UPDATES = [("L0", TILES), ("M0", B), ("T0", TILES), ("T1", TILES), ("M1", B),
           ("L2", TILES), ("M2", B), ("T2", TILES), ("T3", TILES), ("M3", B)]


def rows_before(phase):
    n = 0
    for name, k in UPDATES:
        if name == phase:
            return n
        n += k
    return n


def norms_before(phase):
    n = 0
    for name, k in UPDATES[1:]:
        if name == phase:
            return n
        n += k
    return n


def build(nc, t):
    ctx = ExitStack()
    with ctx:
        def sb(name, shape, dt=F32):
            return ctx.enter_context(nc.sbuf_tensor(name, shape, dt))

        def sem(name):
            return ctx.enter_context(nc.semaphore(name))

        x = sb("x", [P, TILES, D])
        x0 = sb("x0", [P, TILES, D])
        ctxT = sb("ctxT", [P, 2, DH, B * C])
        cols = sb("cols", [P, NCOLS])
        brow = sb("brow", [P, len(ROWS), D])
        ident = sb("ident", [P, P])
        perm = sb("perm", [VO, VO])
        ones = sb("ones", [1, P])
        e16 = sb("e16", [1, VO])
        e16q = sb("e16q", [1, P])
        mask_i = sb("mask_i", [1, B * C], I32)
        mask_u = sb("mask_u", [1, B * C], U8)
        mask = sb("mask", [1, 2, B * C])
        arena = sb("arena", [P, 16384])
        A = arena[:, 0:8192].rearrange("p (d g r s k) -> p d g r s k", d=DH, g=2, r=PAIRS, s=4)
        VW = arena[:, 8192:16384].rearrange("p (b r n) -> p b r n", b=B, r=PAIRS)
        QT0 = arena[:, 0:4096].rearrange("p (m n) -> p m n", m=4)
        KT0 = arena[:, 4096:8192].rearrange("p (m n) -> p m n", m=4)
        V0 = arena[:, 8192:8192 + TILES * H * VO].rearrange("p (t h c) -> p t h c", t=TILES, h=H)
        xT = arena[:, 10368:10368 + DH * TOK].rearrange("p (d n) -> p d n", d=DH)
        wp0 = arena[:, 12416:12416 + DH * 1024].rearrange("p (d n) -> p d n", d=DH)
        vw0 = arena[:, 14464:14464 + DH * D].rearrange("p (d n) -> p d n", d=DH)
        ow0 = arena[:, 14976:14976 + DH * D].rearrange("p (d n) -> p d n", d=DH)
        KC = sb("KC", [P, 4, B * C])
        VC = sb("VC", [P, B, PAIRS, 2, VO])
        ctxD = sb("ctxD", [P, DH, B, 2 * C])
        Ab = sb("Ab", [P, DH, 2, H])
        cb = sb("cb", [1, 2, PAIRS, 4, C])
        cbb = sb("cbb", [1, 2, H])
        VWb = sb("VWb", [VO, 2, D])
        bvz = sb("bvz", [P, H, VO])
        bo = sb("bo", [1, 4, D])
        ring = sb("ring", [P, RING, WIDTH])
        wp2 = ring[:, 0:2, :]
        vw2 = ring[:, 2, :].rearrange("p (w d n) -> p w d n", w=2, d=DH)
        w1 = sb("w1", [P, DH, F])
        w2 = sb("w2", [P, FT, D])
        KT = sb("KT", [P, 2, B * C + 1])
        VT = sb("VT", [P, 2, B * C])
        z = sb("z", [P, 2, 2, D])
        hT = sb("hT", [P, 2, DH, 2 * P])
        stat = sb("stat", [P, 2, 2, 6])
        mv = sb("mv", [P, 2, 2, 2])
        var = sb("var", [P, 2, 2])
        rstd = sb("rstd", [P, 2, 2])
        neg_half = sb("neg_half", [P, 2])
        sq = sb("sq", [P, D])
        PN = H * C + H + 1
        prob = sb("prob", [P, 2, PN])
        pT = sb("pT", [P, 2, 9, P])
        mx = sb("mx", [P, 2, H])
        mx2 = sb("mx2", [P, 2, H])
        sm = sb("sm", [P, 2, H])
        rinv = sb("rinv", [P, 2, H])
        nb = sb("nb", [P, 2, 2, 2])
        qT2 = arena[:, 4096:5120].rearrange("p (k m n) -> p k m n", k=2, m=4)
        on = sb("on", [P, 2, D])
        oT = sb("oT", [P, 2, DH, P])
        hid = arena[:, 0:4096].rearrange("p (k f n) -> p k f n", k=2, f=FT)
        ps = ctx.enter_context(nc.psum_tensor("ps", [P, 8, 512], F32))

        in_vec = sem("in_vec")
        in_act = sem("in_act")
        in_w0 = sem("in_w0")
        in_mlp = sem("in_mlp")
        in_bv = sem("in_bv")
        in_l2 = sem("in_l2")
        in_ring = [sem(f"in_ring{i}") for i in range(RING)]
        stored = sem("stored")
        pool_set = sem("pool_set")
        consts_ready = sem("consts_ready")
        mask_ready = sem("mask_ready")
        xb_ready = sem("xb_ready")
        proj_ps = sem("proj_ps")
        proj_act = sem("proj_act")
        proj_dve = sem("proj_dve")
        s0_ps = sem("s0_ps")
        nb_ready = sem("nb_ready")
        p0_ready = sem("p0_ready")
        t0_ps = sem("t0_ps")
        pt0_act = sem("pt0_act")
        pt0_dve = sem("pt0_dve")
        kv_ps = sem("kv_ps")
        k_ready = sem("k_ready")
        kb_ready = sem("kb_ready")
        v_ready = sem("v_ready")
        a_ps = sem("a_ps")
        a_ready = sem("a_ready")
        vw_ps = sem("vw_ps")
        vw_act = sem("vw_act")
        vw_dve = sem("vw_dve")
        head_used = sem("head_used")
        vwb_ps = sem("vwb_ps")
        vwb_ready = sem("vwb_ready")
        z_ready = sem("z_ready")
        zT_ps = sem("zT_ps")
        h_ready = sem("h_ready")
        s_ps = sem("s_ps")
        s_used = sem("s_used")
        e_ready = sem("e_ready")
        rinv_ready = sem("rinv_ready")
        p_ready = sem("p_ready")
        pT_ps = sem("pT_ps")
        pT_act = sem("pT_act")
        pT_dve = sem("pT_dve")
        o_ps = sem("o_ps")
        rows_done = sem("rows_done")
        q_ps = sem("q_ps")
        q_ready = sem("q_ready")
        pv_ps = sem("pv_ps")
        on_ready = sem("on_ready")
        oT_ps = sem("oT_ps")
        oT_ready = sem("oT_ready")
        var_ready = sem("var_ready")
        rstd_ready = sem("rstd_ready")
        zm_ready = sem("zm_ready")
        zmT_ps = sem("zmT_ps")
        hm_ready = sem("hm_ready")
        f1_ps = sem("f1_ps")
        hid_ready = sem("hid_ready")
        f2_ps = sem("f2_ps")
        dve_step = sem("dve_step")

        def col(name, i=0, n=1):
            at = COLS[name][0] + i
            return cols[:, at:at + n]

        def jobs():
            out = []
            for m in range(4):
                out.append(("kc", 0, m, 0))
            for b in range(B):
                out.append(("vc", 0, b, 0))
            for m in range(4):
                for n in range(2):
                    out.append(("q0", 0, m, n))
                    out.append(("k0", 0, m, n))
            for g in range(TILES):
                out.append(("v0", 0, g, 0))
            for m in range(4):
                out.append(("kc", 1, m, 0))
            for b in range(B):
                out.append(("vc", 1, b, 0))
            return out

        JOBS = jobs()
        NJ = len(JOBS)
        NJ0 = NJ - 8

        def act_jobs(n):
            return (n + 1) // 2

        block = ctx.enter_context(nc.Block())

        MLPS = {"M0": ("L0", 0), "M1": ("L1", 1), "M2": ("L2", 2), "M3": ("L3", 3)}

        @block.sync
        def _(sp):
            sp.dma_start(ctxT[:, :, :, :], t["ctxT"]).then_inc(in_act, 16)
            sp.dma_start(ctxD[:, :, :, :], t["ctxD"]).then_inc(in_act, 16)
            sp.dma_start(xT, t["xT"]).then_inc(in_act, 16)
            sp.dma_start(cols[:, :], t["cols"]).then_inc(in_vec, 16)
            sp.dma_start(mask_i[:, :], t["mask_i"]).then_inc(in_vec, 16)
            sp.dma_start(mask_u[:, :], t["mask_u"]).then_inc(in_vec, 16)
            sp.dma_start(bo[:, :, :], t["bo"]).then_inc(in_vec, 16)
            sp.dma_start(wp0, t["wp0"]).then_inc(in_w0, 16)
            sp.dma_start(vw0, t["vw0"]).then_inc(in_w0, 16)
            sp.dma_start(ow0, t["ow0"]).then_inc(in_w0, 16)
            sp.dma_start(x[:, :, :], t["x"]).then_inc(in_w0, 16)
            sp.dma_start(brow[:, :, :], t["brow"]).then_inc(in_w0, 16)

            def load_mlp(l):
                if l > 0:
                    sp.wait_ge(rows_done, rows_before(f"M{l - 1}") + B)
                sp.dma_start(w1[:, :, :], t["w1"][l]).then_inc(in_mlp, 16)
                sp.dma_start(w2[:, :, :], t["w2"][l]).then_inc(in_mlp, 16)

            def load_keys(a):
                if a > 0:
                    sp.wait_ge(vwb_ps, 2 * a - 1)
                sp.dma_start(bvz[:, :, :], t["bvz"][a]).then_inc(in_bv, 16)
                for h in range(H):
                    n = a * H + h
                    if n >= RING:
                        sp.wait_ge(head_used, n - RING + 1)
                    sp.dma_start(ring[:, n % RING, :], t["heads"][a, h]).then_inc(in_ring[n % RING], 16)

            load_mlp(0)
            load_keys(0)
            load_mlp(1)
            load_keys(1)
            sp.wait_ge(head_used, 2 * H)
            sp.dma_start(wp2, t["wp2"]).then_inc(in_l2, 16)
            sp.dma_start(vw2, t["vw2"]).then_inc(in_l2, 16)
            load_mlp(2)
            sp.wait_ge(rows_done, rows_before("M2"))
            load_keys(2)
            load_mlp(3)
            load_keys(3)
            for b in range(B):
                sp.wait_ge(rows_done, rows_before("M3") + b + 1)
                sp.dma_start(t["out"][b], x[:, 2 * b:2 * b + 2, :]).then_inc(stored, 16)
            sp.wait_ge(stored, 16 * B)

        @block.gpsimd
        def _(pool):
            g = nc.gpsimd
            g.memset(ident[:, :], 0.0).then_inc(pool_set, 1)
            g.memset(perm[:, :], 0.0).then_inc(pool_set, 1)
            g.memset(ones[:, :], 1.0).then_inc(pool_set, 1)
            g.memset(e16[:, :], 0.0).then_inc(pool_set, 1)
            g.memset(e16q[:, :], 0.0).then_inc(pool_set, 1)
            g.memset(VC[:, :, :, :, :], 0.0).then_inc(pool_set, 1)
            g.memset(V0, 1.0).then_inc(pool_set, 1)
            g.memset(prob[:, :, PN - 1:PN], 1.0).then_inc(pool_set, 1)
            pool.wait_ge(pool_set, 8)
            g.affine_select(out=ident[:, :], in_=ident[:, :], compare_op=ALU.not_equal, fill=1.0,
                            base=0, pattern=[[-1, P]], channel_multiplier=1).then_inc(pool_set, 1)
            pv = perm[:, 0:H].rearrange("p (a two) -> p a two", two=2)
            g.affine_select(out=pv[:, :, 1], in_=pv[:, :, 1], compare_op=ALU.not_equal, fill=1.0,
                            base=0, pattern=[[-2, PAIRS]], channel_multiplier=1).then_inc(pool_set, 1)
            g.affine_select(out=pv[:, :, 0], in_=pv[:, :, 0], compare_op=ALU.not_equal, fill=1.0,
                            base=-1, pattern=[[-2, PAIRS]], channel_multiplier=1).then_inc(pool_set, 1)
            g.affine_select(out=perm[:, H:VO], in_=perm[:, H:VO], compare_op=ALU.not_equal, fill=1.0,
                            base=-H, pattern=[[-1, 1]], channel_multiplier=1).then_inc(pool_set, 1)
            g.memset(e16[:, HD:VO], 1.0).then_inc(pool_set, 1)
            g.memset(e16q[:, :].rearrange("p (q r) -> p q r", q=4)[:, :, HD:HD + 1], 1.0).then_inc(pool_set, 1)
            pool.wait_ge(pool_set, 14)
            g.memset(VC[0:C, :, :, 0, HD:VO], 1.0).then_inc(pool_set, 1)
            pool.wait_ge(pool_set, 15)
            g.memset(VC[C:P, :, :, 1, HD:VO], 1.0).then_inc(pool_set, 1)
            pool.wait_ge(pool_set, 16)
            g.memset(neg_half[:, :], -0.5).then_inc(consts_ready, 1)
            pool.wait_ge(consts_ready, 1)

            def add_row(dst, n, name):
                g.tensor_tensor(dst[:, n, :], x[:, n, :], brow[:, ROWS.index(name), :], ALU.add).then_inc(xb_ready, 1)

            pool.wait_ge(in_w0, 16 * 5)
            for n in range(TILES):
                add_row(x0, n, "L0_out_b")
            pool.wait_ge(xb_ready, TILES)

            def keys(a):
                for h in range(H):
                    n = a * H + h
                    if n >= 2:
                        pool.wait_ge(a_ps, n - 1)
                    else:
                        pool.wait_ge(in_vec, 64)
                    l, i = ATTN[a]
                    g.tensor_copy(KT[:, n % 2, B * C:B * C + 1], col(f"{l}_bias_k{i}", h)).then_inc(kb_ready, 1)

            def power(phase, i, width):
                n, k = norms_before(phase) + i, i % 2
                pool.wait_ge(var_ready, n + 1)
                g.tensor_tensor(rstd[:, k, 0:width], var[:, k, 0:width], neg_half[:, 0:width], ALU.pow)\
                    .then_inc(rstd_ready, 1)

            def tokens(a):
                power(f"T{a}", 0, 1)
                power(f"T{a}", 1, 1)
                for n in range(TILES):
                    k = n % 2
                    if n + 2 < TILES:
                        power(f"T{a}", n + 2, 1)
                    pool.wait_ge(rinv_ready, 8 * a + n + 1)
                    pm = prob[:, k, 0:H * C].rearrange("p (h c) -> p h c", h=H)
                    g.tensor_tensor(pm, pm, rinv[:, k, :].unsqueeze(2).broadcast_to([P, H, C]), ALU.mult)
                    pb = prob[:, k, H * C:H * C + H]
                    g.tensor_tensor(pb, pb, rinv[:, k, :], ALU.mult).then_inc(p_ready, 1)

            def mlp_rows(l, name):
                power(f"M{l}", 0, 2)
                power(f"M{l}", 1, 2)
                for b in range(B):
                    if 1 <= b < B - 1:
                        power(f"M{l}", b + 1, 2)
                    for n in (2 * b, 2 * b + 1):
                        if l > 0:
                            pool.wait_ge(zm_ready, l * B + b + 1)
                        add_row(x, n, name)

            mlp_rows(0, "L0_mlp_b2")
            keys(0)
            tokens(0)
            keys(1)
            tokens(1)
            mlp_rows(1, "L1_b_fc2")
            power("L2", 0, 1)
            power("L2", 1, 1)
            for n in range(TILES):
                if n + 2 < TILES:
                    power("L2", n + 2, 1)
                pool.wait_ge(z_ready, 2 * TILES + n + 1)
                add_row(x, n, "L2_cproj_b")
            mlp_rows(2, "L2_proj_b")
            keys(2)
            tokens(2)
            keys(3)
            tokens(3)
            mlp_rows(3, "L3_b_fc2")

        @block.tensor
        def _(pe):
            mm = nc.tensor.matmul

            def project(lo, hi):
                for n in range(lo, hi):
                    kind, l, i, j = JOBS[n]
                    if n >= 8:
                        if n % 2 == 0:
                            pe.wait_ge(proj_act, (n - 8) // 2 + 1)
                        else:
                            pe.wait_ge(proj_dve, (n - 8) // 2 + 1)
                    o = ps[:, n % 8, :]
                    wp = wp0 if l == 0 else wp2
                    if kind == "kc":
                        for d in range(DH):
                            mm(o[:, 0:B * C], wp[:, d, 512 + i * P:512 + (i + 1) * P], ctxT[:, 0, d, :],
                               start=(d == 0), stop=False)
                        mm(o[:, 0:B * C], e16q[:, :], mask[:, l, :], start=False, stop=True).then_inc(proj_ps, 1)
                    elif kind == "vc":
                        w = vw0 if l == 0 else vw2[:, 0, :, :]
                        for d in range(DH):
                            m = mm(o[:, 0:D], ctxD[:, d, i, :], w[:, d, :], start=(d == 0), stop=(d == 1))
                        m.then_inc(proj_ps, 1)
                    elif kind == "v0":
                        for d in range(DH):
                            m = mm(o[:, 0:D], xT[:, d, i * P:(i + 1) * P], vw0[:, d, :],
                                   start=(d == 0), stop=(d == 1))
                        m.then_inc(proj_ps, 1)
                    else:
                        at = (0 if kind == "q0" else 512) + i * P
                        for d in range(DH):
                            m = mm(o[:, :], wp0[:, d, at:at + P], xT[:, d, j * 512:(j + 1) * 512],
                                   start=(d == 0), stop=(d == 1))
                        m.then_inc(proj_ps, 1)

            def attend0():
                pe.wait_ge(proj_act, act_jobs(NJ0))
                pe.wait_ge(proj_dve, NJ0 // 2)
                N = TILES * PAIRS

                def scores(n):
                    g, r = n // PAIRS, n % PAIRS
                    b, m = g // 2, r // 2
                    if n >= 2:
                        pe.wait_ge(p0_ready, n - 1)
                    for e in range(2):
                        j = 2 * (r % 2) + e
                        q = QT0[32 * j:32 * j + 32, m, g * P:(g + 1) * P]
                        lat = KT0[32 * j:32 * j + 32, m, b * S:(b + 1) * S]
                        kc = KC[32 * j:32 * j + 32, m, b * C:(b + 1) * C]
                        at_lat, at_c = (0, S) if e == 0 else (C, 0)
                        mm(ps[:, j, at_lat:at_lat + S], q, lat, start=True, stop=True)
                        last = mm(ps[:, j, at_c:at_c + C], q, kc, start=True, stop=True)
                    last.then_inc(s0_ps, 1)

                def turn(n):
                    pe.wait_ge(p0_ready, n + 1)
                    if n >= 1:
                        pe.wait_ge(pt0_act, n)
                        pe.wait_ge(pt0_dve, n)
                    for c in range(5):
                        last = nc.tensor.transpose(ps[:, 4 + c // 3, (c % 3) * P:(c % 3 + 1) * P],
                                                   prob[:, n % 2, c * P:(c + 1) * P], ident[:, :])
                    last.then_inc(t0_ps, 1)

                def values(n):
                    g, r = n // PAIRS, n % PAIRS
                    b, k = g // 2, n % 2
                    pe.wait_ge(pt0_act, n + 1)
                    pe.wait_ge(pt0_dve, n + 1)
                    if r == 0 and g >= 1:
                        pe.wait_ge(on_ready, g)
                    o = ps[:, 6, r * 2 * VO:(r + 1) * 2 * VO]
                    mm(o, pT[:, k, 2, :], VC[:, b, r, :, :].rearrange("p e c -> p (e c)"), start=True, stop=False)
                    for e in range(2):
                        for u in range(2):
                            last = mm(o[:, e * VO:(e + 1) * VO], pT[:, k, 3 * e + u, :], V0[:, 2 * b + u, 2 * r + e, :],
                                      start=False, stop=(e == 1 and u == 1))
                    if r == PAIRS - 1:
                        last.then_inc(pv_ps, 1)

                def output(g):
                    k = g % 2
                    pe.wait_ge(on_ready, g + 1)
                    if g >= 1:
                        pe.wait_ge(rows_done, g)
                    for d in range(DH):
                        last = nc.tensor.transpose(ps[:, 7, d * P:(d + 1) * P], on[:, k, d * P:(d + 1) * P], ident[:, :])
                    last.then_inc(oT_ps, 1)
                    pe.wait_ge(oT_ready, g + 1)
                    for d in range(DH):
                        last = mm(ps[:, 7, 256:512], oT[:, k, d, :], ow0[:, d, :], start=(d == 0), stop=(d == 1))
                    last.then_inc(o_ps, 1)

                for i in range(N + 2):
                    if i < N:
                        scores(i)
                    if 1 <= i <= N:
                        turn(i - 1)
                    if i >= 2:
                        values(i - 2)
                    if i >= 6 and (i - 6) % PAIRS == PAIRS - 1:
                        output((i - 6) // PAIRS)
                output(TILES - 1)

            def keys(a):
                l, i = ATTN[a]
                pe.wait_ge(rows_done, rows_before(f"T{a}"))

                def heads_kv(h):
                    n = a * H + h
                    k, w = n % 2, ring[:, n % RING, :]
                    pe.wait_ge(in_ring[n % RING], 16 * (n // RING + 1))
                    if h >= 2:
                        pe.wait_ge(k_ready, n - 1)
                        pe.wait_ge(v_ready, n - 1)
                    for d in range(DH):
                        mm(ps[:, k, 0:B * C], w[:, d * P:(d + 1) * P], ctxT[:, 0, d, :], start=(d == 0), stop=(d == 1))
                    for d in range(DH):
                        last = mm(ps[:, k, 256:512], w[:, 256 + d * P:256 + (d + 1) * P], ctxT[:, h % 2, d, :],
                                  start=(d == 0), stop=(d == 1))
                    last.then_inc(kv_ps, 1)

                def products(h):
                    n = a * H + h
                    k, w = n % 2, ring[:, n % RING, :]
                    pe.wait_ge(k_ready, n + 1)
                    pe.wait_ge(kb_ready, n + 1)
                    if n >= 1:
                        pe.wait_ge(a_ready, n)
                    for d in range(DH):
                        mm(ps[:, 2 + d, 0:B * C + 1], w[:, 512 + d * P:512 + (d + 1) * P], KT[:, k, :], start=True, stop=True)
                    mm(ps[0:1, 4, 0:B * C + 1], col(f"{l}_bq{i}", h), KT[:, k, :], start=True, stop=True).then_inc(a_ps, 1)
                    pe.wait_ge(v_ready, n + 1)
                    if n >= 2:
                        pe.wait_ge(vw_act, n - 1)
                        pe.wait_ge(vw_dve, n - 1)
                    for g in range(2):
                        last = mm(ps[:, 5 + k, g * D:(g + 1) * D], VT[:, k, g * P:(g + 1) * P], w[:, 768:1024],
                                  start=True, stop=True)
                    last.then_inc(vw_ps, 1)
                    if h == 0:
                        pe.wait_ge(in_bv, 16 * (a + 1))
                    mm(ps[0:VO, 7, 0:D], bvz[:, h, :], w[:, 768:1024], start=(h == 0), stop=False).then_inc(head_used, 1)

                for step in range(H + 1):
                    if step < H:
                        heads_kv(step)
                    if step >= 1:
                        products(step - 1)
                mm(ps[0:VO, 7, 0:D], e16[:, :], bo[:, a, :], start=False, stop=True).then_inc(vwb_ps, 1)
                pe.wait_ge(vwb_ready, 2 * a + 1)
                mm(ps[0:VO, 0, 0:D], perm[:, :], VWb[:, 0, :], start=True, stop=True).then_inc(vwb_ps, 1)

            def turn_z(tile, n):
                k = tile % 2
                pe.wait_ge(z_ready, n + 1)
                if n >= 1:
                    pe.wait_ge(h_ready, n)
                for d in range(DH):
                    last = nc.tensor.transpose(ps[:, 7, d * P:(d + 1) * P], z[:, k, 0, d * P:(d + 1) * P], ident[:, :])
                last.then_inc(zT_ps, 1)

            def tokens(a, seq):
                base = seq * TILES
                pe.wait_ge(vwb_ready, 2 * a + 2)
                pe.wait_ge(a_ready, H * (a + 1))
                pe.wait_ge(vw_act, H * (a + 1))
                pe.wait_ge(vw_dve, H * (a + 1))

                def scores(g):
                    n, k, b = base + g, g % 2, g // 2
                    pe.wait_ge(h_ready, n + 1)
                    if g >= 1:
                        pe.wait_ge(s_used, n)
                    for half in range(2):
                        o = ps[:, half, :]
                        cols_of = slice(4 * half, 4 * half + 4)
                        sl = slice(2 * (b % 2), 2 * (b % 2) + 2)
                        for d in range(DH):
                            mm(o, hT[:, k, d, 0:P],
                               A[:, d, b // 2, cols_of, sl, :].rearrange("p r s k -> p r (s k)"),
                               start=(d == 0), stop=False)
                        mm(o, ones[:, :], cb[:, b // 2, cols_of, sl, :].rearrange("p r s k -> p r (s k)"),
                           start=False, stop=True)
                    for d in range(DH):
                        mm(ps[:, 2, 0:H], hT[:, k, d, 0:P], Ab[:, d, b % 2, :], start=(d == 0), stop=False)
                    mm(ps[:, 2, 0:H], ones[:, :], cbb[:, b % 2, :], start=False, stop=True).then_inc(s_ps, 1)

                def turn_p(g):
                    n, k = base + g, g % 2
                    pe.wait_ge(p_ready, 8 * a + g + 1)
                    if n >= 1:
                        pe.wait_ge(pT_act, n)
                        pe.wait_ge(pT_dve, n)
                    for c in range(PAIRS):
                        nc.tensor.transpose(ps[:, 3 + c // 4, (c % 4) * P:(c % 4 + 1) * P],
                                            prob[:, k, c * P:(c + 1) * P], ident[:, :])
                    nc.tensor.transpose(ps[0:VO, 5, 0:P], prob[:, k, H * C:PN], ident[:, :]).then_inc(pT_ps, 1)

                def output(g):
                    n, k, b = base + g, g % 2, g // 2
                    pe.wait_ge(pT_act, n + 1)
                    pe.wait_ge(pT_dve, n + 1)
                    if g >= 1:
                        pe.wait_ge(rows_done, rows_before(f"T{a}") + g)
                    for c in range(PAIRS):
                        mm(ps[:, 6, 0:D], pT[:, k, c, :], VW[:, b, c, :], start=(c == 0), stop=False)
                    mm(ps[:, 6, 0:D], pT[0:VO, k, 8, :], VWb[:, b % 2, :], start=False, stop=True).then_inc(o_ps, 1)

                turn_z(0, base)
                for i in range(TILES + 1):
                    if i < TILES:
                        scores(i)
                    if i >= 1:
                        turn_p(i - 1)
                    if i + 1 < TILES:
                        turn_z(i + 1, base + i + 1)
                    if i >= 1:
                        output(i - 1)

            def attend2(seq):
                base = seq * TILES
                pe.wait_ge(rows_done, rows_before("L2"))
                pe.wait_ge(in_l2, 32)
                project(NJ0, NJ)
                pe.wait_ge(proj_act, act_jobs(NJ))
                pe.wait_ge(proj_dve, NJ // 2)

                def queries(g):
                    n, k = base + g, g % 2
                    pe.wait_ge(h_ready, n + 1)
                    for m in range(4):
                        for d in range(DH):
                            last = mm(ps[:, 4, m * P:(m + 1) * P], wp2[:, d, m * P:(m + 1) * P], hT[:, k, d, 0:P],
                                      start=(d == 0), stop=(d == 1))
                    last.then_inc(q_ps, 1)

                def scores(g):
                    k, b = g % 2, g // 2
                    pe.wait_ge(q_ready, g + 1)
                    if g >= 1:
                        pe.wait_ge(s_used, base + g)
                    for h in range(H):
                        j, m = h % 4, h // 4
                        last = mm(ps[:, j, m * C:(m + 1) * C], qT2[32 * j:32 * j + 32, k, m, :],
                                  KC[32 * j:32 * j + 32, m, b * C:(b + 1) * C], start=True, stop=True)
                    last.then_inc(s_ps, 1)

                def turn_p(g):
                    n, k = base + g, g % 2
                    pe.wait_ge(e_ready, n + 1)
                    if g + 1 < TILES:
                        pe.wait_ge(q_ready, g + 2)
                    if g >= 1:
                        pe.wait_ge(rows_done, rows_before("L2") + g)
                    for c in range(PAIRS):
                        last = nc.tensor.transpose(ps[:, 4 + c // 4, (c % 4) * P:(c % 4 + 1) * P],
                                                   prob[:, k, c * P:(c + 1) * P], ident[:, :])
                    last.then_inc(pT_ps, 1)

                def values(g):
                    n, k, b = base + g, g % 2, g // 2
                    pe.wait_ge(pT_act, n + 1)
                    pe.wait_ge(pT_dve, n + 1)
                    if g >= 1:
                        pe.wait_ge(on_ready, TILES + g)
                    for r in range(PAIRS):
                        last = mm(ps[:, 6, r * 2 * VO:(r + 1) * 2 * VO], pT[:, k, r, :],
                                  VC[:, b, r, :, :].rearrange("p e c -> p (e c)"), start=True, stop=True)
                    last.then_inc(pv_ps, 1)

                def output(g):
                    k = g % 2
                    pe.wait_ge(on_ready, TILES + g + 1)
                    for d in range(DH):
                        last = nc.tensor.transpose(ps[:, 7, 256 + d * P:256 + (d + 1) * P],
                                                   on[:, k, d * P:(d + 1) * P], ident[:, :])
                    last.then_inc(oT_ps, 1)
                    pe.wait_ge(oT_ready, TILES + g + 1)
                    for d in range(DH):
                        last = mm(ps[:, 5, 0:D], oT[:, k, d, :], vw2[:, 1, d, :], start=(d == 0), stop=(d == 1))
                    last.then_inc(o_ps, 1)

                turn_z(0, base)
                queries(0)
                for i in range(TILES + 1):
                    if i < TILES:
                        scores(i)
                    if i >= 1:
                        turn_p(i - 1)
                        values(i - 1)
                    if i + 1 < TILES:
                        turn_z(i + 1, base + i + 1)
                        queries(i + 1)
                    if i >= 1:
                        output(i - 1)

            def mlp(l):
                base = l * B
                pe.wait_ge(rows_done, rows_before(f"M{l}"))
                pe.wait_ge(in_mlp, 32 * (l + 1))

                def turn(b):
                    k = b % 2
                    pe.wait_ge(zm_ready, base + b + 1)
                    if b >= 1:
                        pe.wait_ge(hm_ready, base + b)
                    for d in range(DH):
                        for u in range(2):
                            last = nc.tensor.transpose(ps[:, 4, d * 256 + u * P:d * 256 + (u + 1) * P],
                                                       z[:, k, u, d * P:(d + 1) * P], ident[:, :])
                    last.then_inc(zmT_ps, 1)

                def up(b):
                    k = b % 2
                    pe.wait_ge(hm_ready, base + b + 1)
                    for f in range(FT):
                        if b >= 1 and f % 2 == 0:
                            pe.wait_ge(hid_ready, (base + b - 1) * FT + f + 2)
                        for d in range(DH):
                            last = mm(ps[:, f // 2, (f % 2) * 256:(f % 2 + 1) * 256], w1[:, d, f * P:(f + 1) * P],
                                      hT[:, k, d, :], start=(d == 0), stop=(d == 1))
                        last.then_inc(f1_ps, 1)

                def down(b):
                    k = b % 2
                    pe.wait_ge(hid_ready, (base + b + 1) * FT)
                    if b >= 1:
                        pe.wait_ge(rows_done, rows_before(f"M{l}") + b)
                    for u in range(2):
                        for f in range(FT):
                            last = mm(ps[:, 5 + u, 0:D], hid[:, k, f, u * P:(u + 1) * P], w2[:, f, :],
                                      start=(f == 0), stop=(f == FT - 1))
                    last.then_inc(f2_ps, 1)

                turn(0)
                for i in range(B + 1):
                    if i < B:
                        up(i)
                    if i + 1 < B:
                        turn(i + 1)
                    if i >= 1:
                        down(i - 1)

            pe.wait_ge(in_act, 16 * 3)
            pe.wait_ge(in_w0, 16 * 5)
            pe.wait_ge(consts_ready, 1)
            pe.wait_ge(mask_ready, 1)
            project(0, NJ0)
            attend0()
            mlp(0)
            keys(0)
            tokens(0, 0)
            keys(1)
            tokens(1, 1)
            mlp(1)
            attend2(2)
            mlp(2)
            keys(2)
            tokens(2, 3)
            keys(3)
            tokens(3, 4)
            mlp(3)

        def job_out(eng, copy, n):
            kind, l, i, j = JOBS[n]
            o = ps[:, n % 8, :]
            pre = "L0" if l == 0 else "L2"
            if kind == "kc":
                return copy(KC[:, i, :], o[:, 0:B * C], col(f"{pre}_k_b", i))
            if kind == "q0":
                return copy(QT0[:, i, j * 512:(j + 1) * 512], o, col("L0_q_b", i))
            if kind == "k0":
                return copy(KT0[:, i, j * 512:(j + 1) * 512], o, col("L0_k_b", i))
            if kind == "v0":
                return copy(V0[:, i, :, 0:HD], o[:, 0:D].rearrange("p (h c) -> p h c", h=H), None)
            ov = o[:, 0:D].rearrange("p (r e c) -> p r e c", r=PAIRS, e=2)
            copy(VC[0:C, i, :, 0, 0:HD], ov[0:C, :, 0, :], None)
            return copy(VC[C:P, i, :, 1, 0:HD], ov[C:P, :, 1, :], None)

        @block.scalar
        def _(act):
            a_ = nc.scalar.activation

            def copy(out, in_, bias):
                if bias is None:
                    return a_(out, in_, ACT.Copy)
                return a_(out, in_, ACT.Identity, bias=bias)

            act.wait_ge(in_vec, 64)
            act.wait_ge(consts_ready, 1)
            for n in range(0, NJ0, 2):
                act.wait_ge(proj_ps, n + 1)
                job_out(act, copy, n).then_inc(proj_act, 1)

            def exp0(n):
                act.wait_ge(nb_ready, n + 1)
                if n >= 2:
                    act.wait_ge(t0_ps, n - 1)
                r = n % PAIRS
                for e in range(2):
                    j = 2 * (r % 2) + e
                    last = a_(prob[:, n % 2, e * KEYS0:(e + 1) * KEYS0], ps[:, j, 0:KEYS0], ACT.Exp,
                              bias=nb[:, n % 2, 1, e:e + 1], scale=1.0 / HD)
                last.then_inc(p0_ready, 1)

            def copy0(n):
                act.wait_ge(t0_ps, n + 1)
                k = n % 2
                if n >= 2 and (n - 2) % PAIRS == PAIRS - 1:
                    act.wait_ge(pv_ps, (n - 2) // PAIRS + 1)
                a_(pT[:, k, 3:5, :], ps[:, 5, 0:2 * P].rearrange("p (c n) -> p c n", c=2), ACT.Copy).then_inc(pt0_act, 1)

            def turned_o(n, bias, at):
                k = n % 2
                act.wait_ge(oT_ps, n + 1)
                for d in range(DH):
                    last = a_(oT[:, k, d, :], ps[:, 7, at + d * P:at + (d + 1) * P], ACT.Identity, bias=col(bias, d))
                last.then_inc(oT_ready, 1)

            N = TILES * PAIRS
            for i in range(N + 2):
                if i < N:
                    exp0(i)
                if 1 <= i <= N:
                    copy0(i - 1)
                if i >= 6 and (i - 6) % PAIRS == PAIRS - 1:
                    turned_o((i - 6) // PAIRS, "L0_v_b", 0)
            turned_o(TILES - 1, "L0_v_b", 0)

            def scaled(n, scale, offset):
                k = n % 2
                act.wait_ge(zT_ps, n + 1)
                for d in range(DH):
                    last = a_(hT[:, k, d, 0:P], ps[:, 7, d * P:(d + 1) * P], ACT.Identity,
                              scale=col(scale, d), bias=col(offset, d))
                last.then_inc(h_ready, 1)

            def mlp(l, scale, offset, bias, gelu):
                base = l * B

                def turned(b):
                    k = b % 2
                    act.wait_ge(zmT_ps, base + b + 1)
                    for d in range(DH):
                        last = a_(hT[:, k, d, :], ps[:, 4, d * 256:(d + 1) * 256], ACT.Identity,
                                  scale=col(scale, d), bias=col(offset, d))
                    last.then_inc(hm_ready, 1)

                turned(0)
                for b in range(B):
                    if b >= 2:
                        act.wait_ge(f2_ps, base + b - 1)
                    for f in range(FT):
                        if f % 2 == 0:
                            act.wait_ge(f1_ps, (base + b) * FT + f + 2)
                        a_(hid[:, b % 2, f, :], ps[:, f // 2, (f % 2) * 256:(f % 2 + 1) * 256], gelu,
                           bias=col(bias, f)).then_inc(hid_ready, 1)
                    if b + 1 < B:
                        turned(b + 1)

            def keys(a):
                l, i = ATTN[a]
                act.wait_ge(rows_done, rows_before(f"T{a}"))
                for step in range(H + 1):
                    n = a * H + step
                    k = n % 2
                    if step < H:
                        act.wait_ge(kv_ps, n + 1)
                        if n >= 2:
                            act.wait_ge(a_ps, n - 1)
                        a_(KT[:, k, 0:B * C], ps[:, k, 0:B * C], ACT.Identity, bias=col(f"{l}_bk{i}", step))\
                            .then_inc(k_ready, 1)
                        if n >= 2:
                            act.wait_ge(vw_ps, n - 1)
                        a_(VT[:, k, :], ps[:, k, 256:512], ACT.Identity, bias=col(f"{l}_bv{i}", step))\
                            .then_inc(v_ready, 1)
                    if step >= 1:
                        n, h = n - 1, step - 1
                        act.wait_ge(vw_ps, n + 1)
                        a_(VW[C:P, 1 - h % 2:B:2, h // 2, :], ps[C:P, 5 + n % 2, :].rearrange("p (g n) -> p g n", g=2),
                           ACT.Copy).then_inc(vw_act, 1)

            def tokens(a, seq):
                base = seq * TILES
                l, i = ATTN[a]
                scaled(base, f"{l}_ln{i}_scale", f"{l}_ln{i}_offset")
                for g in range(TILES + 1):
                    if g >= 1:
                        n, k = base + g - 1, (g - 1) % 2
                        act.wait_ge(pT_ps, n + 1)
                        a_(pT[:, k, 0:4, :], ps[:, 3, :].rearrange("p (c n) -> p c n", c=4), ACT.Copy).then_inc(pT_act, 1)
                    if g + 1 < TILES:
                        scaled(base + g + 1, f"{l}_ln{i}_scale", f"{l}_ln{i}_offset")
                    if g < TILES:
                        n, k = base + g, g % 2
                        act.wait_ge(s_used, n + 1)
                        a_(prob[:, k, 0:H * C + H], prob[:, k, 0:H * C + H], ACT.Exp, scale=float(HK) ** -0.5)\
                            .then_inc(e_ready, 1)

            def attend2(seq):
                base = seq * TILES
                for n in range(NJ0, NJ, 2):
                    act.wait_ge(proj_ps, n + 1)
                    job_out(act, copy, n).then_inc(proj_act, 1)
                scaled(base, "L2_ln1_w", "L2_ln1_b")
                for g in range(TILES + 1):
                    if g >= 1:
                        n, k = base + g - 1, (g - 1) % 2
                        act.wait_ge(pT_ps, n + 1)
                        a_(pT[:, k, 0:4, :], ps[:, 4, :].rearrange("p (c n) -> p c n", c=4), ACT.Copy).then_inc(pT_act, 1)
                    if g < TILES:
                        n, k = base + g, g % 2
                        act.wait_ge(s_used, n + 1)
                        a_(prob[:, k, 0:H * C], prob[:, k, 0:H * C], ACT.Exp, scale=float(HD) ** -0.5)\
                            .then_inc(e_ready, 1)
                    if g + 1 < TILES:
                        scaled(base + g + 1, "L2_ln1_w", "L2_ln1_b")
                    if g >= 1:
                        turned_o(TILES + g - 1, "L2_v_b", 256)

            mlp(0, "L0_postnorm_w", "zero", "L0_mlp_b1", ACT.Gelu_apprx_tanh)
            keys(0)
            tokens(0, 0)
            keys(1)
            tokens(1, 1)
            mlp(1, "L1_ln_mlp_scale", "L1_ln_mlp_offset", "L1_b_fc1", ACT.Gelu)
            attend2(2)
            mlp(2, "L2_ln2_w", "L2_ln2_b", "L2_fc_b", ACT.Gelu_apprx_tanh)
            keys(2)
            tokens(2, 3)
            keys(3)
            tokens(3, 4)
            mlp(3, "L3_ln_mlp_scale", "L3_ln_mlp_offset", "L3_b_fc1", ACT.Gelu)

        @block.vector
        def _(dve):
            v = nc.vector
            steps = [0]

            def link(ins):
                steps[0] += 1
                ins.then_inc(dve_step, 1)
                dve.wait_ge(dve_step, steps[0])

            def copy(out, in_, bias):
                if bias is None:
                    return v.tensor_copy(out, in_)
                return v.tensor_scalar(out, in_, bias, None, ALU.add)

            dve.wait_ge(in_vec, 64)
            link(v.tensor_copy(mask[:, 0, :], mask_i[:, :]))
            link(v.tensor_scalar(mask[:, 0, :], mask[:, 0, :], 0.0, MASKED, ALU.is_equal, ALU.mult))
            link(v.tensor_copy(mask[:, 1, :], mask_u[:, :]))
            v.tensor_scalar(mask[:, 1, :], mask[:, 1, :], 0.0, MASKED, ALU.is_equal, ALU.mult).then_inc(mask_ready, 1)

            dve.wait_ge(consts_ready, 1)
            for n in range(1, NJ0, 2):
                dve.wait_ge(proj_ps, n + 1)
                job_out(dve, copy, n).then_inc(proj_dve, 1)

            def normal_o(n):
                k = n % 2
                dve.wait_ge(pv_ps, n + 1)
                o = ps[:, 6, 0:H * VO].rearrange("p (h c) -> p h c", h=H)
                link(v.reciprocal(rinv[:, k, :], o[:, :, HD]))
                v.tensor_tensor(on[:, k, :].rearrange("p (h c) -> p h c", h=H), o[:, :, 0:HD],
                                rinv[:, k, :].unsqueeze(2).broadcast_to([P, H, HD]), ALU.mult).then_inc(on_ready, 1)

            def max0(n):
                r = n % PAIRS
                dve.wait_ge(s0_ps, n + 1)
                if n >= 2:
                    dve.wait_ge(p0_ready, n - 1)
                j = 2 * (r % 2)
                link(v.tensor_reduce(nb[:, n % 2, 0, :], ps[:, j:j + 2, 0:KEYS0], AX.X, ALU.max))
                v.tensor_scalar(nb[:, n % 2, 1, :], nb[:, n % 2, 0, :], -1.0 / HD, None, ALU.mult).then_inc(nb_ready, 1)

            def copy0(n):
                dve.wait_ge(t0_ps, n + 1)
                v.tensor_copy(pT[:, n % 2, 0:3, :], ps[:, 4, 0:3 * P].rearrange("p (c n) -> p c n", c=3))\
                    .then_inc(pt0_dve, 1)

            def rows0(g):
                dve.wait_ge(o_ps, g + 1)
                dve.wait_ge(xb_ready, g + 1)
                v.tensor_tensor(x0[:, g, :], ps[:, 7, 256:512], x0[:, g, :], ALU.add).then_inc(rows_done, 1)

            N = TILES * PAIRS
            for i in range(N + 2):
                if i < N:
                    max0(i)
                if 1 <= i <= N:
                    copy0(i - 1)
                if i >= 2 and (i - 2) % PAIRS == PAIRS - 1:
                    normal_o((i - 2) // PAIRS)
                if i >= 6 and (i - 6) % PAIRS == PAIRS - 1:
                    rows0((i - 6) // PAIRS)
            rows0(TILES - 1)

            def spread(src, k, u, rms):
                if rms:
                    link(v.tensor_tensor_reduce(sq[:, :], src, src, 1.0 / D, 0.0, ALU.mult, ALU.add, mv[:, k, u, 1:2]))
                else:
                    link(v.bn_stats(stat[:, k, u, :], src))
                    link(v.bn_aggr(mv[:, k, u, :], stat[:, k, u, :]))
                return v.tensor_scalar(var[:, k, u:u + 1], mv[:, k, u, 1:2], 1e-6 if rms else 1e-5, None, ALU.add)

            def normalise(dst, src, k, u, rms):
                if rms:
                    return v.tensor_scalar(dst, src, rstd[:, k, u:u + 1], None, ALU.mult)
                return v.tensor_scalar(dst, src, mv[:, k, u, 0:1], rstd[:, k, u:u + 1], ALU.subtract, ALU.mult)

            def mlp(l):
                base = l * B
                src, rms = (x0, True) if l == 0 else (x, False)

                def norm(b):
                    k = b % 2
                    for u in range(2):
                        last = spread(src[:, 2 * b + u, :], k, u, rms)
                    last.then_inc(var_ready, 1)
                    if b >= 2:
                        dve.wait_ge(zmT_ps, base + b - 1)
                    dve.wait_ge(rstd_ready, norms_before(f"M{l}") + b + 1)
                    for u in range(2):
                        last = normalise(z[:, k, u, :], src[:, 2 * b + u, :], k, u, rms)
                    last.then_inc(zm_ready, 1)

                dve.wait_ge(rows_done, rows_before(f"M{l}"))
                norm(0)
                norm(1)
                for b in range(B):
                    if b + 2 < B:
                        norm(b + 2)
                    dve.wait_ge(f2_ps, base + b + 1)
                    dve.wait_ge(xb_ready, TILES * XB_AT[f"M{l}"] + 2 * b + 2)
                    v.tensor_tensor(x[:, 2 * b:2 * b + 2, :], ps[:, 5:7, 0:D], x[:, 2 * b:2 * b + 2, :], ALU.add)\
                        .then_inc(rows_done, 1)

            def keys(a):
                for h in range(H):
                    n = a * H + h
                    k, par = n % 2, h % 2
                    dve.wait_ge(a_ps, n + 1)
                    slots = slice(0, 4, 3) if par == 0 else slice(1, 3)
                    for d in range(DH):
                        v.tensor_copy(A[:, d, :, h // 2, slots, :],
                                      ps[:, 2 + d, 0:B * C].rearrange("p (g s k) -> p g s k", g=2, s=2))
                    v.tensor_copy(cb[:, :, h // 2, slots, :],
                                  ps[0:1, 4, 0:B * C].rearrange("p (g s k) -> p g s k", g=2, s=2))
                    for e in range(2):
                        at = h ^ e
                        v.tensor_copy(Ab[:, :, e, at:at + 1], ps[:, 2:4, B * C:B * C + 1])
                        last = v.tensor_copy(cbb[:, e, at:at + 1], ps[0:1, 4, B * C:B * C + 1])
                    last.then_inc(a_ready, 1)
                    dve.wait_ge(vw_ps, n + 1)
                    v.tensor_copy(VW[0:C, par:B:2, h // 2, :], ps[0:C, 5 + k, :].rearrange("p (g n) -> p g n", g=2))\
                        .then_inc(vw_dve, 1)
                dve.wait_ge(vwb_ps, 2 * a + 1)
                v.tensor_copy(VWb[:, 0, :], ps[0:VO, 7, 0:D]).then_inc(vwb_ready, 1)
                dve.wait_ge(vwb_ps, 2 * a + 2)
                v.tensor_copy(VWb[:, 1, :], ps[0:VO, 0, 0:D]).then_inc(vwb_ready, 1)

            def tile_spread(g):
                spread(x[:, g, :], g % 2, 0, False).then_inc(var_ready, 1)

            def tile_z(phase, n, g):
                k = g % 2
                if n >= 2:
                    dve.wait_ge(zT_ps, n - 1)
                dve.wait_ge(rstd_ready, norms_before(phase) + g + 1)
                normalise(z[:, k, 0, :], x[:, g, :], k, 0, False).then_inc(z_ready, 1)

            def tokens(a, seq):
                base = seq * TILES
                dve.wait_ge(rows_done, rows_before(f"T{a}"))
                tile_spread(0)
                tile_spread(1)
                tile_z(f"T{a}", base, 0)
                for g in range(TILES + 1):
                    if g + 2 < TILES:
                        tile_spread(g + 2)
                    if g + 1 < TILES:
                        tile_z(f"T{a}", base + g + 1, g + 1)
                    if g >= 1:
                        n, k = base + g - 1, (g - 1) % 2
                        dve.wait_ge(pT_ps, n + 1)
                        v.tensor_copy(pT[:, k, 4:8, :], ps[:, 4, :].rearrange("p (c n) -> p c n", c=4))
                        v.tensor_copy(pT[0:VO, k, 8, :], ps[0:VO, 5, 0:P]).then_inc(pT_dve, 1)
                    if g < TILES:
                        n, k = base + g, g % 2
                        dve.wait_ge(s_ps, n + 1)
                        main = ps[:, 0:2, :].rearrange("p q (h c) -> p (q h) c", c=C)
                        pm = prob[:, k, 0:H * C].rearrange("p (h c) -> p h c", h=H)
                        pb = prob[:, k, H * C:H * C + H]
                        link(v.tensor_reduce(mx[:, k, :], main, AX.X, ALU.max))
                        link(v.tensor_tensor(mx2[:, k, :], mx[:, k, :], ps[:, 2, 0:H], ALU.max))
                        v.tensor_tensor(pm, main, mx2[:, k, :].unsqueeze(2).broadcast_to([P, H, C]), ALU.subtract)
                        v.tensor_tensor(pb, ps[:, 2, 0:H], mx2[:, k, :], ALU.subtract).then_inc(s_used, 1)
                        dve.wait_ge(e_ready, n + 1)
                        link(v.tensor_reduce(sm[:, k, :], pm, AX.X, ALU.add))
                        link(v.tensor_tensor(sm[:, k, :], sm[:, k, :], pb, ALU.add))
                        v.reciprocal(rinv[:, k, :], sm[:, k, :]).then_inc(rinv_ready, 1)
                    if g >= 1:
                        dve.wait_ge(o_ps, TILES + base + g)
                        v.tensor_tensor(x[:, g - 1, :], ps[:, 6, 0:D], x[:, g - 1, :], ALU.add).then_inc(rows_done, 1)

            def attend2(seq):
                base = seq * TILES
                dve.wait_ge(rows_done, rows_before("L2"))
                for n in range(NJ0 + 1, NJ, 2):
                    dve.wait_ge(proj_ps, n + 1)
                    job_out(dve, copy, n).then_inc(proj_dve, 1)

                def queries(g):
                    dve.wait_ge(q_ps, g + 1)
                    v.tensor_tensor(qT2[:, g % 2, :, :], ps[:, 4, :].rearrange("p (m n) -> p m n", m=4),
                                    col("L2_q_b", 0, 4).unsqueeze(2).broadcast_to([P, 4, P]), ALU.add)\
                        .then_inc(q_ready, 1)

                tile_spread(0)
                tile_spread(1)
                tile_z("L2", base, 0)
                queries(0)
                for g in range(TILES + 1):
                    if g + 2 < TILES:
                        tile_spread(g + 2)
                    if g + 1 < TILES:
                        tile_z("L2", base + g + 1, g + 1)
                    if g >= 1:
                        n, k = base + g - 1, (g - 1) % 2
                        dve.wait_ge(pT_ps, n + 1)
                        v.tensor_copy(pT[:, k, 4:8, :], ps[:, 5, :].rearrange("p (c n) -> p c n", c=4)).then_inc(pT_dve, 1)
                    if g < TILES:
                        n, k = base + g, g % 2
                        dve.wait_ge(s_ps, n + 1)
                        main = ps[:, 0:4, 0:4 * C].rearrange("p j (m c) -> p j m c", c=C)
                        mj = mx[:, k, :].rearrange("p (j m) -> p j m", j=4)
                        pm = prob[:, k, 0:H * C].rearrange("p (m j c) -> p j m c", m=4, j=4)
                        link(v.tensor_reduce(mj, main, AX.X, ALU.max))
                        v.tensor_tensor(pm, main, mj.unsqueeze(3).broadcast_to([P, 4, 4, C]), ALU.subtract)\
                            .then_inc(s_used, 1)
                    if g >= 1:
                        normal_o(TILES + g - 1)
                    if g + 1 < TILES:
                        queries(g + 1)
                    if g >= 1:
                        dve.wait_ge(o_ps, TILES + base + g)
                        dve.wait_ge(xb_ready, TILES * XB_AT["L2"] + g)
                        v.tensor_tensor(x[:, g - 1, :], ps[:, 5, 0:D], x[:, g - 1, :], ALU.add).then_inc(rows_done, 1)

            XB_AT = {"M0": 1, "M1": 2, "L2": 3, "M2": 4, "M3": 5}
            mlp(0)
            keys(0)
            tokens(0, 0)
            keys(1)
            tokens(1, 1)
            mlp(1)
            attend2(2)
            mlp(2)
            keys(2)
            tokens(2, 3)
            keys(3)
            tokens(3, 4)
            mlp(3)


def _halves(w):
    return np.ascontiguousarray(np.asarray(w).reshape(-1, P, w.shape[-1]).transpose(1, 0, 2))


def _padded(w):
    out = np.zeros((w.shape[0], H, 32), w.dtype)
    out[:, :, :HD] = w.reshape(w.shape[0], H, HD)
    return out.reshape(w.shape[0], H * 32)


def _padded_bias(v, row16):
    out = np.zeros((H, 32), v.dtype)
    out[:, :HD] = v.reshape(H, HD)
    out[:, HD] = row16
    return out.reshape(4, P).T


def _layout(i):
    i = {k.replace("_xattn_", "_"): np.asarray(v) for k, v in i.items()}
    f = np.float32
    kvw = i["L0_kv_w"].reshape(D, D, 2)
    kvb = i["L0_kv_b"].reshape(D, 2)
    xT = np.ascontiguousarray(i["x"].reshape(TOK, D).T)
    cT = np.ascontiguousarray(i["ctx_2048"].reshape(B * C, D).T)
    cTs = np.ascontiguousarray(cT.reshape(D, 2, 2, C)[:, :, ::-1].reshape(D, B * C))
    cD = np.repeat(cT.reshape(D, B, 1, C), 2, axis=2).reshape(D, B * 2 * C)
    cols = np.zeros((P, NCOLS), f)
    for name, (at, n) in COLS.items():
        if name == "zero":
            continue
        if name == "L0_k_b":
            v = _padded_bias(kvb[:, 0], 0.0)
        elif name == "L0_v_b":
            v = kvb[:, 1].reshape(n, P).T
        elif name in ("L0_q_b", "L2_q_b"):
            v = _padded_bias(i[name], 1.0)
        elif name == "L2_k_b":
            v = _padded_bias(i[name], 0.0)
        else:
            v = i[name].reshape(n, P).T
        cols[:, at:at + n] = v
    brow = np.stack([i[r] for r in ROWS])
    heads = np.zeros((4, H, P, WIDTH), f)
    bvz = np.zeros((4, P, H, VO), f)
    for a, (l, k) in enumerate(ATTN):
        wk = i[f"{l}_wk{k}"].reshape(DH, P, H, HK).transpose(2, 1, 0, 3).reshape(H, P, D)
        wv = i[f"{l}_wv{k}"].reshape(DH, P, H, HK).transpose(2, 1, 0, 3).reshape(H, P, D)
        wqT = i[f"{l}_wq{k}"].T.reshape(H, HK, D)
        wo = i[f"{l}_wo{k}"].reshape(H, HK, D)
        heads[a] = np.concatenate([wk, wv, wqT, wo], axis=2)
        bv = i[f"{l}_bias_v{k}"].reshape(H, HK)
        for h in range(H):
            bvz[a, :, h, h] = bv[h]
    return {
        "ctxT": np.stack([_halves(cT), _halves(cTs)], axis=1),
        "ctxD": _halves(cD).reshape(P, DH, B, 2 * C),
        "xT": _halves(xT),
        "x": np.ascontiguousarray(i["x"].reshape(TILES, P, D).transpose(1, 0, 2)),
        "cols": cols,
        "mask_i": i["mask_BxS2_ik0"].reshape(1, B * C),
        "mask_u": np.ascontiguousarray(i["mask_BxS2_bf1"]).view(np.uint8).reshape(1, B * C),
        "bo": np.stack([i[f"{l}_bo{k}"] for l, k in ATTN])[None],
        "wp0": _halves(np.concatenate([_padded(i["L0_q_w"]), _padded(kvw[:, :, 0])], axis=1)),
        "vw0": _halves(np.ascontiguousarray(kvw[:, :, 1])),
        "ow0": _halves(i["L0_out_w"]),
        "wp2": _halves(np.concatenate([_padded(i["L2_q_w"]), _padded(i["L2_k_w"])], axis=1)),
        "vw2": np.stack([_halves(i["L2_v_w"]), _halves(i["L2_cproj_w"])], axis=1),
        "brow": brow,
        "w1": np.stack([_halves(i[k]) for k in ("L0_mlp_w1", "L1_w_fc1", "L2_fc_w", "L3_w_fc1")]),
        "w2": np.stack([_halves(i[k]) for k in ("L0_mlp_w2", "L1_w_fc2", "L2_proj_w", "L3_w_fc2")]),
        "bvz": bvz,
        "heads": heads,
    }


def kernel(**inputs):
    import concourse.bacc as bacc
    from concourse.bass_utils import run_bass_kernel_spmd

    nc = bacc.Bacc("TRN2", target_bir_lowering=False, num_devices=1)
    arrays, t = {}, {}
    for name, a in _layout(inputs).items():
        a = np.ascontiguousarray(a)
        arrays[f"in_{name}_dram"] = a
        t[name] = nc.dram_tensor(f"in_{name}_dram", a.shape, mybir.dt.from_np(a.dtype), kind="ExternalInput").ap()
    t["brow"] = t["brow"].unsqueeze(0).broadcast_to([P, len(ROWS), D])
    out = nc.dram_tensor("out_0_dram", (B, S, D), F32, kind="ExternalOutput").ap()
    t["out"] = [out[b].rearrange("(u p) n -> p u n", p=P) for b in range(B)]
    build(nc, t)
    r = run_bass_kernel_spmd(nc, [arrays], core_ids=[0])
    return r.results[0]["out_0_dram"]
```

```python
import numpy as np
from contextlib import ExitStack

import concourse.bass as bass
from concourse import mybir

F32 = mybir.dt.float32
F32R = mybir.dt.float32r
I32 = mybir.dt.int32
U8 = mybir.dt.uint8
ACT = mybir.ActivationFunctionType
ALU = mybir.AluOpType
AX = mybir.AxisListType

P = 128
D = 256
DH = D // P
B = 4
S = 256
C = 64
TOK = B * S
TILES = TOK // P
H = 16
PAIRS = H // 2
HD = 16
HK = 128
F = 1024
FT = F // P
KEYS0 = S + C
VO = HD + 1
MASKED = -1.0e30
WIDTH = 4 * D
RING = 3
ATTN = [("L1", 1), ("L1", 2), ("L3", 1), ("L3", 2)]

COLS = {}


def _col(name, n):
    COLS[name] = (sum(w for _, w in COLS.values()), n)


for _l, _i in ATTN:
    _col(f"{_l}_bq{_i}", 2 * H)
    for _v in ("bk", "bv", "bias_k"):
        _col(f"{_l}_{_v}{_i}", H)
    _col(f"{_l}_ln{_i}_scale", DH)
    _col(f"{_l}_ln{_i}_offset", DH)
for _l in ("L1", "L3"):
    _col(f"{_l}_ln_mlp_scale", DH)
    _col(f"{_l}_ln_mlp_offset", DH)
    _col(f"{_l}_b_fc1", FT)
_col("L0_q_b", PAIRS)
_col("L0_k_b", PAIRS)
_col("cb_parts", 2)
_col("q_parts", 2)
_col("k_parts", 2)
_col("L0_v_b", DH)
_col("L0_postnorm_w", DH)
_col("L0_mlp_b1", FT)
_col("L2_ln1_w", DH)
_col("L2_ln1_b", DH)
_col("L2_q_b", 4)
_col("L2_k_b", 4)
_col("L2_v_b", DH)
_col("L2_ln2_w", DH)
_col("L2_ln2_b", DH)
_col("L2_fc_b", FT)
_col("zero", DH)
NCOLS = sum(w for _, w in COLS.values())
ROWS = ["L0_out_b", "L0_mlp_b2", "L1_b_fc2", "L2_cproj_b", "L2_proj_b", "L3_b_fc2"]

UPDATES = [("L0", TILES), ("M0", B), ("T0", TILES), ("T1", TILES), ("M1", B),
           ("L2", TILES), ("M2", B), ("T2", TILES), ("T3", TILES), ("M3", B)]


def rows_before(phase):
    n = 0
    for name, k in UPDATES:
        if name == phase:
            return n
        n += k
    return n


def norms_before(phase):
    n = 0
    for name, k in UPDATES[1:]:
        if name == phase:
            return n
        n += k
    return n


def build(nc, t):
    ctx = ExitStack()
    with ctx:
        def sb(name, shape, dt=F32):
            return ctx.enter_context(nc.sbuf_tensor(name, shape, dt))

        def sem(name):
            return ctx.enter_context(nc.semaphore(name))

        x = sb("x", [P, TILES, D])
        x0 = sb("x0", [P, TILES, D])
        ctxT = sb("ctxT", [P, 2, DH, B * C])
        cols = sb("cols", [P, NCOLS])
        brow = sb("brow", [P, len(ROWS), D])
        ident = sb("ident", [P, P])
        perm = sb("perm", [VO, VO])
        ones = sb("ones", [2, P])
        ones_r = sb("ones_r", [2, P], F32R)
        e16 = sb("e16", [1, VO])
        e16q = sb("e16q", [1, P])
        e48 = sb("e48", [1, P])
        mask_i = sb("mask_i", [1, B * C], I32)
        mask_u = sb("mask_u", [1, B * C], U8)
        mask = sb("mask", [1, 2, B * C])
        arena = sb("arena", [P, 16384])
        A = arena[:, 0:8192].rearrange("p (d g r s k) -> p d g r s k", d=DH, g=2, r=PAIRS, s=4)
        VW = arena[:, 8192:16384].rearrange("p (b r n) -> p b r n", b=B, r=PAIRS)
        on0 = arena[:, 0:2048].rearrange("p (t n) -> p t n", t=TILES)
        kinT = arena[:, 2048:4608].rearrange("p (d b n) -> p d b n", d=DH, b=B)
        ws0 = arena[:, 4608:8704].rearrange("p (d w r n) -> p d w r n", d=DH, w=2, r=PAIRS)
        V0 = arena[:, 8704:8704 + TILES * H * VO].rearrange("p (t h c) -> p t h c", t=TILES, h=H)
        vw0 = arena[:, 10880:10880 + DH * D].rearrange("p (d n) -> p d n", d=DH)
        ow0 = arena[:, 11392:11392 + DH * D].rearrange("p (d n) -> p d n", d=DH)
        KQ = sb("KQ", [P, 3, 2, KEYS0], F32R)
        kq_full = sb("kq_full", [P, 2, KEYS0])
        kq_round = sb("kq_round", [P, 2, KEYS0], F32R)
        kq_rest = sb("kq_rest", [P, 2, KEYS0])
        KC = arena[:, 5632:6656].rearrange("p (m n) -> p m n", m=4)
        VC = sb("VC", [P, B, PAIRS, 2, VO])
        ctxD = sb("ctxD", [P, DH, B, 2 * C])
        Ab = sb("Ab", [P, DH, 2, H])
        cb = sb("cb", [2, 2, PAIRS, 4, C], F32R)
        cbb = sb("cbb", [2, 2, H], F32R)
        cb_round = sb("cb_round", [2, B * C + 1], F32R)
        VWb = sb("VWb", [VO, 2, D])
        bvz = sb("bvz", [P, H, VO])
        bo = sb("bo", [1, 4, D])
        ring = sb("ring", [P, RING, WIDTH])
        wp2 = ring[:, 0:2, :]
        vw2 = ring[:, 2, :].rearrange("p (w d n) -> p w d n", w=2, d=DH)
        w1 = sb("w1", [P, DH, F])
        w2 = sb("w2", [P, FT, D])
        KT = sb("KT", [P, 2, B * C + 1])
        VT = sb("VT", [P, 2, B * C])
        z = sb("z", [P, 2, 2, D])
        hT = sb("hT", [P, 2, DH, 2 * P])
        stat = sb("stat", [P, 2, 2, 6])
        mv = sb("mv", [P, 2, 2, 2])
        var = sb("var", [P, 2, 2])
        rstd = sb("rstd", [P, 2, 2])
        neg_half = sb("neg_half", [P, 2])
        sq = sb("sq", [P, D])
        PN = H * C + H + 1
        prob = sb("prob", [P, 2, PN])
        pT = sb("pT", [P, 2, 9, P])
        mx = sb("mx", [P, 2, H])
        mx2 = sb("mx2", [P, 2, H])
        sm = sb("sm", [P, 2, H])
        rinv = sb("rinv", [P, 2, H])
        nb = sb("nb", [P, 2, 2, 2])
        qT2 = arena[:, 4096:5120].rearrange("p (k m n) -> p k m n", k=2, m=4)
        on = arena[:, 5120:5632].rearrange("p (k n) -> p k n", k=2)
        oT = sb("oT", [P, 2, DH, P])
        hid = arena[:, 0:4096].rearrange("p (k f n) -> p k f n", k=2, f=FT)
        ps = ctx.enter_context(nc.psum_tensor("ps", [P, 8, 512], F32))

        in_vec = sem("in_vec")
        in_act = sem("in_act")
        in_w0 = sem("in_w0")
        in_ws = sem("in_ws")
        in_mlp = sem("in_mlp")
        in_bv = sem("in_bv")
        in_l2 = sem("in_l2")
        in_ring = [sem(f"in_ring{i}") for i in range(RING)]
        stored = sem("stored")
        pool_set = sem("pool_set")
        consts_ready = sem("consts_ready")
        mask_ready = sem("mask_ready")
        ones_ready = sem("ones_ready")
        xb_ready = sem("xb_ready")
        proj_ps = sem("proj_ps")
        proj_act = sem("proj_act")
        proj_dve = sem("proj_dve")
        s0_ps = sem("s0_ps")
        nb_ready = sem("nb_ready")
        p0_ready = sem("p0_ready")
        kq_ps = sem("kq_ps")
        kq_copied = sem("kq_copied")
        kq_step = sem("kq_step")
        kq_ready = sem("kq_ready")
        pv0_ps = sem("pv0_ps")
        pv0_used = sem("pv0_used")
        t0_ps = sem("t0_ps")
        pt0_act = sem("pt0_act")
        pt0_dve = sem("pt0_dve")
        kv_ps = sem("kv_ps")
        k_ready = sem("k_ready")
        kb_ready = sem("kb_ready")
        v_ready = sem("v_ready")
        a_ps = sem("a_ps")
        a_ready = sem("a_ready")
        vw_ps = sem("vw_ps")
        vw_act = sem("vw_act")
        vw_dve = sem("vw_dve")
        head_used = sem("head_used")
        vwb_ps = sem("vwb_ps")
        vwb_ready = sem("vwb_ready")
        z_ready = sem("z_ready")
        zT_ps = sem("zT_ps")
        h_ready = sem("h_ready")
        s_ps = sem("s_ps")
        s_used = sem("s_used")
        s_half = sem("s_half")
        sub_half = sem("sub_half")
        e_half = sem("e_half")
        p_half = sem("p_half")
        e_ready = sem("e_ready")
        rinv_ready = sem("rinv_ready")
        p_ready = sem("p_ready")
        pT_ps = sem("pT_ps")
        pT_act = sem("pT_act")
        pT_dve = sem("pT_dve")
        o_ps = sem("o_ps")
        rows_done = sem("rows_done")
        q_ps = sem("q_ps")
        q_ready = sem("q_ready")
        pv_ps = sem("pv_ps")
        on_ready = sem("on_ready")
        oT_ps = sem("oT_ps")
        oT_ready = sem("oT_ready")
        var_ready = sem("var_ready")
        rstd_ready = sem("rstd_ready")
        zm_ready = sem("zm_ready")
        zmT_ps = sem("zmT_ps")
        hm_ready = sem("hm_ready")
        f1_ps = sem("f1_ps")
        hid_ready = sem("hid_ready")
        f2_ps = sem("f2_ps")
        dve_step = sem("dve_step")

        def col(name, i=0, n=1):
            at = COLS[name][0] + i
            return cols[:, at:at + n]

        HALF = H // 2 * C

        def jobs():
            out = []
            for b in range(B):
                out.append(("vc", 0, b, 0))
            for g in range(TILES):
                out.append(("v0", 0, g, 0))
            for m in range(4):
                out.append(("kc", 1, m, 0))
            for b in range(B):
                out.append(("vc", 1, b, 0))
            return out

        JOBS = jobs()
        NJ = len(JOBS)
        NJ0 = NJ - 8

        def act_jobs(n):
            return (n + 1) // 2

        OUT0 = 2 * PAIRS + 4

        block = ctx.enter_context(nc.Block())

        MLPS = {"M0": ("L0", 0), "M1": ("L1", 1), "M2": ("L2", 2), "M3": ("L3", 3)}

        @block.sync
        def _(sp):
            sp.dma_start(ctxD[:, :, :, :], t["ctxD"]).then_inc(in_act, 16)
            sp.dma_start(kinT, t["kinT"]).then_inc(in_act, 16)
            sp.dma_start(vw0, t["vw0"]).then_inc(in_act, 16)
            sp.dma_start(cols[:, :], t["cols"]).then_inc(in_vec, 16)
            sp.dma_start(mask_i[:, :], t["mask_i"]).then_inc(in_vec, 16)
            sp.dma_start(mask_u[:, :], t["mask_u"]).then_inc(in_vec, 16)
            sp.dma_start(bo[:, :, :], t["bo"]).then_inc(in_vec, 16)
            sp.dma_start(ws0, t["ws0"]).then_inc(in_ws, 16)
            sp.dma_start(ctxT[:, :, :, :], t["ctxT"]).then_inc(in_w0, 16)
            sp.dma_start(ow0, t["ow0"]).then_inc(in_w0, 16)
            sp.dma_start(x[:, :, :], t["x"]).then_inc(in_w0, 16)
            sp.dma_start(brow[:, :, :], t["brow"]).then_inc(in_w0, 16)

            def load_mlp(l):
                if l > 0:
                    sp.wait_ge(rows_done, rows_before(f"M{l - 1}") + B)
                sp.dma_start(w1[:, :, :], t["w1"][l]).then_inc(in_mlp, 16)
                sp.dma_start(w2[:, :, :], t["w2"][l]).then_inc(in_mlp, 16)

            def load_keys(a):
                if a > 0:
                    sp.wait_ge(vwb_ps, 2 * a - 1)
                sp.dma_start(bvz[:, :, :], t["bvz"][a]).then_inc(in_bv, 16)
                for h in range(H):
                    n = a * H + h
                    if n >= RING:
                        sp.wait_ge(head_used, n - RING + 1)
                    sp.dma_start(ring[:, n % RING, :], t["heads"][a, h]).then_inc(in_ring[n % RING], 16)

            load_mlp(0)
            load_keys(0)
            load_mlp(1)
            load_keys(1)
            sp.wait_ge(head_used, 2 * H)
            sp.dma_start(wp2, t["wp2"]).then_inc(in_l2, 16)
            sp.dma_start(vw2, t["vw2"]).then_inc(in_l2, 16)
            load_mlp(2)
            sp.wait_ge(rows_done, rows_before("M2"))
            load_keys(2)
            load_mlp(3)
            load_keys(3)
            for b in range(B):
                sp.wait_ge(rows_done, rows_before("M3") + b + 1)
                sp.dma_start(t["out"][b], x[:, 2 * b:2 * b + 2, :]).then_inc(stored, 16)
            sp.wait_ge(stored, 16 * B)

        @block.gpsimd
        def _(pool):
            g = nc.gpsimd
            g.memset(ident[:, :], 0.0).then_inc(pool_set, 1)
            g.memset(perm[:, :], 0.0).then_inc(pool_set, 1)
            g.memset(ones[:, :], 1.0).then_inc(pool_set, 1)
            g.memset(e16[:, :], 0.0).then_inc(pool_set, 1)
            g.memset(e16q[:, :], 0.0).then_inc(pool_set, 1)
            g.memset(e48[:, :], 0.0).then_inc(pool_set, 1)
            g.memset(VC[:, :, :, :, :], 0.0).then_inc(pool_set, 1)
            g.memset(V0, 1.0).then_inc(pool_set, 1)
            g.memset(prob[:, :, PN - 1:PN], 1.0).then_inc(pool_set, 1)
            pool.wait_ge(pool_set, 9)
            g.affine_select(out=ident[:, :], in_=ident[:, :], compare_op=ALU.not_equal, fill=1.0,
                            base=0, pattern=[[-1, P]], channel_multiplier=1).then_inc(pool_set, 1)
            pv = perm[:, 0:H].rearrange("p (a two) -> p a two", two=2)
            g.affine_select(out=pv[:, :, 1], in_=pv[:, :, 1], compare_op=ALU.not_equal, fill=1.0,
                            base=0, pattern=[[-2, PAIRS]], channel_multiplier=1).then_inc(pool_set, 1)
            g.affine_select(out=pv[:, :, 0], in_=pv[:, :, 0], compare_op=ALU.not_equal, fill=1.0,
                            base=-1, pattern=[[-2, PAIRS]], channel_multiplier=1).then_inc(pool_set, 1)
            g.affine_select(out=perm[:, H:VO], in_=perm[:, H:VO], compare_op=ALU.not_equal, fill=1.0,
                            base=-H, pattern=[[-1, 1]], channel_multiplier=1).then_inc(pool_set, 1)
            g.memset(e16[:, HD:VO], 1.0).then_inc(pool_set, 1)
            g.memset(e16q[:, :].rearrange("p (q r) -> p q r", q=4)[:, :, HD:HD + 1], 1.0).then_inc(pool_set, 1)
            g.memset(e48[:, :].rearrange("p (q r) -> p q r", q=2)[:, :, 48:49], 1.0).then_inc(pool_set, 1)
            pool.wait_ge(pool_set, 16)
            g.memset(VC[0:C, :, :, 0, HD:VO], 1.0).then_inc(pool_set, 1)
            pool.wait_ge(pool_set, 17)
            g.memset(VC[C:P, :, :, 1, HD:VO], 1.0).then_inc(pool_set, 1)
            pool.wait_ge(pool_set, 18)
            g.memset(neg_half[:, :], -0.5).then_inc(consts_ready, 1)
            pool.wait_ge(consts_ready, 1)

            def add_row(dst, n, name):
                g.tensor_tensor(dst[:, n, :], x[:, n, :], brow[:, ROWS.index(name), :], ALU.add).then_inc(xb_ready, 1)

            pool.wait_ge(in_vec, 64)

            def keys(a, heads):
                for h in heads:
                    n = a * H + h
                    if n >= 2:
                        pool.wait_ge(a_ps, n - 1)
                    else:
                        pool.wait_ge(in_vec, 64)
                    l, i = ATTN[a]
                    g.tensor_copy(KT[:, n % 2, B * C:B * C + 1], col(f"{l}_bias_k{i}", h)).then_inc(kb_ready, 1)

            def parts(n):
                pair, w, k = n // 2, n % 2, n % 2
                width = S if w else KEYS0
                pat = "q_parts" if w else "k_parts"
                full = kq_full[:, k, 0:width]
                pool.wait_ge(kq_copied, n + 1)
                g.tensor_scalar(kq_round[:, k, 0:width], full, col(pat, 1), None, ALU.mult).then_inc(kq_step, 1)
                g.tensor_scalar(kq_rest[:, k, 0:width], full, col(pat, 0), None, ALU.mult).then_inc(kq_step, 1)
                pool.wait_ge(kq_step, 2 * n + 2)
                if pair >= 3:
                    pool.wait_ge(s0_ps, 2 * (pair - 3) + 2)
                g.tensor_tensor(KQ[:, pair % 3, w, 0:width], kq_rest[:, k, 0:width],
                                kq_round[:, k, 0:width].bitcast(F32), ALU.add).then_inc(kq_ready, 1)

            for n in range(4):
                parts(n)
            pool.wait_ge(in_w0, 16 * 4)
            for n in range(TILES):
                add_row(x0, n, "L0_out_b")
            for n in range(4, 2 * B * PAIRS):
                parts(n)

            def power(phase, i, width):
                n, k = norms_before(phase) + i, i % 2
                pool.wait_ge(var_ready, n + 1)
                g.tensor_tensor(rstd[:, k, 0:width], var[:, k, 0:width], neg_half[:, 0:width], ALU.pow)\
                    .then_inc(rstd_ready, 1)

            def first_norms(a):
                power(f"T{a}", 0, 1)
                power(f"T{a}", 1, 1)

            def tokens(a):
                for n in range(TILES):
                    k = n % 2
                    if n + 2 < TILES:
                        power(f"T{a}", n + 2, 1)
                    pool.wait_ge(rinv_ready, 8 * a + n + 1)
                    pm = prob[:, k, 0:H // 2 * C].rearrange("p (h c) -> p h c", c=C)
                    g.tensor_tensor(pm, pm, rinv[:, k, 0:H // 2].unsqueeze(2).broadcast_to([P, H // 2, C]), ALU.mult)
                    pb = prob[:, k, H * C:H * C + H]
                    g.tensor_tensor(pb, pb, rinv[:, k, :], ALU.mult).then_inc(p_ready, 1)

            def mlp_rows(l, name):
                power(f"M{l}", 0, 2)
                power(f"M{l}", 1, 2)
                for b in range(B):
                    if 1 <= b < B - 1:
                        power(f"M{l}", b + 1, 2)
                    for n in (2 * b, 2 * b + 1):
                        if l > 0:
                            pool.wait_ge(zm_ready, l * B + b + 1)
                        add_row(x, n, name)

            pool.wait_ge(xb_ready, TILES)
            mlp_rows(0, "L0_mlp_b2")
            keys(0, range(2))
            first_norms(0)
            keys(0, range(2, H))
            tokens(0)
            keys(1, range(2))
            first_norms(1)
            keys(1, range(2, H))
            tokens(1)
            mlp_rows(1, "L1_b_fc2")
            power("L2", 0, 1)
            power("L2", 1, 1)
            for n in range(TILES):
                if n + 2 < TILES:
                    power("L2", n + 2, 1)
                pool.wait_ge(z_ready, 2 * TILES + n + 1)
                add_row(x, n, "L2_cproj_b")
            mlp_rows(2, "L2_proj_b")
            keys(2, range(2))
            first_norms(2)
            keys(2, range(2, H))
            tokens(2)
            keys(3, range(2))
            first_norms(3)
            keys(3, range(2, H))
            tokens(3)
            mlp_rows(3, "L3_b_fc2")

        @block.tensor
        def _(pe):
            mm = nc.tensor.matmul

            def project(lo, hi):
                for n in range(lo, hi):
                    kind, l, i, j = JOBS[n]
                    if n >= 7:
                        pe.wait_ge(proj_act if (n - 7) % 2 == 0 else proj_dve, (n - 7) // 2 + 1)
                    o = ps[:, n % 7, :]
                    if kind == "kc":
                        for d in range(DH):
                            mm(o[:, 0:B * C], wp2[:, d, 512 + i * P:512 + (i + 1) * P], ctxT[:, 0, d, :],
                               start=(d == 0), stop=False)
                        mm(o[:, 0:B * C], e16q[:, :], mask[:, l, :], start=False, stop=True).then_inc(proj_ps, 1)
                    elif kind == "vc":
                        w = vw0 if l == 0 else vw2[:, 0, :, :]
                        for d in range(DH):
                            m = mm(o[:, 0:D], ctxD[:, d, i, :], w[:, d, :], start=(d == 0), stop=(d == 1))
                        m.then_inc(proj_ps, 1)
                    else:
                        rows = kinT[:, :, i // 2, C + (i % 2) * P:C + (i % 2 + 1) * P]
                        for d in range(DH):
                            m = mm(o[:, 0:D], rows[:, d, :], vw0[:, d, :], start=(d == 0), stop=(d == 1))
                        m.then_inc(proj_ps, 1)

            def attend0():
                pe.wait_ge(in_ws, 16)
                N = TILES * PAIRS

                def pair_of(n):
                    return n // 2, n // 2 // PAIRS, (n // 2) % PAIRS, n % 2

                def spread(n):
                    pair, w = n // 2, n % 2
                    b, r = pair // PAIRS, pair % PAIRS
                    if n >= 1:
                        pe.wait_ge(kq_copied, n)
                    for d in range(DH):
                        if w == 0:
                            mm(ps[:, 7, 0:KEYS0], ws0[:, d, 1, r, :], kinT[:, d, b, :], start=(d == 0), stop=False)
                        else:
                            last = mm(ps[:, 7, 0:S], ws0[:, d, 0, r, :], kinT[:, d, b, C:KEYS0],
                                      start=(d == 0), stop=(d == 1))
                    if w == 0:
                        last = mm(ps[:, 7, 0:C], e48[:, :], mask[:, 0, b * C:(b + 1) * C], start=False, stop=True)
                    last.then_inc(kq_ps, 1)

                def scores(n):
                    pair, b, r, u = pair_of(n)
                    pe.wait_ge(kq_ready, 2 * pair + 2)
                    if n >= 2:
                        pe.wait_ge(p0_ready, n - 1)
                    for e in range(2):
                        j = 2 * u + e
                        q = KQ[C * e:C * e + C, pair % 3, 1, u * P:(u + 1) * P]
                        kc = KQ[C * e:C * e + C, pair % 3, 0, 0:C]
                        lat = KQ[C * e:C * e + C, pair % 3, 0, C:KEYS0]
                        if e == 0:
                            mm(ps[:, j, 0:S], q, lat, start=True, stop=True)
                            mm(ps[:, j, S:KEYS0], q, kc, start=True, stop=True)
                        else:
                            last = mm(ps[:, j, 0:KEYS0], q, KQ[C * e:C * e + C, pair % 3, 0, :], start=True, stop=True)
                    last.then_inc(s0_ps, 1)

                def turn(n):
                    pe.wait_ge(p0_ready, n + 1)
                    if n >= 1:
                        pe.wait_ge(pt0_act, n)
                        pe.wait_ge(pt0_dve, n)
                    for c in range(5):
                        last = nc.tensor.transpose(ps[:, 4 + c // 3, (c % 3) * P:(c % 3 + 1) * P],
                                                   prob[:, n % 2, c * P:(c + 1) * P], ident[:, :])
                    last.then_inc(t0_ps, 1)

                def values(n):
                    pair, b, r, u = pair_of(n)
                    k = n % 2
                    pe.wait_ge(pt0_act, n + 1)
                    pe.wait_ge(pt0_dve, n + 1)
                    if n >= 1:
                        pe.wait_ge(pv0_used, n)
                    o = ps[:, 6, 0:2 * VO]
                    mm(o, pT[:, k, 2, :], VC[:, b, r, :, :].rearrange("p e c -> p (e c)"), start=True, stop=False)
                    for e in range(2):
                        for v in range(2):
                            last = mm(o[:, e * VO:(e + 1) * VO], pT[:, k, 3 * e + v, :], V0[:, 2 * b + v, 2 * r + e, :],
                                      start=False, stop=(e == 1 and v == 1))
                    last.then_inc(pv0_ps, 1)

                def output_turn(g):
                    pe.wait_ge(pv0_used, 2 * PAIRS * (g // 2 + 1))
                    for d in range(DH):
                        last = nc.tensor.transpose(ps[:, 7, d * P:(d + 1) * P], on0[:, g, d * P:(d + 1) * P], ident[:, :])
                    last.then_inc(oT_ps, 1)

                def output(g):
                    k = g % 2
                    pe.wait_ge(oT_ready, g + 1)
                    for d in range(DH):
                        last = mm(ps[:, 7, 256:512], oT[:, k, d, :], ow0[:, d, :], start=(d == 0), stop=(d == 1))
                    last.then_inc(o_ps, 1)

                for n in range(4):
                    spread(n)
                pe.wait_ge(proj_act, act_jobs(NJ0))
                pe.wait_ge(proj_dve, NJ0 // 2)
                for i in range(N + 3):
                    if i < N:
                        scores(i)
                    if i + 4 < 2 * B * PAIRS:
                        if i >= OUT0 and (i - OUT0) % (2 * PAIRS) in (2, 4):
                            g = 2 * ((i - OUT0) // (2 * PAIRS)) + (i - OUT0) % (2 * PAIRS) // 2 - 1
                            pe.wait_ge(rows_done, g + 1)
                        if i >= OUT0 and (i - OUT0) % (2 * PAIRS) in (1, 3):
                            g = 2 * ((i - OUT0) // (2 * PAIRS)) + (i - OUT0) % (2 * PAIRS) // 2
                            pe.wait_ge(oT_ready, g + 1)
                        spread(i + 4)
                    if 2 <= i < N + 2:
                        turn(i - 2)
                    if i >= 3:
                        values(i - 3)
                    if i >= OUT0 and i < N:
                        step = (i - OUT0) % (2 * PAIRS)
                        g = 2 * ((i - OUT0) // (2 * PAIRS)) + step // 2
                        if step in (0, 2):
                            pe.wait_ge(kq_copied, min(i + 5, 2 * B * PAIRS))
                            output_turn(g)
                        if step in (1, 3):
                            pe.wait_ge(kq_copied, min(i + 5, 2 * B * PAIRS))
                            output(g)
                for g in (TILES - 2, TILES - 1):
                    pe.wait_ge(rows_done, g)
                    output_turn(g)
                    output(g)

            def heads_kv(a, h):
                n = a * H + h
                k, w = n % 2, ring[:, n % RING, :]
                pe.wait_ge(in_ring[n % RING], 16 * (n // RING + 1))
                if h >= 2:
                    pe.wait_ge(k_ready, n - 1)
                    pe.wait_ge(v_ready, n - 1)
                for d in range(DH):
                    mm(ps[:, k, 0:B * C], w[:, d * P:(d + 1) * P], ctxT[:, 0, d, :], start=(d == 0), stop=(d == 1))
                for d in range(DH):
                    last = mm(ps[:, k, 256:512], w[:, 256 + d * P:256 + (d + 1) * P], ctxT[:, h % 2, d, :],
                              start=(d == 0), stop=(d == 1))
                last.then_inc(kv_ps, 1)

            def turn_z(tile, n, bank=7):
                k = tile % 2
                pe.wait_ge(z_ready, n + 1)
                if n >= 1:
                    pe.wait_ge(h_ready, n)
                for d in range(DH):
                    last = nc.tensor.transpose(ps[:, bank, d * P:(d + 1) * P], z[:, k, 0, d * P:(d + 1) * P], ident[:, :])
                last.then_inc(zT_ps, 1)

            def keys(a, seq):
                l, i = ATTN[a]

                def products(h):
                    n = a * H + h
                    k, w = n % 2, ring[:, n % RING, :]
                    pe.wait_ge(k_ready, n + 1)
                    pe.wait_ge(kb_ready, n + 1)
                    if n >= 1:
                        pe.wait_ge(a_ready, n)
                    for d in range(DH):
                        mm(ps[:, 2 + d, 0:B * C + 1], w[:, 512 + d * P:512 + (d + 1) * P], KT[:, k, :], start=True, stop=True)
                    mm(ps[0:2, 4, 0:B * C + 1], col(f"{l}_bq{i}", 2 * h, 2), KT[:, k, :], start=True, stop=True).then_inc(a_ps, 1)
                    pe.wait_ge(v_ready, n + 1)
                    if h == 0:
                        pe.wait_ge(rows_done, rows_before(f"T{a}"))
                    if n >= 2:
                        pe.wait_ge(vw_act, n - 1)
                        pe.wait_ge(vw_dve, n - 1)
                    for g in range(2):
                        last = mm(ps[:, 5 + k, g * D:(g + 1) * D], VT[:, k, g * P:(g + 1) * P], w[:, 768:1024],
                                  start=True, stop=True)
                    last.then_inc(vw_ps, 1)
                    if h == 0:
                        pe.wait_ge(in_bv, 16 * (a + 1))
                    mm(ps[0:VO, 7, 0:D], bvz[:, h, :], w[:, 768:1024], start=(h == 0), stop=False).then_inc(head_used, 1)

                for h in range(H):
                    if h >= 1 and h + 1 < H:
                        heads_kv(a, h + 1)
                    if h == 1:
                        pe.wait_ge(h_ready, seq * TILES + 1)
                    products(h)
                    if h == 0:
                        turn_z(0, seq * TILES, bank=6)
                mm(ps[0:VO, 7, 0:D], e16[:, :], bo[:, a, :], start=False, stop=True).then_inc(vwb_ps, 1)

            def tokens(a, seq):
                base = seq * TILES
                pe.wait_ge(a_ready, H * (a + 1))
                pe.wait_ge(ones_ready, 1)

                def odd_bias_rows():
                    pe.wait_ge(vwb_ready, 2 * a + 1)
                    pe.wait_ge(vw_act, H * (a + 1))
                    pe.wait_ge(vw_dve, H * (a + 1))
                    mm(ps[0:VO, 6, 0:D], perm[:, :], VWb[:, 0, :], start=True, stop=True).then_inc(vwb_ps, 1)

                def scores(g):
                    n, k, b = base + g, g % 2, g // 2
                    pe.wait_ge(h_ready, n + 1)
                    if g >= 1:
                        pe.wait_ge(s_used, n)
                    for half in range(2):
                        if half == 1 and g >= 1:
                            turn_p(g - 1)
                        o = ps[:, half, :]
                        cols_of = slice(4 * half, 4 * half + 4)
                        sl = slice(2 * (b % 2), 2 * (b % 2) + 2)
                        for d in range(DH):
                            mm(o, hT[:, k, d, 0:P],
                               A[:, d, b // 2, cols_of, sl, :].rearrange("p r s k -> p r (s k)"),
                               start=(d == 0), stop=False)
                        last = mm(o, ones_r[:, :], cb[:, b // 2, cols_of, sl, :].rearrange("p r s k -> p r (s k)"),
                                  start=False, stop=True)
                        if half == 0:
                            last.then_inc(s_half, 1)
                    for d in range(DH):
                        mm(ps[:, 2, 0:H], hT[:, k, d, 0:P], Ab[:, d, b % 2, :], start=(d == 0), stop=False)
                    mm(ps[:, 2, 0:H], ones_r[:, :], cbb[:, b % 2, :], start=False, stop=True).then_inc(s_ps, 1)

                def turn_p(g):
                    n, k = base + g, g % 2
                    pe.wait_ge(p_ready, 8 * a + g + 1)
                    pe.wait_ge(p_half, 8 * a + g + 1)
                    if n >= 1:
                        pe.wait_ge(pT_act, n)
                    if 8 * a + g >= 1:
                        pe.wait_ge(pT_dve, 8 * a + g)
                    for c in range(PAIRS):
                        nc.tensor.transpose(ps[:, 3 + c // 4, (c % 4) * P:(c % 4 + 1) * P],
                                            prob[:, k, c * P:(c + 1) * P], ident[:, :])
                    nc.tensor.transpose(ps[0:VO, 5, 0:P], prob[:, k, H * C:PN], ident[:, :]).then_inc(pT_ps, 1)

                def output(g):
                    n, k, b = base + g, g % 2, g // 2
                    pe.wait_ge(pT_act, n + 1)
                    pe.wait_ge(pT_dve, 8 * a + g + 1)
                    if g == 0:
                        pe.wait_ge(vwb_ready, 2 * a + 2)
                    if g >= 1:
                        pe.wait_ge(rows_done, rows_before(f"T{a}") + g)
                    for c in range(PAIRS):
                        mm(ps[:, 6, 0:D], pT[:, k, c, :], VW[:, b, c, :], start=(c == 0), stop=False)
                    mm(ps[:, 6, 0:D], pT[0:VO, k, 8, :], VWb[:, b % 2, :], start=False, stop=True).then_inc(o_ps, 1)

                for i in range(TILES + 1):
                    if i < TILES:
                        scores(i)
                        if i == 0:
                            odd_bias_rows()
                    else:
                        if a % 2 == 0:
                            pe.wait_ge(s_used, base + TILES)
                            heads_kv(a + 1, 0)
                            heads_kv(a + 1, 1)
                        turn_p(i - 1)
                    if i + 1 < TILES:
                        turn_z(i + 1, base + i + 1)
                    if i >= 1:
                        output(i - 1)

            def attend2(seq):
                base = seq * TILES
                pe.wait_ge(rows_done, rows_before("L2"))
                pe.wait_ge(in_l2, 32)
                project(NJ0, NJ)
                pe.wait_ge(proj_act, act_jobs(NJ))
                pe.wait_ge(proj_dve, NJ // 2)

                def queries(g):
                    pe.wait_ge(h_ready, base + g + 1)
                    if g >= 1:
                        pe.wait_ge(q_ready, g)
                    for m in range(4):
                        for d in range(DH):
                            last = mm(ps[:, 4, m * P:(m + 1) * P], wp2[:, d, m * P:(m + 1) * P], hT[:, g % 2, d, 0:P],
                                      start=(d == 0), stop=(d == 1))
                    last.then_inc(q_ps, 1)

                def scores(g):
                    k, b = g % 2, g // 2
                    pe.wait_ge(q_ready, g + 1)
                    for h in range(H):
                        j, m = h % 4, h // 4
                        last = mm(ps[:, j, m * C:(m + 1) * C], qT2[32 * j:32 * j + 32, k, m, :],
                                  KC[32 * j:32 * j + 32, m, b * C:(b + 1) * C], start=True, stop=True)
                    last.then_inc(s_ps, 1)

                def turn_p(g):
                    n, k = base + g, g % 2
                    pe.wait_ge(e_ready, n + 1)
                    pe.wait_ge(pT_act, n)
                    for c in range(PAIRS):
                        last = nc.tensor.transpose(ps[:, 5 + c // 4, (c % 4) * P:(c % 4 + 1) * P],
                                                   prob[:, k, c * P:(c + 1) * P], ident[:, :])
                    last.then_inc(pT_ps, 1)

                def values(g):
                    n, k, b = base + g, g % 2, g // 2
                    pe.wait_ge(pT_act, n + 1)
                    for r in range(PAIRS):
                        at = 256 + r % 4 * 2 * VO
                        last = mm(ps[:, r // 4, at:at + 2 * VO], pT[:, k, r, :],
                                  VC[:, b, r, :, :].rearrange("p e c -> p (e c)"), start=True, stop=True)
                    last.then_inc(pv_ps, 1)

                def output(g):
                    pe.wait_ge(oT_ready, TILES + g + 1)
                    for d in range(DH):
                        last = mm(ps[:, 3, 256:512], oT[:, g % 2, d, :], vw2[:, 1, d, :], start=(d == 0), stop=(d == 1))
                    last.then_inc(o_ps, 1)

                def turns(gz, go):
                    if 1 <= gz <= TILES:
                        pe.wait_ge(h_ready, base + gz)
                    if 1 <= go <= TILES:
                        pe.wait_ge(oT_ready, TILES + go)
                    if 0 <= go < TILES:
                        pe.wait_ge(on_ready, go + 1)
                        for d in range(DH):
                            last = nc.tensor.transpose(ps[:, 7, 256 + d * P:256 + (d + 1) * P],
                                                       on[:, go % 2, d * P:(d + 1) * P], ident[:, :])
                        last.then_inc(oT_ps, 1)
                    if gz < TILES:
                        pe.wait_ge(z_ready, base + gz + 1)
                        for d in range(DH):
                            last = nc.tensor.transpose(ps[:, 7, d * P:(d + 1) * P],
                                                       z[:, gz % 2, 0, d * P:(d + 1) * P], ident[:, :])
                        last.then_inc(zT_ps, 1)

                turns(0, -1)
                turns(1, -1)
                queries(0)
                for i in range(TILES + 3):
                    if 1 <= i <= TILES:
                        pe.wait_ge(s_used, base + i)
                    if i >= 3:
                        pe.wait_ge(on_ready, i - 2)
                    if i >= 4:
                        pe.wait_ge(rows_done, rows_before("L2") + i - 3)
                    if 2 <= i < TILES + 2:
                        values(i - 2)
                    if i >= 3:
                        output(i - 3)
                    if i < TILES:
                        scores(i)
                    if 1 <= i <= TILES:
                        turn_p(i - 1)
                    if i + 1 < TILES:
                        queries(i + 1)
                    if i < TILES + 2:
                        turns(i + 2, i - 2)

            def mlp(l):
                base = l * B
                pe.wait_ge(in_mlp, 32 * (l + 1))

                def turn(b):
                    k = b % 2
                    pe.wait_ge(zm_ready, base + b + 1)
                    if b >= 1:
                        pe.wait_ge(hm_ready, base + b)
                    for d in range(DH):
                        for u in range(2):
                            last = nc.tensor.transpose(ps[:, 4, d * 256 + u * P:d * 256 + (u + 1) * P],
                                                       z[:, k, u, d * P:(d + 1) * P], ident[:, :])
                    last.then_inc(zmT_ps, 1)

                def up(b):
                    k = b % 2
                    pe.wait_ge(hm_ready, base + b + 1)
                    for f in range(FT):
                        if b >= 1 and f % 2 == 0:
                            pe.wait_ge(hid_ready, (base + b - 1) * FT + f + 2)
                        for d in range(DH):
                            last = mm(ps[:, f // 2, (f % 2) * 256:(f % 2 + 1) * 256], w1[:, d, f * P:(f + 1) * P],
                                      hT[:, k, d, :], start=(d == 0), stop=(d == 1))
                        last.then_inc(f1_ps, 1)

                def down(b):
                    k = b % 2
                    pe.wait_ge(hid_ready, (base + b + 1) * FT)
                    if b >= 1:
                        pe.wait_ge(rows_done, rows_before(f"M{l}") + b)
                    for u in range(2):
                        for f in range(FT):
                            last = mm(ps[:, 5 + u, 0:D], hid[:, k, f, u * P:(u + 1) * P], w2[:, f, :],
                                      start=(f == 0), stop=(f == FT - 1))
                    last.then_inc(f2_ps, 1)

                turn(0)
                pe.wait_ge(rows_done, rows_before(f"M{l}"))
                for i in range(B + 1):
                    if i < B:
                        up(i)
                    elif l % 2 == 0:
                        pe.wait_ge(hid_ready, (base + B - 1) * FT + 4)
                        heads_kv(l, 0)
                        heads_kv(l, 1)
                    if i + 1 < B:
                        turn(i + 1)
                    if i >= 1:
                        down(i - 1)

            pe.wait_ge(in_act, 16 * 3)
            pe.wait_ge(consts_ready, 1)
            pe.wait_ge(mask_ready, 1)
            project(0, NJ0)
            attend0()
            mlp(0)
            keys(0, 0)
            tokens(0, 0)
            keys(1, 1)
            tokens(1, 1)
            mlp(1)
            attend2(2)
            mlp(2)
            keys(2, 3)
            tokens(2, 3)
            keys(3, 4)
            tokens(3, 4)
            mlp(3)

        def job_out(eng, copy, n):
            kind, l, i, j = JOBS[n]
            o = ps[:, n % 7, :]
            pre = "L0" if l == 0 else "L2"
            if kind == "kc":
                return copy(KC[:, i, :], o[:, 0:B * C], col(f"{pre}_k_b", i))
            if kind == "v0":
                return copy(V0[:, i, :, 0:HD], o[:, 0:D].rearrange("p (h c) -> p h c", h=H), None)
            ov = o[:, 0:D].rearrange("p (r e c) -> p r e c", r=PAIRS, e=2)
            copy(VC[0:C, i, :, 0, 0:HD], ov[0:C, :, 0, :], None)
            return copy(VC[C:P, i, :, 1, 0:HD], ov[C:P, :, 1, :], None)

        @block.scalar
        def _(act):
            a_ = nc.scalar.activation

            def copy(out, in_, bias):
                if bias is None:
                    return a_(out, in_, ACT.Copy)
                return a_(out, in_, ACT.Identity, bias=bias)

            act.wait_ge(in_vec, 64)
            act.wait_ge(consts_ready, 1)
            for n in range(0, NJ0, 2):
                act.wait_ge(proj_ps, n + 1)
                job_out(act, copy, n).then_inc(proj_act, 1)

            def spread0(n):
                pair, w = n // 2, n % 2
                width = S if w else KEYS0
                act.wait_ge(kq_ps, n + 1)
                if n >= 2:
                    act.wait_ge(kq_ready, n - 1)
                a_(kq_full[:, n % 2, 0:width], ps[:, 7, 0:width], ACT.Identity,
                   bias=col("L0_q_b" if w else "L0_k_b", pair % PAIRS)).then_inc(kq_copied, 1)

            def exp0(n):
                act.wait_ge(nb_ready, n + 1)
                if n >= 2:
                    act.wait_ge(t0_ps, n - 1)
                for e in range(2):
                    j = 2 * (n % 2) + e
                    last = a_(prob[:, n % 2, e * KEYS0:(e + 1) * KEYS0], ps[:, j, 0:KEYS0], ACT.Exp,
                              bias=nb[:, n % 2, 1, e:e + 1], scale=1.0 / HD)
                last.then_inc(p0_ready, 1)

            def copy0(n):
                act.wait_ge(t0_ps, n + 1)
                k = n % 2
                if n >= 2:
                    act.wait_ge(pv0_ps, n - 1)
                a_(pT[:, k, 3:5, :], ps[:, 5, 0:2 * P].rearrange("p (c n) -> p c n", c=2), ACT.Copy).then_inc(pt0_act, 1)

            def turned_o(n, bias, at):
                k = n % 2
                act.wait_ge(oT_ps, n + 1)
                for d in range(DH):
                    last = a_(oT[:, k, d, :], ps[:, 7, at + d * P:at + (d + 1) * P], ACT.Identity, bias=col(bias, d))
                last.then_inc(oT_ready, 1)

            N = TILES * PAIRS
            for n in range(4):
                spread0(n)
            for i in range(N + 3):
                if i + 4 < 2 * B * PAIRS:
                    spread0(i + 4)
                if i < N:
                    exp0(i)
                if 2 <= i < N + 2:
                    copy0(i - 2)
                if OUT0 <= i < N and (i - OUT0) % (2 * PAIRS) in (0, 2):
                    turned_o(2 * ((i - OUT0) // (2 * PAIRS)) + (i - OUT0) % (2 * PAIRS) // 2, "L0_v_b", 0)
            turned_o(TILES - 2, "L0_v_b", 0)
            turned_o(TILES - 1, "L0_v_b", 0)

            def scaled(n, scale, offset, bank=7):
                k = n % 2
                act.wait_ge(zT_ps, n + 1)
                for d in range(DH):
                    last = a_(hT[:, k, d, 0:P], ps[:, bank, d * P:(d + 1) * P], ACT.Identity,
                              scale=col(scale, d), bias=col(offset, d))
                last.then_inc(h_ready, 1)

            def mlp(l, scale, offset, bias, gelu):
                base = l * B

                def turned(b):
                    k = b % 2
                    act.wait_ge(zmT_ps, base + b + 1)
                    for d in range(DH):
                        last = a_(hT[:, k, d, :], ps[:, 4, d * 256:(d + 1) * 256], ACT.Identity,
                                  scale=col(scale, d), bias=col(offset, d))
                    last.then_inc(hm_ready, 1)

                turned(0)
                for b in range(B):
                    if b >= 2:
                        act.wait_ge(f2_ps, base + b - 1)
                    for f in range(FT):
                        if f % 2 == 0:
                            act.wait_ge(f1_ps, (base + b) * FT + f + 2)
                        a_(hid[:, b % 2, f, :], ps[:, f // 2, (f % 2) * 256:(f % 2 + 1) * 256], gelu,
                           bias=col(bias, f)).then_inc(hid_ready, 1)
                    if b + 1 < B:
                        turned(b + 1)

            def keys(a, seq):
                l, i = ATTN[a]
                for step in range(H + 1):
                    n = a * H + step
                    k = n % 2
                    if step < H:
                        act.wait_ge(kv_ps, n + 1)
                        if n >= 2:
                            act.wait_ge(a_ps, n - 1)
                        a_(KT[:, k, 0:B * C], ps[:, k, 0:B * C], ACT.Identity, bias=col(f"{l}_bk{i}", step))\
                            .then_inc(k_ready, 1)
                        if n >= 2:
                            act.wait_ge(vw_ps, n - 1)
                        a_(VT[:, k, :], ps[:, k, 256:512], ACT.Identity, bias=col(f"{l}_bv{i}", step))\
                            .then_inc(v_ready, 1)
                    if step >= 1:
                        n, h = n - 1, step - 1
                        act.wait_ge(vw_ps, n + 1)
                        a_(VW[C:P, 1 - h % 2:B:2, h // 2, :], ps[C:P, 5 + n % 2, :].rearrange("p (g n) -> p g n", g=2),
                           ACT.Copy).then_inc(vw_act, 1)
                    if step == 1:
                        scaled(seq * TILES, f"{l}_ln{i}_scale", f"{l}_ln{i}_offset", bank=6)

            def tokens(a, seq):
                base = seq * TILES
                l, i = ATTN[a]
                for g in range(TILES + 1):
                    if g >= 1:
                        n, k = base + g - 1, (g - 1) % 2
                        act.wait_ge(pT_ps, n + 1)
                        a_(pT[:, k, 0:4, :], ps[:, 3, :].rearrange("p (c n) -> p c n", c=4), ACT.Copy).then_inc(pT_act, 1)
                    if g + 1 < TILES:
                        scaled(base + g + 1, f"{l}_ln{i}_scale", f"{l}_ln{i}_offset")
                    if g < TILES:
                        n, k = base + g, g % 2
                        act.wait_ge(sub_half, 8 * a + g + 1)
                        a_(prob[:, k, 0:HALF], prob[:, k, 0:HALF], ACT.Exp, scale=float(HK) ** -0.5).then_inc(e_half, 1)
                        act.wait_ge(s_used, n + 1)
                        a_(prob[:, k, HALF:H * C + H], prob[:, k, HALF:H * C + H], ACT.Exp, scale=float(HK) ** -0.5)\
                            .then_inc(e_ready, 1)

            def attend2(seq):
                base = seq * TILES
                for n in range(NJ0, NJ, 2):
                    act.wait_ge(proj_ps, n + 1)
                    job_out(act, copy, n).then_inc(proj_act, 1)
                scaled(base, "L2_ln1_w", "L2_ln1_b")
                scaled(base + 1, "L2_ln1_w", "L2_ln1_b")
                for i in range(TILES + 2):
                    if 1 <= i <= TILES:
                        n, k = base + i - 1, (i - 1) % 2
                        act.wait_ge(pT_ps, n + 1)
                        for half in range(2):
                            last = a_(pT[:, k, 4 * half:4 * half + 4, :],
                                      ps[:, 5 + half, :].rearrange("p (c n) -> p c n", c=4), ACT.Copy)
                        last.then_inc(pT_act, 1)
                    if i < TILES:
                        n, k = base + i, i % 2
                        act.wait_ge(s_used, n + 1)
                        a_(prob[:, k, 0:H * C], prob[:, k, 0:H * C], ACT.Exp, scale=float(HD) ** -0.5)\
                            .then_inc(e_ready, 1)
                    if i >= 2:
                        if i + 2 < TILES:
                            act.wait_ge(zT_ps, base + i + 3)
                        turned_o(TILES + i - 2, "L2_v_b", 256)
                    if i + 2 < TILES:
                        scaled(base + i + 2, "L2_ln1_w", "L2_ln1_b")

            mlp(0, "L0_postnorm_w", "zero", "L0_mlp_b1", ACT.Gelu_apprx_tanh)
            keys(0, 0)
            tokens(0, 0)
            keys(1, 1)
            tokens(1, 1)
            mlp(1, "L1_ln_mlp_scale", "L1_ln_mlp_offset", "L1_b_fc1", ACT.Gelu)
            attend2(2)
            mlp(2, "L2_ln2_w", "L2_ln2_b", "L2_fc_b", ACT.Gelu_apprx_tanh)
            keys(2, 3)
            tokens(2, 3)
            keys(3, 4)
            tokens(3, 4)
            mlp(3, "L3_ln_mlp_scale", "L3_ln_mlp_offset", "L3_b_fc1", ACT.Gelu)

        @block.vector
        def _(dve):
            v = nc.vector
            steps = [0]

            def link(ins):
                steps[0] += 1
                ins.then_inc(dve_step, 1)
                dve.wait_ge(dve_step, steps[0])

            def copy(out, in_, bias):
                if bias is None:
                    return v.tensor_copy(out, in_)
                return v.tensor_scalar(out, in_, bias, None, ALU.add)

            dve.wait_ge(in_vec, 64)
            link(v.tensor_copy(mask[:, 0, :], mask_i[:, :]))
            link(v.tensor_scalar(mask[:, 0, :], mask[:, 0, :], 0.0, MASKED, ALU.is_equal, ALU.mult))
            link(v.tensor_copy(mask[:, 1, :], mask_u[:, :]))
            v.tensor_scalar(mask[:, 1, :], mask[:, 1, :], 0.0, MASKED, ALU.is_equal, ALU.mult).then_inc(mask_ready, 1)

            dve.wait_ge(consts_ready, 1)
            v.tensor_copy(ones_r[:, :], ones[:, :]).then_inc(ones_ready, 1)
            for n in range(1, NJ0, 2):
                dve.wait_ge(proj_ps, n + 1)
                job_out(dve, copy, n).then_inc(proj_dve, 1)

            def max0(n):
                dve.wait_ge(s0_ps, n + 1)
                if n >= 2:
                    dve.wait_ge(p0_ready, n - 1)
                j = 2 * (n % 2)
                link(v.tensor_reduce(nb[:, n % 2, 0, :], ps[:, j:j + 2, 0:KEYS0], AX.X, ALU.max))
                v.tensor_scalar(nb[:, n % 2, 1, :], nb[:, n % 2, 0, :], -1.0 / HD, None, ALU.mult).then_inc(nb_ready, 1)

            def copy0(n):
                dve.wait_ge(t0_ps, n + 1)
                if n >= 2:
                    dve.wait_ge(pv0_ps, n - 1)
                v.tensor_copy(pT[:, n % 2, 0:3, :], ps[:, 4, 0:3 * P].rearrange("p (c n) -> p c n", c=3))\
                    .then_inc(pt0_dve, 1)

            def normal0(n):
                pair, k = n // 2, n % 2
                b, r = pair // PAIRS, pair % PAIRS
                dve.wait_ge(pv0_ps, n + 1)
                o = ps[:, 6, 0:2 * VO].rearrange("p (h c) -> p h c", h=2)
                link(v.reciprocal(rinv[:, k, 0:2], o[:, :, HD]))
                v.tensor_tensor(on0[:, 2 * b + k, 2 * HD * r:2 * HD * (r + 1)].rearrange("p (h c) -> p h c", h=2),
                                o[:, :, 0:HD], rinv[:, k, 0:2].unsqueeze(2).broadcast_to([P, 2, HD]), ALU.mult)\
                    .then_inc(pv0_used, 1)

            def rows0(g):
                dve.wait_ge(o_ps, g + 1)
                dve.wait_ge(xb_ready, g + 1)
                v.tensor_tensor(x0[:, g, :], ps[:, 7, 256:512], x0[:, g, :], ALU.add).then_inc(rows_done, 1)

            N = TILES * PAIRS
            for i in range(N + 4):
                if i < N:
                    max0(i)
                if i >= 4:
                    normal0(i - 4)
                if 2 <= i < N + 2:
                    copy0(i - 2)
                if OUT0 <= i < N and (i - OUT0) % (2 * PAIRS) in (1, 3):
                    rows0(2 * ((i - OUT0) // (2 * PAIRS)) + (i - OUT0) % (2 * PAIRS) // 2)

            def spread(src, k, u, rms):
                if rms:
                    link(v.tensor_tensor_reduce(sq[:, :], src, src, 1.0 / D, 0.0, ALU.mult, ALU.add, mv[:, k, u, 1:2]))
                else:
                    link(v.bn_stats(stat[:, k, u, :], src))
                    link(v.bn_aggr(mv[:, k, u, :], stat[:, k, u, :]))
                return v.tensor_scalar(var[:, k, u:u + 1], mv[:, k, u, 1:2], 1e-6 if rms else 1e-5, None, ALU.add)

            def normalise(dst, src, k, u, rms):
                if rms:
                    return v.tensor_scalar(dst, src, rstd[:, k, u:u + 1], None, ALU.mult)
                return v.tensor_scalar(dst, src, mv[:, k, u, 0:1], rstd[:, k, u:u + 1], ALU.subtract, ALU.mult)

            def mlp_spread(l, b):
                src, rms = (x0, True) if l == 0 else (x, False)
                for u in range(2):
                    last = spread(src[:, 2 * b + u, :], b % 2, u, rms)
                last.then_inc(var_ready, 1)

            def mlp_z(l, b):
                src, rms = (x0, True) if l == 0 else (x, False)
                k = b % 2
                if b >= 2:
                    dve.wait_ge(zmT_ps, l * B + b - 1)
                dve.wait_ge(rstd_ready, norms_before(f"M{l}") + b + 1)
                for u in range(2):
                    last = normalise(z[:, k, u, :], src[:, 2 * b + u, :], k, u, rms)
                last.then_inc(zm_ready, 1)

            def mlp(l):
                base = l * B
                dve.wait_ge(rows_done, rows_before(f"M{l}"))
                mlp_spread(l, 1)
                mlp_z(l, 1)
                for b in range(B):
                    if b + 2 < B:
                        mlp_spread(l, b + 2)
                        mlp_z(l, b + 2)
                    if l == 1 and b == B - 1:
                        dve.wait_ge(zmT_ps, base + B)
                        dve.wait_ge(rows_done, rows_before("M1") + B // 2 + 1)
                        first_z2()
                    dve.wait_ge(f2_ps, base + b + 1)
                    dve.wait_ge(xb_ready, TILES * XB_AT[f"M{l}"] + 2 * b + 2)
                    v.tensor_tensor(x[:, 2 * b:2 * b + 2, :], ps[:, 5:7, 0:D], x[:, 2 * b:2 * b + 2, :], ALU.add)\
                        .then_inc(rows_done, 1)

            def first_z2():
                tile_spread(0)
                tile_spread(1)
                for g in range(2):
                    tile_z("L2", 2 * TILES + g, g)
                    tile_spread(g + 2)

            CBP = COLS["cb_parts"][0]

            def keys(a, seq):
                dve.wait_ge(rows_done, rows_before(f"T{a}"))
                tile_spread(0)
                tile_spread(1)
                tile_z(f"T{a}", seq * TILES, 0)
                for h in range(H):
                    n = a * H + h
                    k, par = n % 2, h % 2
                    dve.wait_ge(a_ps, n + 1)
                    slots = slice(0, 4, 3) if par == 0 else slice(1, 3)
                    for d in range(DH):
                        v.tensor_copy(A[:, d, :, h // 2, slots, :],
                                      ps[:, 2 + d, 0:B * C].rearrange("p (g s k) -> p g s k", g=2, s=2))
                    link(v.tensor_scalar(cb_round[:, :], ps[0:2, 4, 0:B * C + 1], cols[0:2, CBP + 1:CBP + 2], None,
                                         ALU.mult))

                    def parts(dst, lo, hi, fold):
                        return v.scalar_tensor_tensor(dst, fold(ps[0:2, 4, lo:hi]), cols[0:2, CBP:CBP + 1],
                                                      fold(cb_round[:, lo:hi].bitcast(F32)), ALU.mult, ALU.add)

                    for g in range(2):
                        parts(cb[:, g, h // 2, slots, :], 2 * g * C, 2 * (g + 1) * C,
                              lambda ap: ap.rearrange("p (s k) -> p s k", s=2))
                    for e in range(2):
                        at = h ^ e
                        v.tensor_copy(Ab[:, :, e, at:at + 1], ps[:, 2:4, B * C:B * C + 1])
                        last = parts(cbb[:, e, at:at + 1], B * C, B * C + 1, lambda ap: ap)
                    last.then_inc(a_ready, 1)
                    dve.wait_ge(vw_ps, n + 1)
                    v.tensor_copy(VW[0:C, par:B:2, h // 2, :], ps[0:C, 5 + k, :].rearrange("p (g n) -> p g n", g=2))\
                        .then_inc(vw_dve, 1)
                dve.wait_ge(vwb_ps, 2 * a + 1)
                v.tensor_copy(VWb[:, 0, :], ps[0:VO, 7, 0:D]).then_inc(vwb_ready, 1)

            def tile_spread(g):
                spread(x[:, g, :], g % 2, 0, False).then_inc(var_ready, 1)

            def tile_z(phase, n, g):
                k = g % 2
                if n >= 2:
                    dve.wait_ge(zT_ps, n - 1)
                dve.wait_ge(rstd_ready, norms_before(phase) + g + 1)
                normalise(z[:, k, 0, :], x[:, g, :], k, 0, False).then_inc(z_ready, 1)

            def tokens(a, seq):
                base = seq * TILES
                for g in range(TILES + 1):
                    if g + 2 < TILES:
                        tile_spread(g + 2)
                    if g + 1 < TILES:
                        tile_z(f"T{a}", base + g + 1, g + 1)
                    if g == TILES and a % 2 == 1:
                        dve.wait_ge(rows_done, rows_before(f"T{a}") + 2)
                        mlp_spread(a, 0)
                    n, k = base + g, g % 2
                    if g < TILES:
                        main = [ps[:, half, :].rearrange("p (h c) -> p h c", c=C) for half in range(2)]
                        dve.wait_ge(s_half, 8 * a + g + 1)
                        v.tensor_reduce(mx[:, k, 0:H // 2], main[0], AX.X, ALU.max)
                    if g >= 1:
                        dve.wait_ge(pT_ps, n)
                        v.tensor_copy(pT[:, 1 - k, 4:8, :], ps[:, 4, :].rearrange("p (c n) -> p c n", c=4))
                        v.tensor_copy(pT[0:VO, 1 - k, 8, :], ps[0:VO, 5, 0:P]).then_inc(pT_dve, 1)
                    if g == TILES and a % 2 == 1:
                        mlp_z(a, 0)
                    if g < TILES:
                        pm = [prob[:, k, half * HALF:(half + 1) * HALF].rearrange("p (h c) -> p h c", c=C)
                              for half in range(2)]
                        pb = prob[:, k, H * C:H * C + H]

                        def of(stats, half):
                            return stats[:, k, half * H // 2:(half + 1) * H // 2].unsqueeze(2)\
                                .broadcast_to([P, H // 2, C])

                        dve.wait_ge(s_ps, n + 1)
                        link(v.tensor_reduce(mx[:, k, H // 2:H], main[1], AX.X, ALU.max))
                        link(v.tensor_tensor(mx2[:, k, :], mx[:, k, :], ps[:, 2, 0:H], ALU.max))
                        v.tensor_tensor(pm[0], main[0], of(mx2, 0), ALU.subtract).then_inc(sub_half, 1)
                        v.tensor_tensor(pm[1], main[1], of(mx2, 1), ALU.subtract)
                        v.tensor_tensor(pb, ps[:, 2, 0:H], mx2[:, k, :], ALU.subtract).then_inc(s_used, 1)
                        if g == 0:
                            dve.wait_ge(vwb_ps, 2 * a + 2)
                            v.tensor_copy(VWb[:, 1, :], ps[0:VO, 6, 0:D]).then_inc(vwb_ready, 1)
                        dve.wait_ge(e_half, 8 * a + g + 1)
                        v.tensor_reduce(sm[:, k, 0:H // 2], pm[0], AX.X, ALU.add)
                        dve.wait_ge(e_ready, n + 1)
                        link(v.tensor_reduce(sm[:, k, H // 2:H], pm[1], AX.X, ALU.add))
                        link(v.tensor_tensor(sm[:, k, :], sm[:, k, :], pb, ALU.add))
                        v.reciprocal(rinv[:, k, :], sm[:, k, :]).then_inc(rinv_ready, 1)
                        dve.wait_ge(rinv_ready, 8 * a + g + 1)
                        v.tensor_tensor(pm[1], pm[1], of(rinv, 1), ALU.mult).then_inc(p_half, 1)
                    if g >= 1:
                        dve.wait_ge(o_ps, TILES + base + g)
                        v.tensor_tensor(x[:, g - 1, :], ps[:, 6, 0:D], x[:, g - 1, :], ALU.add).then_inc(rows_done, 1)

            def attend2(seq):
                base = seq * TILES
                dve.wait_ge(rows_done, rows_before("L2"))
                for n in range(NJ0 + 1, NJ, 2):
                    dve.wait_ge(proj_ps, n + 1)
                    job_out(dve, copy, n).then_inc(proj_dve, 1)

                def queries(g):
                    dve.wait_ge(q_ps, g + 1)
                    v.tensor_tensor(qT2[:, g % 2, :, :], ps[:, 4, :].rearrange("p (m n) -> p m n", m=4),
                                    col("L2_q_b", 0, 4).unsqueeze(2).broadcast_to([P, 4, P]), ALU.add)\
                        .then_inc(q_ready, 1)

                def values(g):
                    k = g % 2
                    dve.wait_ge(pv_ps, g + 1)
                    o = ps[:, 0:2, 256:256 + PAIRS * VO].rearrange("p q (h c) -> p q h c", h=PAIRS)
                    rk = rinv[:, k, :].rearrange("p (q h) -> p q h", q=2)
                    link(v.reciprocal(rk, o[:, :, :, HD]))
                    v.tensor_tensor(on[:, k, :].rearrange("p (q h c) -> p q h c", q=2, h=PAIRS), o[:, :, :, 0:HD],
                                    rk.unsqueeze(3).broadcast_to([P, 2, PAIRS, HD]), ALU.mult).then_inc(on_ready, 1)

                tile_z("L2", base + 2, 2)
                queries(0)
                for i in range(TILES + 3):
                    if i < TILES:
                        dve.wait_ge(s_ps, base + i + 1)
                    if 2 <= i < TILES + 2:
                        values(i - 2)
                    if i < TILES:
                        k = i % 2
                        main = ps[:, 0:4, 0:4 * C].rearrange("p j (m c) -> p j m c", c=C)
                        mj = mx[:, k, :].rearrange("p (j m) -> p j m", j=4)
                        pm = prob[:, k, 0:H * C].rearrange("p (m j c) -> p j m c", m=4, j=4)
                        link(v.tensor_reduce(mj, main, AX.X, ALU.max))
                        v.tensor_tensor(pm, main, mj.unsqueeze(3).broadcast_to([P, 4, 4, C]), ALU.subtract)\
                            .then_inc(s_used, 1)
                    if i == TILES:
                        dve.wait_ge(rows_done, rows_before("L2") + 2)
                        mlp_spread(2, 0)
                    if i == TILES + 1:
                        mlp_z(2, 0)
                    if i >= 3:
                        g = i - 3
                        dve.wait_ge(o_ps, TILES + base + g + 1)
                        dve.wait_ge(xb_ready, TILES * XB_AT["L2"] + g + 1)
                        v.tensor_tensor(x[:, g, :], ps[:, 3, 256:512], x[:, g, :], ALU.add).then_inc(rows_done, 1)
                    if i + 1 < TILES:
                        queries(i + 1)
                    if i + 4 < TILES:
                        tile_spread(i + 4)
                    if i + 3 < TILES:
                        tile_z("L2", base + i + 3, i + 3)

            XB_AT = {"M0": 1, "M1": 2, "L2": 3, "M2": 4, "M3": 5}
            dve.wait_ge(rows_done, 2)
            mlp_spread(0, 0)
            rows0(TILES - 2)
            mlp_z(0, 0)
            rows0(TILES - 1)
            mlp(0)
            keys(0, 0)
            tokens(0, 0)
            keys(1, 1)
            tokens(1, 1)
            mlp(1)
            attend2(2)
            mlp(2)
            keys(2, 3)
            tokens(2, 3)
            keys(3, 4)
            tokens(3, 4)
            mlp(3)


def _halves(w):
    return np.ascontiguousarray(np.asarray(w).reshape(-1, P, w.shape[-1]).transpose(1, 0, 2))


def _padded(w):
    out = np.zeros((w.shape[0], H, 32), w.dtype)
    out[:, :, :HD] = w.reshape(w.shape[0], H, HD)
    return out.reshape(w.shape[0], H * 32)


def _spread(w):
    out = np.zeros((w.shape[0], H, 4, HD), w.dtype)
    out[:, :, :3] = w.reshape(w.shape[0], H, 1, HD)
    return out.reshape(w.shape[0], H * 4 * HD)


def _spread_bias(v, row48):
    out = np.zeros((H, 4, HD), v.dtype)
    out[:, :3] = v.reshape(H, 1, HD)
    out[:, 3, 0] = row48
    return out.reshape(PAIRS, P).T


def _parts(blocks):
    one = np.repeat([(1.0, -1.0) if b == "L" else (0.0, 1.0) for b in blocks], HD, axis=0)
    return np.tile(one, (2, 1)).astype(np.float32)


def _padded_bias(v, row16):
    out = np.zeros((H, 32), v.dtype)
    out[:, :HD] = v.reshape(H, HD)
    out[:, HD] = row16
    return out.reshape(4, P).T


def _layout(i):
    i = {k.replace("_xattn_", "_"): np.asarray(v) for k, v in i.items()}
    f = np.float32
    kvw = i["L0_kv_w"].reshape(D, D, 2)
    kvb = i["L0_kv_b"].reshape(D, 2)
    kin = np.concatenate([i["ctx_2048"], i["x"]], axis=1)
    kinT = _halves(np.ascontiguousarray(kin.reshape(B * KEYS0, D).T)).reshape(P, DH, B, KEYS0)
    cT = np.ascontiguousarray(i["ctx_2048"].reshape(B * C, D).T)
    cTs = np.ascontiguousarray(cT.reshape(D, 2, 2, C)[:, :, ::-1].reshape(D, B * C))
    cD = np.repeat(cT.reshape(D, B, 1, C), 2, axis=2).reshape(D, B * 2 * C)
    cols = np.zeros((P, NCOLS), f)
    for name, (at, n) in COLS.items():
        if name == "zero":
            continue
        if name == "cb_parts":
            v = np.zeros((P, 2), f)
            v[0:2] = ((0.0, 1.0), (1.0, -1.0))
        elif name == "q_parts":
            v = _parts("HHLH")
        elif name == "k_parts":
            v = _parts("HLHH")
        elif "_bq" in name:
            v = np.repeat(i[name].reshape(H, P), 2, axis=0).T
        elif name == "L0_k_b":
            v = _spread_bias(kvb[:, 0], 0.0)
        elif name == "L0_q_b":
            v = _spread_bias(i[name], 1.0)
        elif name == "L0_v_b":
            v = kvb[:, 1].reshape(n, P).T
        elif name == "L2_q_b":
            v = _padded_bias(i[name], 1.0)
        elif name == "L2_k_b":
            v = _padded_bias(i[name], 0.0)
        else:
            v = i[name].reshape(n, P).T
        cols[:, at:at + n] = v
    brow = np.stack([i[r] for r in ROWS])
    heads = np.zeros((4, H, P, WIDTH), f)
    bvz = np.zeros((4, P, H, VO), f)
    for a, (l, k) in enumerate(ATTN):
        wk = i[f"{l}_wk{k}"].reshape(DH, P, H, HK).transpose(2, 1, 0, 3).reshape(H, P, D)
        wv = i[f"{l}_wv{k}"].reshape(DH, P, H, HK).transpose(2, 1, 0, 3).reshape(H, P, D)
        wqT = i[f"{l}_wq{k}"].T.reshape(H, HK, D)
        wo = i[f"{l}_wo{k}"].reshape(H, HK, D)
        heads[a] = np.concatenate([wk, wv, wqT, wo], axis=2)
        bv = i[f"{l}_bias_v{k}"].reshape(H, HK)
        for h in range(H):
            bvz[a, :, h, h] = bv[h]
    return {
        "ctxT": np.stack([_halves(cT), _halves(cTs)], axis=1),
        "ctxD": _halves(cD).reshape(P, DH, B, 2 * C),
        "kinT": kinT,
        "x": np.ascontiguousarray(i["x"].reshape(TILES, P, D).transpose(1, 0, 2)),
        "cols": cols,
        "mask_i": i["mask_BxS2_ik0"].reshape(1, B * C),
        "mask_u": np.ascontiguousarray(i["mask_BxS2_bf1"]).view(np.uint8).reshape(1, B * C),
        "bo": np.stack([i[f"{l}_bo{k}"] for l, k in ATTN])[None],
        "ws0": np.stack([_halves(_spread(i["L0_q_w"])), _halves(_spread(kvw[:, :, 0]))], axis=2)
        .reshape(P, DH, 2, PAIRS, P),
        "vw0": _halves(np.ascontiguousarray(kvw[:, :, 1])),
        "ow0": _halves(i["L0_out_w"]),
        "wp2": _halves(np.concatenate([_padded(i["L2_q_w"]), _padded(i["L2_k_w"])], axis=1)),
        "vw2": np.stack([_halves(i["L2_v_w"]), _halves(i["L2_cproj_w"])], axis=1),
        "brow": brow,
        "w1": np.stack([_halves(i[k]) for k in ("L0_mlp_w1", "L1_w_fc1", "L2_fc_w", "L3_w_fc1")]),
        "w2": np.stack([_halves(i[k]) for k in ("L0_mlp_w2", "L1_w_fc2", "L2_proj_w", "L3_w_fc2")]),
        "bvz": bvz,
        "heads": heads,
    }


def kernel(**inputs):
    import concourse.bacc as bacc
    from concourse.bass_utils import run_bass_kernel_spmd

    nc = bacc.Bacc("TRN2", target_bir_lowering=False, num_devices=1)
    arrays, t = {}, {}
    for name, a in _layout(inputs).items():
        a = np.ascontiguousarray(a)
        arrays[f"in_{name}_dram"] = a
        t[name] = nc.dram_tensor(f"in_{name}_dram", a.shape, mybir.dt.from_np(a.dtype), kind="ExternalInput").ap()
    t["brow"] = t["brow"].unsqueeze(0).broadcast_to([P, len(ROWS), D])
    out = nc.dram_tensor("out_0_dram", (B, S, D), F32, kind="ExternalOutput").ap()
    t["out"] = [out[b].rearrange("(u p) n -> p u n", p=P) for b in range(B)]
    build(nc, t)
    r = run_bass_kernel_spmd(nc, [arrays], core_ids=[0])
    return r.results[0]["out_0_dram"]
```

```python
import numpy as np
from contextlib import ExitStack

import concourse.bass as bass
from concourse import mybir

F32 = mybir.dt.float32
F32R = mybir.dt.float32r
I32 = mybir.dt.int32
U8 = mybir.dt.uint8
ACT = mybir.ActivationFunctionType
ALU = mybir.AluOpType
AX = mybir.AxisListType

P = 128
D = 256
DH = D // P
B = 4
S = 256
C = 64
TOK = B * S
TILES = TOK // P
H = 16
PAIRS = H // 2
HD = 16
HK = 128
F = 1024
FT = F // P
KEYS0 = S + C
VO = HD + 1
MASKED = -1.0e30
WIDTH = 4 * D
RING = 3
ATTN = [("L1", 1), ("L1", 2), ("L3", 1), ("L3", 2)]

COLS = {}


def _col(name, n):
    COLS[name] = (sum(w for _, w in COLS.values()), n)


for _l, _i in ATTN:
    _col(f"{_l}_bq{_i}", 2 * H)
    for _v in ("bk", "bv", "bias_k"):
        _col(f"{_l}_{_v}{_i}", H)
    _col(f"{_l}_ln{_i}_scale", DH)
    _col(f"{_l}_ln{_i}_offset", DH)
for _l in ("L1", "L3"):
    _col(f"{_l}_ln_mlp_scale", DH)
    _col(f"{_l}_ln_mlp_offset", DH)
    _col(f"{_l}_b_fc1", FT)
_col("L0_q_b", DH)
_col("L0_k_b", DH)
_col("cb_parts", 2)
_col("row48", 1)
_col("L0_v_b", DH)
_col("L0_postnorm_w", DH)
_col("L0_mlp_b1", FT)
_col("L2_ln1_w", DH)
_col("L2_ln1_b", DH)
_col("L2_q_b", 4)
_col("L2_k_b", 4)
_col("L2_v_b", DH)
_col("L2_ln2_w", DH)
_col("L2_ln2_b", DH)
_col("L2_fc_b", FT)
_col("zero", DH)
NCOLS = sum(w for _, w in COLS.values())
ROWS = ["L0_out_b", "L0_mlp_b2", "L1_b_fc2", "L2_cproj_b", "L2_proj_b", "L3_b_fc2"]

UPDATES = [("L0", TILES), ("M0", B), ("T0", TILES), ("T1", TILES), ("M1", B),
           ("L2", TILES), ("M2", B), ("T2", TILES), ("T3", TILES), ("M3", B)]


def rows_before(phase):
    n = 0
    for name, k in UPDATES:
        if name == phase:
            return n
        n += k
    return n


def norms_before(phase):
    n = 0
    for name, k in UPDATES[1:]:
        if name == phase:
            return n
        n += k
    return n


def build(nc, t):
    ctx = ExitStack()
    with ctx:
        def sb(name, shape, dt=F32):
            return ctx.enter_context(nc.sbuf_tensor(name, shape, dt))

        def sem(name):
            return ctx.enter_context(nc.semaphore(name))

        x = sb("x", [P, TILES, D])
        ctxT = sb("ctxT", [P, 2, DH, B * C])
        cols = sb("cols", [P, NCOLS])
        brow = sb("brow", [P, len(ROWS), D])
        ident = sb("ident", [P, P])
        perm = sb("perm", [VO, VO])
        ones = sb("ones", [2, P])
        ones_r = sb("ones_r", [2, P], F32R)
        e16 = sb("e16", [1, VO])
        e16q = sb("e16q", [1, P])
        e48 = sb("e48", [P, P])
        mask_i = sb("mask_i", [P, B * C], I32)
        mask_u = sb("mask_u", [1, B * C], U8)
        mask = sb("mask", [P, 2, B * C])
        arena = sb("arena", [P, 16384])
        A = arena[:, 0:8192].rearrange("p (d g r s k) -> p d g r s k", d=DH, g=2, r=PAIRS, s=4)
        VW = arena[:, 8192:16384].rearrange("p (b r n) -> p b r n", b=B, r=PAIRS)
        oT0 = arena[:, 0:2 * 2 * DH * P].rearrange("p (k u d n) -> p k u d n", k=2, u=2, d=DH)
        kinT = arena[:, 2048:4608].rearrange("p (d b n) -> p d b n", d=DH, b=B)
        w0 = arena[:, 4608:5632].rearrange("p (w d n) -> p w d n", w=2, d=DH)
        V0 = arena[:, 5632:9728].rearrange("p (t r c) -> p t r c", t=TILES, r=PAIRS)
        vw0 = arena[:, 9728:10240].rearrange("p (d n) -> p d n", d=DH)
        ow0 = arena[:, 10240:10752].rearrange("p (d n) -> p d n", d=DH)
        copies_f = arena[:, 10752:11264].rearrange("p (w c n) -> p w c n", w=2, c=2)
        x0 = arena[:, 11264:13312].rearrange("p (t n) -> p t n", t=TILES)
        VC0 = arena[:, 13312:14336].rearrange("p (b r c) -> p b r c", b=B, r=PAIRS)
        prob0 = arena[:, 14336:14336 + 3 * 2 * KEYS0].rearrange("p (k n) -> p k n", k=3)
        HL = sb("HL", [P, DH, 2, KEYS0 + S], F32R)
        copies = sb("copies", [P, 2, 2, P], F32R)
        KQ = sb("KQ", [P, 3, 2, KEYS0], F32R)
        kq_full = arena[:, 1024:1024 + 2 * KEYS0].rearrange("p (k n) -> p k n", k=2)
        KC = arena[:, 5632:9728].rearrange("p (m b n) -> p m b n", m=4, b=B)
        VC = sb("VC", [P, B, PAIRS, 2, VO])
        ctxD = sb("ctxD", [P, DH, B, 2 * C])
        Ab = sb("Ab", [P, DH, 2 * H])
        cb = sb("cb", [2, 2, PAIRS, 4, C], F32R)
        cbb = sb("cbb", [2, 2 * H], F32R)
        cb_round = sb("cb_round", [2, B * C + 2], F32R)
        VWb = sb("VWb", [VO, 2, D])
        bvz = sb("bvz", [P, H, VO])
        bo = sb("bo", [1, 4, D])
        ring = sb("ring", [P, RING, WIDTH])
        wp2 = ring[:, 0:2, :]
        vw2 = ring[:, 2, :].rearrange("p (w d n) -> p w d n", w=2, d=DH)
        w1 = sb("w1", [P, DH, F])
        w2 = sb("w2", [P, FT, D])
        KW = B * C + 2
        split_a = HL[:, :, :, :].rearrange("p m c n -> p (m c n)")
        VT = split_a[:, 0:4 * B * C].rearrange("p (k c n) -> p k c n", k=2, c=2)
        KT = split_a[:, 4 * B * C:4 * B * C + 4 * KW].rearrange("p (k c n) -> p k c n", k=2, c=2)
        split_b = KQ[:, :, :, :].rearrange("p k w n -> p (k w n)")
        bvs = split_b[:, 0:2 * H * VO].rearrange("p (c n) -> p c n", c=2)
        bqs = split_b[:, 2 * H * VO:2 * H * VO + 4 * H].rearrange("p (c n) -> p c n", c=2)
        ww = sb("ww", [P, 2, 2, 2 * D], F32R)
        z = sb("z", [P, 2, 2, D])
        hT = sb("hT", [P, 2, DH, 2 * P])
        stat = sb("stat", [P, 2, 2, 6])
        mv = sb("mv", [P, 2, 2, 2])
        var = sb("var", [P, 2, 2])
        rstd = sb("rstd", [P, 2, 2])
        neg_half = sb("neg_half", [P, 2])
        sq = sb("sq", [P, D])
        PN = H * C + H + 1
        prob = sb("prob", [P, 2, PN])
        pT = sb("pT", [P, 2, 9, P])
        mx = sb("mx", [P, 2, H])
        mx2 = sb("mx2", [P, 2, H])
        sm = sb("sm", [P, 2, H])
        rinv = sb("rinv", [P, 2, H])
        nb = sb("nb", [P, 2, 2, 2])
        qT2 = arena[:, 4096:5120].rearrange("p (k m n) -> p k m n", k=2, m=4)
        on = arena[:, 5120:5632].rearrange("p (k n) -> p k n", k=2)
        oT = sb("oT", [P, 2, DH, P])
        hid = arena[:, 0:4096].rearrange("p (k f n) -> p k f n", k=2, f=FT)
        ps = ctx.enter_context(nc.psum_tensor("ps", [P, 8, 512], F32))

        in_vec = sem("in_vec")
        in_act = sem("in_act")
        in_kin = sem("in_kin")
        in_w0 = sem("in_w0")
        in_base = sem("in_base")
        in_mlp = sem("in_mlp")
        in_bv = sem("in_bv")
        in_l2 = sem("in_l2")
        in_ring = [sem(f"in_ring{i}") for i in range(RING)]
        stored = sem("stored")
        pool_set = sem("pool_set")
        consts_ready = sem("consts_ready")
        mask_ready = sem("mask_ready")
        ones_ready = sem("ones_ready")
        xb_ready = sem("xb_ready")
        proj_ps = sem("proj_ps")
        proj_act = sem("proj_act")
        proj_dve = sem("proj_dve")
        s0_ps = sem("s0_ps")
        nb_ready = sem("nb_ready")
        p0_ready = sem("p0_ready")
        kq_ps = sem("kq_ps")
        base_ps = sem("base_ps")
        base_copied = sem("base_copied")
        hl_step = sem("hl_step")
        hl_ready = sem("hl_ready")
        copies_ready = sem("copies_ready")
        kq_ready = sem("kq_ready")
        pv0_ps = sem("pv0_ps")
        o0_ready = sem("o0_ready")
        rinv0_ready = sem("rinv0_ready")
        w0_pool = sem("w0_pool")
        t0_ps = sem("t0_ps")
        pt0_ready = sem("pt0_ready")
        kv_ps = sem("kv_ps")
        k_ready = sem("k_ready")
        k_rest = sem("k_rest")
        kb_round = sem("kb_round")
        kb_ready = sem("kb_ready")
        v_ready = sem("v_ready")
        v_rest = sem("v_rest")
        ww_ready = sem("ww_ready")
        ww_rest = sem("ww_rest")
        bv_ready = sem("bv_ready")
        bv_rest = sem("bv_rest")
        a_ps = sem("a_ps")
        a_ready = sem("a_ready")
        a_act = sem("a_act")
        vw_ps = sem("vw_ps")
        vw_act = sem("vw_act")
        vw_dve = sem("vw_dve")
        head_used = sem("head_used")
        vwb_ps = sem("vwb_ps")
        vwb_ready = sem("vwb_ready")
        z_ready = sem("z_ready")
        zT_ps = sem("zT_ps")
        h_ready = sem("h_ready")
        s_ps = sem("s_ps")
        s_used = sem("s_used")
        s_half = sem("s_half")
        sub_half = sem("sub_half")
        e_half = sem("e_half")
        p_half = sem("p_half")
        e_ready = sem("e_ready")
        rinv_ready = sem("rinv_ready")
        p_ready = sem("p_ready")
        pT_ps = sem("pT_ps")
        pT_act = sem("pT_act")
        pT_dve = sem("pT_dve")
        o_ps = sem("o_ps")
        rows_done = sem("rows_done")
        kc_clear = sem("kc_clear")
        q_ps = sem("q_ps")
        q_ready = sem("q_ready")
        pv_ps = sem("pv_ps")
        on_ready = sem("on_ready")
        oT_ps = sem("oT_ps")
        oT_ready = sem("oT_ready")
        var_ready = sem("var_ready")
        rstd_ready = sem("rstd_ready")
        zm_ready = sem("zm_ready")
        zmT_ps = sem("zmT_ps")
        hm_ready = sem("hm_ready")
        f1_ps = sem("f1_ps")
        hid_ready = sem("hid_ready")
        f2_ps = sem("f2_ps")
        dve_step = sem("dve_step")

        def col(name, i=0, n=1):
            at = COLS[name][0] + i
            return cols[:, at:at + n]

        PASSES = ((0, 0), (0, 1), (1, 0))
        HALF = H // 2 * C

        def jobs():
            out = []
            for b in range(B):
                out.append(("vc", 0, b, 0))
                for g in (2 * b, 2 * b + 1):
                    out.append(("v0", 0, g, 0))
            for m in range(4):
                out.append(("kc", 1, m, 0))
            for b in range(B):
                out.append(("vc", 1, b, 0))
            return out

        JOBS = jobs()
        NJ = len(JOBS)
        NJ0 = NJ - 8

        def job_bank(n):
            return 4 + n if n < 3 else 7 if n < NJ0 else (n - NJ0) % 7

        def both_orders(h):
            odd = H + (h ^ 1)
            return slice(h, odd + 1, odd - h)

        def act_jobs(n):
            return (n + 1) // 2

        BASE_BANK = (7, 7, 4, 5)
        OUT0 = 2 * PAIRS + 4

        block = ctx.enter_context(nc.Block())

        MLPS = {"M0": ("L0", 0), "M1": ("L1", 1), "M2": ("L2", 2), "M3": ("L3", 3)}

        @block.sync
        def _(sp):
            sp.dma_start(w0, t["w0"]).then_inc(in_base, 16)
            sp.dma_start(kinT[:, :, 0, :], t["kinT"][:, :, 0, :]).then_inc(in_base, 16)
            sp.dma_start(cols[:, :], t["cols"]).then_inc(in_vec, 16)
            sp.dma_start(copies_f, t["copies"]).then_inc(in_vec, 16)
            sp.dma_start(mask_i[:, :], t["mask_i"]).then_inc(in_vec, 16)
            sp.dma_start(mask_u[:, :], t["mask_u"]).then_inc(in_vec, 16)
            sp.dma_start(bo[:, :, :], t["bo"]).then_inc(in_vec, 16)
            sp.dma_start(vw0, t["vw0"]).then_inc(in_act, 16)
            sp.dma_start(ctxD[:, :, :, :], t["ctxD"]).then_inc(in_act, 16)
            sp.dma_start(kinT[:, :, 1:B, :], t["kinT"][:, :, 1:B, :]).then_inc(in_kin, 16)
            sp.dma_start(ctxT[:, :, :, :], t["ctxT"]).then_inc(in_w0, 16)
            sp.dma_start(ow0, t["ow0"]).then_inc(in_w0, 16)
            sp.dma_start(x[:, :, :], t["x"]).then_inc(in_w0, 16)
            sp.dma_start(brow[:, :, :], t["brow"]).then_inc(in_w0, 16)

            def load_mlp(l):
                if l > 0:
                    sp.wait_ge(rows_done, rows_before(f"M{l - 1}") + B)
                sp.dma_start(w1[:, :, :], t["w1"][l]).then_inc(in_mlp, 16)
                sp.dma_start(w2[:, :, :], t["w2"][l]).then_inc(in_mlp, 16)

            def load_keys(a):
                if a > 0:
                    sp.wait_ge(vwb_ps, 2 * a - 1)
                sp.dma_start(bvz[:, :, :], t["bvz"][a]).then_inc(in_bv, 16)
                for h in range(H):
                    n = a * H + h
                    if n >= RING:
                        sp.wait_ge(head_used, n - RING + 1)
                    sp.dma_start(ring[:, n % RING, :], t["heads"][a, h]).then_inc(in_ring[n % RING], 16)

            load_mlp(0)
            load_keys(0)
            load_mlp(1)
            load_keys(1)
            sp.wait_ge(head_used, 2 * H)
            sp.dma_start(wp2, t["wp2"]).then_inc(in_l2, 16)
            sp.dma_start(vw2, t["vw2"]).then_inc(in_l2, 16)
            load_mlp(2)
            sp.wait_ge(rows_done, rows_before("M2"))
            load_keys(2)
            load_mlp(3)
            load_keys(3)
            for b in range(B):
                sp.wait_ge(rows_done, rows_before("M3") + b + 1)
                sp.dma_start(t["out"][b], x[:, 2 * b:2 * b + 2, :]).then_inc(stored, 16)
            sp.wait_ge(stored, 16 * B)

        @block.gpsimd
        def _(pool):
            g = nc.gpsimd
            g.memset(ident[:, :], 0.0).then_inc(pool_set, 1)
            g.memset(perm[:, :], 0.0).then_inc(pool_set, 1)
            g.memset(ones[:, :], 1.0).then_inc(pool_set, 1)
            g.memset(e16[:, :], 0.0).then_inc(pool_set, 1)
            g.memset(e16q[:, :], 0.0).then_inc(pool_set, 1)
            g.memset(e48[:, :], 0.0).then_inc(pool_set, 1)
            g.memset(VC[:, :, :, :, :], 0.0).then_inc(pool_set, 1)
            g.memset(VC0, 0.0).then_inc(pool_set, 1)
            g.memset(V0, 0.0).then_inc(pool_set, 1)
            g.memset(prob[:, :, PN - 1:PN], 1.0).then_inc(pool_set, 1)
            pool.wait_ge(pool_set, 10)
            g.affine_select(out=ident[:, :], in_=ident[:, :], compare_op=ALU.not_equal, fill=1.0,
                            base=0, pattern=[[-1, P]], channel_multiplier=1).then_inc(pool_set, 1)
            pv = perm[:, 0:H].rearrange("p (a two) -> p a two", two=2)
            g.affine_select(out=pv[:, :, 1], in_=pv[:, :, 1], compare_op=ALU.not_equal, fill=1.0,
                            base=0, pattern=[[-2, PAIRS]], channel_multiplier=1).then_inc(pool_set, 1)
            g.affine_select(out=pv[:, :, 0], in_=pv[:, :, 0], compare_op=ALU.not_equal, fill=1.0,
                            base=-1, pattern=[[-2, PAIRS]], channel_multiplier=1).then_inc(pool_set, 1)
            g.affine_select(out=perm[:, H:VO], in_=perm[:, H:VO], compare_op=ALU.not_equal, fill=1.0,
                            base=-H, pattern=[[-1, 1]], channel_multiplier=1).then_inc(pool_set, 1)
            g.memset(e16[:, HD:VO], 1.0).then_inc(pool_set, 1)
            g.memset(e16q[:, :].rearrange("p (q r) -> p q r", q=4)[:, :, HD:HD + 1], 1.0).then_inc(pool_set, 1)
            g.memset(e48[:, :].rearrange("p (q r) -> p q r", q=2)[:, :, 48:49], 1.0).then_inc(pool_set, 1)
            pool.wait_ge(pool_set, 17)
            g.memset(VC[0:C, :, :, 0, HD:VO], 1.0).then_inc(pool_set, 1)
            pool.wait_ge(pool_set, 18)
            g.memset(VC[C:P, :, :, 1, HD:VO], 1.0).then_inc(pool_set, 1)
            pool.wait_ge(pool_set, 19)
            g.memset(neg_half[:, :], -0.5).then_inc(consts_ready, 1)
            pool.wait_ge(consts_ready, 1)

            def add_row(dst, n, name):
                g.tensor_tensor(dst[:, n, :], x[:, n, :], brow[:, ROWS.index(name), :], ALU.add).then_inc(xb_ready, 1)

            pool.wait_ge(in_vec, 80)

            def keys(a, heads):
                for h in heads:
                    n = a * H + h
                    if n >= 2:
                        pool.wait_ge(a_ps, n - 1)
                    else:
                        pool.wait_ge(in_vec, 80)
                    l, i = ATTN[a]
                    one = slice(B * C, KW)
                    bias_key = col(f"{l}_bias_k{i}", h).broadcast_to([P, 2])
                    g.tensor_copy(KT[:, n % 2, 0, one], bias_key).then_inc(kb_round, 1)
                    pool.wait_ge(kb_round, n + 1)
                    g.tensor_tensor(KT[:, n % 2, 1, one], bias_key, KT[:, n % 2, 0, one].bitcast(F32), ALU.subtract)\
                        .then_inc(kb_ready, 1)
                    if h == 0:
                        pool.wait_ge(bv_ready, a + 1)
                        g.tensor_tensor(bqs[:, 1, :], col(f"{l}_bq{i}", 0, 2 * H), bqs[:, 0, :].bitcast(F32), ALU.subtract)
                        g.tensor_tensor(bvs[:, 1, :], bvz[:, :, :].rearrange("p h c -> p (h c)"),
                                        bvs[:, 0, :].bitcast(F32), ALU.subtract).then_inc(bv_rest, 1)
                    pool.wait_ge(ww_ready, n + 1)
                    g.tensor_tensor(ww[:, n % 2, 1, :], ring[:, n % RING, 512:1024], ww[:, n % 2, 0, :].bitcast(F32),
                                    ALU.subtract).then_inc(ww_rest, 1)

            pool.wait_ge(in_w0, 16 * 4)
            for n in range(TILES * PAIRS):
                pool.wait_ge(rinv0_ready, n + 1)
                w = prob0[:, n % 3, :].rearrange("p (e c) -> p e c", e=2)
                g.tensor_tensor(w, w, rinv[:, n % 2, 0:2].unsqueeze(2).broadcast_to([P, 2, KEYS0]), ALU.mult)\
                    .then_inc(w0_pool, 1)
                if n < TILES:
                    add_row(x0, n, "L0_out_b")

            def power(phase, i, width):
                n, k = norms_before(phase) + i, i % 2
                pool.wait_ge(var_ready, n + 1)
                g.tensor_tensor(rstd[:, k, 0:width], var[:, k, 0:width], neg_half[:, 0:width], ALU.pow)\
                    .then_inc(rstd_ready, 1)

            def first_norms(a):
                power(f"T{a}", 0, 1)
                power(f"T{a}", 1, 1)

            def tokens(a):
                for n in range(TILES):
                    k = n % 2
                    if n + 2 < TILES:
                        power(f"T{a}", n + 2, 1)
                    pool.wait_ge(rinv_ready, 8 * a + n + 1)
                    pm = prob[:, k, 0:H // 2 * C].rearrange("p (h c) -> p h c", c=C)
                    g.tensor_tensor(pm, pm, rinv[:, k, 0:H // 2].unsqueeze(2).broadcast_to([P, H // 2, C]), ALU.mult)
                    pb = prob[:, k, H * C:H * C + H]
                    g.tensor_tensor(pb, pb, rinv[:, k, :], ALU.mult).then_inc(p_ready, 1)

            def mlp_rows(l, name):
                power(f"M{l}", 0, 2)
                power(f"M{l}", 1, 2)
                for b in range(B):
                    if 1 <= b < B - 1:
                        power(f"M{l}", b + 1, 2)
                    for n in (2 * b, 2 * b + 1):
                        if l > 0:
                            pool.wait_ge(zm_ready, l * B + b + 1)
                        add_row(x, n, name)
                    if l == 1 and b == 0:
                        pool.wait_ge(rows_done, rows_before("M1"))
                        g.memset(arena[:, 5632:9728], 0.0).then_inc(kc_clear, 1)

            pool.wait_ge(xb_ready, TILES)
            mlp_rows(0, "L0_mlp_b2")
            keys(0, range(2))
            first_norms(0)
            keys(0, range(2, H))
            tokens(0)
            keys(1, range(2))
            first_norms(1)
            keys(1, range(2, H))
            tokens(1)
            mlp_rows(1, "L1_b_fc2")
            power("L2", 0, 1)
            power("L2", 1, 1)
            for n in range(TILES):
                if n + 2 < TILES:
                    power("L2", n + 2, 1)
                pool.wait_ge(z_ready, 2 * TILES + n + 1)
                add_row(x, n, "L2_cproj_b")
            mlp_rows(2, "L2_proj_b")
            keys(2, range(2))
            first_norms(2)
            keys(2, range(2, H))
            tokens(2)
            keys(3, range(2))
            first_norms(3)
            keys(3, range(2, H))
            tokens(3)
            mlp_rows(3, "L3_b_fc2")

        @block.tensor
        def _(pe):
            mm = nc.tensor.matmul

            def project(lo, hi):
                for n in range(lo, hi):
                    kind, l, i, j = JOBS[n]
                    if n >= NJ0 + 7:
                        pe.wait_ge(proj_act if (n - 7) % 2 == 0 else proj_dve, (n - 7) // 2 + 1)
                    o = ps[:, job_bank(n), :]
                    if kind == "kc":
                        for d in range(DH):
                            mm(o[:, 0:B * C], wp2[:, d, 512 + i * P:512 + (i + 1) * P], ctxT[:, 0, d, :],
                               start=(d == 0), stop=False)
                        mm(o[:, 0:B * C], e16q[:, :], mask[0:1, l, :], start=False, stop=True).then_inc(proj_ps, 1)
                    elif kind == "vc":
                        w = vw0 if l == 0 else vw2[:, 0, :, :]
                        for d in range(DH):
                            m = mm(o[:, 0:D], ctxD[:, d, i, :], w[:, d, :], start=(d == 0), stop=(d == 1))
                        m.then_inc(proj_ps, 1)
                    else:
                        rows = kinT[:, :, i // 2, C + (i % 2) * P:C + (i % 2 + 1) * P]
                        for d in range(DH):
                            m = mm(o[:, 0:D], rows[:, d, :], vw0[:, d, :], start=(d == 0), stop=(d == 1))
                        m.then_inc(proj_ps, 1)

            def attend0():
                N = TILES * PAIRS

                def pair_of(n):
                    return n // 2, n // 2 // PAIRS, (n // 2) % PAIRS, n % 2

                def base(t):
                    bank = BASE_BANK[t] if t < 4 else 7
                    b, m, w = t // 4, t // 2 % 2, t % 2
                    width = S if w else KEYS0
                    for d in range(DH):
                        last = mm(ps[:, bank, 0:width], w0[:, w, d, m * P:(m + 1) * P], kinT[:, d, b, KEYS0 - width:KEYS0],
                                  start=(d == 0), stop=(d == 1))
                    last.then_inc(base_ps, 1)

                def spread(n):
                    pair, w = n // 2, n % 2
                    b, r = pair // PAIRS, pair % PAIRS
                    m, at = r // 4, slice(32 * (r % 4), 32 * (r % 4) + 32)
                    cols_of = slice(KEYS0, KEYS0 + S) if w else slice(0, KEYS0)
                    width = S if w else KEYS0
                    pe.wait_ge(hl_ready, 4 * b + 2 * m + w + 1)
                    for c in range(2):
                        last = mm(ps[:, 7, 0:width], copies[at, w, c, :], HL[at, m, c, cols_of],
                                  start=(c == 0), stop=(c == 1 and w == 1))
                    if w == 0:
                        one = slice(at.start, at.start + 1)
                        last = mm(ps[:, 7, 0:C], e48[one, :], mask[one, 0, b * C:(b + 1) * C], start=False, stop=True)
                    last.then_inc(kq_ps, 1)

                def scores(n):
                    pair, b, r, u = pair_of(n)
                    pe.wait_ge(kq_ready, 2 * pair + 2)
                    if n >= 2:
                        pe.wait_ge(p0_ready, n - 1)
                    for e in range(2):
                        j = 2 * u + e
                        q = KQ[C * e:C * e + C, pair % 3, 1, u * P:(u + 1) * P]
                        kc = KQ[C * e:C * e + C, pair % 3, 0, 0:C]
                        lat = KQ[C * e:C * e + C, pair % 3, 0, C:KEYS0]
                        if e == 0:
                            mm(ps[:, j, 0:S], q, lat, start=True, stop=True)
                            mm(ps[:, j, S:KEYS0], q, kc, start=True, stop=True)
                        else:
                            last = mm(ps[:, j, 0:KEYS0], q, KQ[C * e:C * e + C, pair % 3, 0, :], start=True, stop=True)
                    last.then_inc(s0_ps, 1)

                def turn(n):
                    pe.wait_ge(w0_pool, n + 1)
                    if n == 0:
                        pe.wait_ge(base_copied, 4)
                    if n >= 1:
                        pe.wait_ge(pt0_ready, n)
                    for c in range(5):
                        last = nc.tensor.transpose(ps[:, 4 + c // 4, (c % 4) * P:(c % 4 + 1) * P],
                                                   prob0[:, n % 3, c * P:(c + 1) * P], ident[:, :])
                    last.then_inc(t0_ps, 1)

                def values(n):
                    pair, b, r, u = pair_of(n)
                    k = n % 2
                    pe.wait_ge(pt0_ready, n + 1)
                    if n % (2 * PAIRS) == 0:
                        pe.wait_ge(proj_act, act_jobs(3 * (b + 1)))
                        pe.wait_ge(proj_dve, 3 * (b + 1) // 2)
                    if pair >= 4:
                        pe.wait_ge(o0_ready, pair - 3)
                    at = slice(32 * (r % 4), 32 * (r % 4) + 32)
                    o = ps[at, 6, u * P:(u + 1) * P]
                    mm(o, VC0[:, b, r, :], pT[:, k, 2, :], start=True, stop=False)
                    for e in range(2):
                        for v in range(2):
                            last = mm(o, V0[:, 2 * b + v, r, 32 * e:32 * e + 32], pT[:, k, 3 * e + v, :],
                                      start=False, stop=(e == 1 and v == 1))
                    last.then_inc(pv0_ps, 1)

                def output(g):
                    if g == 0:
                        pe.wait_ge(in_w0, 16 * 4)
                    pe.wait_ge(o0_ready, PAIRS * (g // 2 + 1))
                    for d in range(DH):
                        last = mm(ps[:, 7, 256:512], oT0[:, g // 2 % 2, g % 2, d, :], ow0[:, d, :],
                                  start=(d == 0), stop=(d == 1))
                    last.then_inc(o_ps, 1)

                def bank7_read(i):
                    step, b = i % (2 * PAIRS), (i - OUT0) // (2 * PAIRS)
                    if i >= OUT0 and step in (4, 5):
                        pe.wait_ge(rows_done, 2 * b + step - 4 + 1)
                    elif 8 <= step < 12 and i // (2 * PAIRS) + 1 < B:
                        pe.wait_ge(base_copied, 4 * (i // (2 * PAIRS) + 1) + step - 8 + 1)
                    elif 12 <= step < 15 and i // (2 * PAIRS) + 1 < B:
                        n = 3 * (i // (2 * PAIRS) + 1) + step - 12
                        pe.wait_ge(proj_act if n % 2 == 0 else proj_dve, n // 2 + 1)
                    else:
                        pe.wait_ge(kq_ready, i + 5)

                base(0)
                pe.wait_ge(in_act, 16 * 2)
                project(0, 1)
                pe.wait_ge(base_copied, 1)
                base(1)
                project(1, 2)
                pe.wait_ge(base_copied, 2)
                pe.wait_ge(consts_ready, 1)
                pe.wait_ge(mask_ready, 1)
                pe.wait_ge(copies_ready, 1)
                spread(0)
                project(2, 3)
                for n in range(1, 4):
                    pe.wait_ge(kq_ready, n)
                    spread(n)
                for i in range(N + 3):
                    if i < N:
                        scores(i)
                    if i + 4 < N:
                        if i == 0:
                            pe.wait_ge(kq_ready, 4)
                        else:
                            bank7_read(i - 1)
                        spread(i + 4)
                    if 2 <= i < N + 2:
                        turn(i - 2)
                    if i >= 3:
                        values(i - 3)
                    step, b = i % (2 * PAIRS), (i - OUT0) // (2 * PAIRS)
                    if i >= OUT0 and step in (4, 5):
                        pe.wait_ge(kq_ready, i + 5)
                        output(2 * b + step - 4)
                    if 8 <= step < 12 and i // (2 * PAIRS) + 1 < B:
                        if i == 8:
                            pe.wait_ge(in_kin, 16)
                        pe.wait_ge(kq_ready, i + 5)
                        base(4 * (i // (2 * PAIRS) + 1) + step - 8)
                    if 12 <= step < 15 and i // (2 * PAIRS) + 1 < B:
                        pe.wait_ge(kq_ready, i + 5)
                        n = 3 * (i // (2 * PAIRS) + 1) + step - 12
                        project(n, n + 1)
                    if i < 2:
                        pe.wait_ge(proj_act if i == 0 else proj_dve, 1)
                        base(i + 2)
                for g in (TILES - 2, TILES - 1):
                    pe.wait_ge(rows_done, g)
                    output(g)

            def heads_kv(a, h):
                n = a * H + h
                k, w = n % 2, ring[:, n % RING, :]
                pe.wait_ge(in_ring[n % RING], 16 * (n // RING + 1))
                if h >= 2:
                    pe.wait_ge(k_ready, n - 1)
                    pe.wait_ge(v_ready, n - 1)
                    pe.wait_ge(k_rest, n - 1)
                    pe.wait_ge(v_rest, n - 1)
                for d in range(DH):
                    mm(ps[:, k, 0:B * C], w[:, d * P:(d + 1) * P], ctxT[:, 0, d, :], start=(d == 0), stop=(d == 1))
                for d in range(DH):
                    last = mm(ps[:, k, 256:512], w[:, 256 + d * P:256 + (d + 1) * P], ctxT[:, h % 2, d, :],
                              start=(d == 0), stop=(d == 1))
                last.then_inc(kv_ps, 1)

            def turn_z(tile, n, bank=7):
                k = tile % 2
                pe.wait_ge(z_ready, n + 1)
                if n >= 1:
                    pe.wait_ge(h_ready, n)
                for d in range(DH):
                    last = nc.tensor.transpose(ps[:, bank, d * P:(d + 1) * P], z[:, k, 0, d * P:(d + 1) * P], ident[:, :])
                last.then_inc(zT_ps, 1)

            def keys(a, seq):
                l, i = ATTN[a]

                def products(h):
                    n = a * H + h
                    k, w = n % 2, ring[:, n % RING, :]
                    pe.wait_ge(k_rest, n + 1)
                    pe.wait_ge(kb_ready, n + 1)
                    pe.wait_ge(ww_rest, n + 1)
                    if h == 0:
                        pe.wait_ge(bv_rest, a + 1)
                    if n >= 1:
                        pe.wait_ge(a_ready, n)
                        pe.wait_ge(a_act, n)
                    for d in range(DH):
                        for p, (c, e) in enumerate(PASSES):
                            mm(ps[:, 2 + d, 0:KW], ww[:, k, c, d * P:(d + 1) * P], KT[:, k, e, :],
                               start=(p == 0), stop=(p == 2))
                    for p, (c, e) in enumerate(PASSES):
                        last = mm(ps[0:2, 4, 0:KW], bqs[:, c, 2 * h:2 * h + 2], KT[:, k, e, :],
                                  start=(p == 0), stop=(p == 2))
                    last.then_inc(a_ps, 1)
                    pe.wait_ge(v_rest, n + 1)
                    if h == 0:
                        pe.wait_ge(rows_done, rows_before(f"T{a}"))
                    if n >= 2:
                        pe.wait_ge(vw_act, n - 1)
                        pe.wait_ge(vw_dve, n - 1)
                    for g in range(2):
                        for p, (c, e) in enumerate(PASSES):
                            last = mm(ps[:, 5 + k, g * D:(g + 1) * D], VT[:, k, c, g * P:(g + 1) * P], ww[:, k, e, D:2 * D],
                                      start=(p == 0), stop=(p == 2))
                    last.then_inc(vw_ps, 1)
                    for p, (c, e) in enumerate(PASSES):
                        last = mm(ps[0:VO, 7, 0:D], bvs[:, c, h * VO:(h + 1) * VO], ww[:, k, e, D:2 * D],
                                  start=(h == 0 and p == 0), stop=False)
                    last.then_inc(head_used, 1)

                for h in range(H):
                    if h >= 1 and h + 1 < H:
                        heads_kv(a, h + 1)
                    if h == 1:
                        pe.wait_ge(h_ready, seq * TILES + 1)
                    products(h)
                    if h == 0:
                        turn_z(0, seq * TILES, bank=6)
                mm(ps[0:VO, 7, 0:D], e16[:, :], bo[:, a, :], start=False, stop=True).then_inc(vwb_ps, 1)

            def tokens(a, seq):
                base = seq * TILES
                pe.wait_ge(a_ready, H * (a + 1))
                pe.wait_ge(a_act, H * (a + 1))
                pe.wait_ge(ones_ready, 1)

                def odd_bias_rows():
                    pe.wait_ge(vwb_ready, 2 * a + 1)
                    pe.wait_ge(vw_act, H * (a + 1))
                    pe.wait_ge(vw_dve, H * (a + 1))
                    mm(ps[0:VO, 6, 0:D], perm[:, :], VWb[:, 0, :], start=True, stop=True).then_inc(vwb_ps, 1)

                def scores(g):
                    n, k, b = base + g, g % 2, g // 2
                    pe.wait_ge(h_ready, n + 1)
                    if g >= 1:
                        pe.wait_ge(s_used, n)
                    for half in range(2):
                        if half == 1 and g >= 1:
                            turn_p(g - 1)
                        o = ps[:, half, :]
                        cols_of = slice(4 * half, 4 * half + 4)
                        sl = slice(2 * (b % 2), 2 * (b % 2) + 2)
                        for d in range(DH):
                            mm(o, hT[:, k, d, 0:P],
                               A[:, d, b // 2, cols_of, sl, :].rearrange("p r s k -> p r (s k)"),
                               start=(d == 0), stop=False)
                        last = mm(o, ones_r[:, :], cb[:, b // 2, cols_of, sl, :].rearrange("p r s k -> p r (s k)"),
                                  start=False, stop=True)
                        if half == 0:
                            last.then_inc(s_half, 1)
                    for d in range(DH):
                        mm(ps[:, 2, 0:H], hT[:, k, d, 0:P], Ab[:, d, b % 2 * H:(b % 2 + 1) * H], start=(d == 0), stop=False)
                    mm(ps[:, 2, 0:H], ones_r[:, :], cbb[:, b % 2 * H:(b % 2 + 1) * H], start=False, stop=True).then_inc(s_ps, 1)

                def turn_p(g):
                    n, k = base + g, g % 2
                    pe.wait_ge(p_ready, 8 * a + g + 1)
                    pe.wait_ge(p_half, 8 * a + g + 1)
                    if n >= 1:
                        pe.wait_ge(pT_act, n)
                    if 8 * a + g >= 1:
                        pe.wait_ge(pT_dve, 8 * a + g)
                    for c in range(PAIRS):
                        nc.tensor.transpose(ps[:, 3 + c // 4, (c % 4) * P:(c % 4 + 1) * P],
                                            prob[:, k, c * P:(c + 1) * P], ident[:, :])
                    nc.tensor.transpose(ps[0:VO, 5, 0:P], prob[:, k, H * C:PN], ident[:, :]).then_inc(pT_ps, 1)

                def output(g):
                    n, k, b = base + g, g % 2, g // 2
                    pe.wait_ge(pT_act, n + 1)
                    pe.wait_ge(pT_dve, 8 * a + g + 1)
                    if g == 0:
                        pe.wait_ge(vwb_ready, 2 * a + 2)
                    if g >= 1:
                        pe.wait_ge(rows_done, rows_before(f"T{a}") + g)
                    for c in range(PAIRS):
                        mm(ps[:, 6, 0:D], pT[:, k, c, :], VW[:, b, c, :], start=(c == 0), stop=False)
                    mm(ps[:, 6, 0:D], pT[0:VO, k, 8, :], VWb[:, b % 2, :], start=False, stop=True).then_inc(o_ps, 1)

                for i in range(TILES + 1):
                    if i < TILES:
                        scores(i)
                        if i == 0:
                            odd_bias_rows()
                    else:
                        if a % 2 == 0:
                            pe.wait_ge(s_used, base + TILES)
                            heads_kv(a + 1, 0)
                            heads_kv(a + 1, 1)
                        turn_p(i - 1)
                    if i + 1 < TILES:
                        turn_z(i + 1, base + i + 1)
                    if i >= 1:
                        output(i - 1)

            def attend2(seq):
                base = seq * TILES
                pe.wait_ge(rows_done, rows_before("L2"))
                pe.wait_ge(in_l2, 32)
                project(NJ0, NJ)
                pe.wait_ge(proj_act, act_jobs(NJ))
                pe.wait_ge(proj_dve, NJ // 2)

                def queries(g):
                    pe.wait_ge(h_ready, base + g + 1)
                    if g >= 1:
                        pe.wait_ge(q_ready, g)
                    for m in range(4):
                        for d in range(DH):
                            last = mm(ps[:, 4, m * P:(m + 1) * P], wp2[:, d, m * P:(m + 1) * P], hT[:, g % 2, d, 0:P],
                                      start=(d == 0), stop=(d == 1))
                    last.then_inc(q_ps, 1)

                def scores(g):
                    k, b = g % 2, g // 2
                    pe.wait_ge(q_ready, g + 1)
                    for m in range(4):
                        last = mm(ps[:, m, 0:4 * C], qT2[:, k, m, :], KC[:, m, b, :], start=True, stop=True)
                    last.then_inc(s_ps, 1)

                def turn_p(g):
                    n, k = base + g, g % 2
                    pe.wait_ge(e_ready, n + 1)
                    pe.wait_ge(pT_act, n)
                    for c in range(PAIRS):
                        last = nc.tensor.transpose(ps[:, 5 + c // 4, (c % 4) * P:(c % 4 + 1) * P],
                                                   prob[:, k, c * P:(c + 1) * P], ident[:, :])
                    last.then_inc(pT_ps, 1)

                def values(g):
                    n, k, b = base + g, g % 2, g // 2
                    pe.wait_ge(pT_act, n + 1)
                    for r in range(PAIRS):
                        at = 256 + r % 4 * 2 * VO
                        last = mm(ps[:, r // 4, at:at + 2 * VO], pT[:, k, r, :],
                                  VC[:, b, r, :, :].rearrange("p e c -> p (e c)"), start=True, stop=True)
                    last.then_inc(pv_ps, 1)

                def output(g):
                    pe.wait_ge(oT_ready, g + 1)
                    for d in range(DH):
                        last = mm(ps[:, 3, 256:512], oT[:, g % 2, d, :], vw2[:, 1, d, :], start=(d == 0), stop=(d == 1))
                    last.then_inc(o_ps, 1)

                def turns(gz, go):
                    if 1 <= gz <= TILES:
                        pe.wait_ge(h_ready, base + gz)
                    if 1 <= go <= TILES:
                        pe.wait_ge(oT_ready, go)
                    if 0 <= go < TILES:
                        pe.wait_ge(on_ready, go + 1)
                        for d in range(DH):
                            last = nc.tensor.transpose(ps[:, 7, 256 + d * P:256 + (d + 1) * P],
                                                       on[:, go % 2, d * P:(d + 1) * P], ident[:, :])
                        last.then_inc(oT_ps, 1)
                    if gz < TILES:
                        pe.wait_ge(z_ready, base + gz + 1)
                        for d in range(DH):
                            last = nc.tensor.transpose(ps[:, 7, d * P:(d + 1) * P],
                                                       z[:, gz % 2, 0, d * P:(d + 1) * P], ident[:, :])
                        last.then_inc(zT_ps, 1)

                turns(0, -1)
                turns(1, -1)
                queries(0)
                for i in range(TILES + 3):
                    if 1 <= i <= TILES:
                        pe.wait_ge(s_used, base + i)
                    if i >= 3:
                        pe.wait_ge(on_ready, i - 2)
                    if i >= 4:
                        pe.wait_ge(rows_done, rows_before("L2") + i - 3)
                    if 2 <= i < TILES + 2:
                        values(i - 2)
                    if i >= 3:
                        output(i - 3)
                    if i < TILES:
                        scores(i)
                    if 1 <= i <= TILES:
                        turn_p(i - 1)
                    if i + 1 < TILES:
                        queries(i + 1)
                    if i < TILES + 2:
                        turns(i + 2, i - 2)

            def mlp(l):
                base = l * B
                pe.wait_ge(in_mlp, 32 * (l + 1))

                def turn(b):
                    k = b % 2
                    pe.wait_ge(zm_ready, base + b + 1)
                    if b >= 1:
                        pe.wait_ge(hm_ready, base + b)
                    for d in range(DH):
                        for u in range(2):
                            last = nc.tensor.transpose(ps[:, 4, d * 256 + u * P:d * 256 + (u + 1) * P],
                                                       z[:, k, u, d * P:(d + 1) * P], ident[:, :])
                    last.then_inc(zmT_ps, 1)

                def up(b):
                    k = b % 2
                    pe.wait_ge(hm_ready, base + b + 1)
                    for f in range(FT):
                        if b >= 1 and f % 2 == 0:
                            pe.wait_ge(hid_ready, (base + b - 1) * FT + f + 2)
                        for d in range(DH):
                            last = mm(ps[:, f // 2, (f % 2) * 256:(f % 2 + 1) * 256], w1[:, d, f * P:(f + 1) * P],
                                      hT[:, k, d, :], start=(d == 0), stop=(d == 1))
                        last.then_inc(f1_ps, 1)
                        if f == FT // 2 - 1 and b + 1 < B:
                            turn(b + 1)

                def down(b):
                    k = b % 2
                    pe.wait_ge(hid_ready, (base + b + 1) * FT)
                    if b >= 1:
                        pe.wait_ge(rows_done, rows_before(f"M{l}") + b)
                    for u in range(2):
                        for f in range(FT):
                            last = mm(ps[:, 5 + u, 0:D], hid[:, k, f, u * P:(u + 1) * P], w2[:, f, :],
                                      start=(f == 0), stop=(f == FT - 1))
                    last.then_inc(f2_ps, 1)

                turn(0)
                pe.wait_ge(rows_done, rows_before(f"M{l}"))
                for i in range(B + 1):
                    if i < B:
                        up(i)
                    elif l % 2 == 0:
                        pe.wait_ge(hid_ready, (base + B - 1) * FT + 4)
                        heads_kv(l, 0)
                        heads_kv(l, 1)
                    if i >= 1:
                        down(i - 1)

            pe.wait_ge(in_base, 32)
            attend0()
            mlp(0)
            keys(0, 0)
            tokens(0, 0)
            keys(1, 1)
            tokens(1, 1)
            mlp(1)
            attend2(2)
            mlp(2)
            keys(2, 3)
            tokens(2, 3)
            keys(3, 4)
            tokens(3, 4)
            mlp(3)

        def job_out(eng, copy, n):
            kind, l, i, j = JOBS[n]
            o = ps[:, job_bank(n), :]
            if kind == "kc":
                c = COLS["L2_k_b"][0] + i
                for j in range(4):
                    at = slice(32 * j, 32 * j + 32)
                    last = copy(KC[at, i, :, j * C:(j + 1) * C], o[at, 0:B * C].rearrange("p (b n) -> p b n", b=B),
                                cols[at, c:c + 1])
                return last
            if kind == "v0":
                ov = o[:, 0:D].rearrange("p (r e c) -> p r e c", r=PAIRS, e=2)
                copy(V0[:, i, :, 0:HD], ov[:, :, 0, :], None)
                return copy(V0[:, i, :, 3 * HD:4 * HD], ov[:, :, 1, :], None)
            ov = o[:, 0:D].rearrange("p (r e c) -> p r e c", r=PAIRS, e=2)
            if l == 0:
                copy(VC0[0:C, i, :, 0:HD], ov[0:C, :, 0, :], None)
                return copy(VC0[C:P, i, :, HD:2 * HD], ov[C:P, :, 1, :], None)
            copy(VC[0:C, i, :, 0, 0:HD], ov[0:C, :, 0, :], None)
            return copy(VC[C:P, i, :, 1, 0:HD], ov[C:P, :, 1, :], None)

        @block.scalar
        def _(act):
            a_ = nc.scalar.activation

            def copy(out, in_, bias):
                if bias is None:
                    return a_(out, in_, ACT.Copy)
                return a_(out, in_, ACT.Identity, bias=bias)

            act.wait_ge(in_vec, 80)

            def base0(t):
                m, w = t // 2 % 2, t % 2
                width = S if w else KEYS0
                act.wait_ge(base_ps, t + 1)
                if t >= 2:
                    act.wait_ge(hl_ready, t - 1)
                bank = BASE_BANK[t] if t < 4 else 7
                a_(kq_full[:, t % 2, 0:width], ps[:, bank, 0:width], ACT.Identity,
                   bias=col("L0_q_b" if w else "L0_k_b", m)).then_inc(base_copied, 1)

            def spread0(n):
                pair, w = n // 2, n % 2
                width = S if w else KEYS0
                act.wait_ge(kq_ps, n + 1)
                if pair >= 3:
                    act.wait_ge(s0_ps, 2 * (pair - 3) + 2)
                a_(KQ[:, pair % 3, w, 0:width], ps[:, 7, 0:width], ACT.Identity,
                   bias=col("row48") if w else col("zero")).then_inc(kq_ready, 1)

            def exp0(n):
                act.wait_ge(nb_ready, n + 1)
                if n >= 2:
                    act.wait_ge(rinv0_ready, n - 1)
                if n >= 3:
                    act.wait_ge(t0_ps, n - 2)
                for e in range(2):
                    j = 2 * (n % 2) + e
                    last = a_(prob0[:, n % 3, e * KEYS0:(e + 1) * KEYS0], ps[:, j, 0:KEYS0], ACT.Exp,
                              bias=nb[:, n % 2, 1, e:e + 1], scale=1.0 / HD, accum_out=sm[:, n % 2, e:e + 1])
                last.then_inc(p0_ready, 1)

            def values0(pair):
                b, rr, m = pair // PAIRS, pair % 4, pair // 4 % 2
                at = slice(32 * rr, 32 * rr + 32)
                act.wait_ge(pv0_ps, 2 * pair + 2)
                if b >= 2:
                    act.wait_ge(o_ps, 2 * (b - 1))
                c = COLS["L0_v_b"][0] + m
                a_(oT0[at, b % 2, :, m, :], ps[at, 6, 0:2 * P].rearrange("p (u n) -> p u n", u=2), ACT.Identity,
                   bias=cols[at, c:c + 1]).then_inc(o0_ready, 1)

            def turned_o(n, bias, at):
                k = n % 2
                act.wait_ge(oT_ps, n + 1)
                for d in range(DH):
                    last = a_(oT[:, k, d, :], ps[:, 7, at + d * P:at + (d + 1) * P], ACT.Identity, bias=col(bias, d))
                last.then_inc(oT_ready, 1)

            N = TILES * PAIRS
            def job0(n):
                act.wait_ge(proj_ps, n + 1)
                job_out(act, copy, n).then_inc(proj_act, 1)

            base0(0)
            act.wait_ge(consts_ready, 1)
            job0(0)
            base0(1)
            spread0(0)
            job0(2)
            for n in range(1, 4):
                spread0(n)
            for i in range(N + 3):
                if i + 4 < N:
                    spread0(i + 4)
                if i < N:
                    exp0(i)
                if i >= 4 and i % 2 == 0:
                    values0((i - 4) // 2)
                step, b = i % (2 * PAIRS), i // (2 * PAIRS) + 1
                if 8 <= step < 12 and b < B:
                    base0(4 * b + step - 8)
                if 12 <= step < 15 and b < B and (3 * b + step - 12) % 2 == 0:
                    job0(3 * b + step - 12)
                if i < 2:
                    base0(i + 2)

            def scaled(n, scale, offset, bank=7):
                k = n % 2
                act.wait_ge(zT_ps, n + 1)
                for d in range(DH):
                    last = a_(hT[:, k, d, 0:P], ps[:, bank, d * P:(d + 1) * P], ACT.Identity,
                              scale=col(scale, d), bias=col(offset, d))
                last.then_inc(h_ready, 1)

            def mlp(l, scale, offset, bias, gelu):
                base = l * B

                def turned(b):
                    k = b % 2
                    act.wait_ge(zmT_ps, base + b + 1)
                    for d in range(DH):
                        last = a_(hT[:, k, d, :], ps[:, 4, d * 256:(d + 1) * 256], ACT.Identity,
                                  scale=col(scale, d), bias=col(offset, d))
                    last.then_inc(hm_ready, 1)

                turned(0)
                for b in range(B):
                    if b >= 2:
                        act.wait_ge(f2_ps, base + b - 1)
                    for f in range(FT):
                        if f % 2 == 0:
                            act.wait_ge(f1_ps, (base + b) * FT + f + 2)
                        a_(hid[:, b % 2, f, :], ps[:, f // 2, (f % 2) * 256:(f % 2 + 1) * 256], gelu,
                           bias=col(bias, f)).then_inc(hid_ready, 1)
                        if f == FT // 2 - 1 and b + 1 < B:
                            turned(b + 1)

            def keys(a, seq):
                l, i = ATTN[a]
                act.wait_ge(in_bv, 16 * (a + 1))
                if a > 0:
                    act.wait_ge(head_used, a * H)
                a_(bqs[:, 0, :], col(f"{l}_bq{i}", 0, 2 * H), ACT.Copy)
                a_(bvs[:, 0, :], bvz[:, :, :].rearrange("p h c -> p (h c)"), ACT.Copy).then_inc(bv_ready, 1)
                for step in range(H + 1):
                    n = a * H + step
                    k = n % 2
                    if step < H:
                        act.wait_ge(kv_ps, n + 1)
                        if n >= 2:
                            act.wait_ge(a_ps, n - 1)
                        a_(KT[:, k, 0, 0:B * C], ps[:, k, 0:B * C], ACT.Identity, bias=col(f"{l}_bk{i}", step))\
                            .then_inc(k_ready, 1)
                        if n >= 2:
                            act.wait_ge(vw_ps, n - 1)
                        a_(VT[:, k, 0, :], ps[:, k, 256:512], ACT.Identity, bias=col(f"{l}_bv{i}", step))\
                            .then_inc(v_ready, 1)
                        if n >= 2:
                            act.wait_ge(head_used, n - 1)
                        a_(ww[:, k, 0, :], ring[:, n % RING, 512:1024], ACT.Copy).then_inc(ww_ready, 1)
                    if step >= 1:
                        n, h = n - 1, step - 1
                        act.wait_ge(a_ps, n + 1)
                        slots = slice(0, 4, 3) if h % 2 == 0 else slice(1, 3)
                        a_(A[:, 1, :, h // 2, slots, :],
                           ps[:, 3, 0:B * C].rearrange("p (g s k) -> p g s k", g=2, s=2), ACT.Copy)
                        a_(Ab[:, 1, both_orders(h)], ps[:, 3, B * C:KW], ACT.Copy).then_inc(a_act, 1)
                        act.wait_ge(vw_ps, n + 1)
                        a_(VW[C:P, 1 - h % 2:B:2, h // 2, :], ps[C:P, 5 + n % 2, :].rearrange("p (g n) -> p g n", g=2),
                           ACT.Copy).then_inc(vw_act, 1)
                    if step == 1:
                        scaled(seq * TILES, f"{l}_ln{i}_scale", f"{l}_ln{i}_offset", bank=6)

            def tokens(a, seq):
                base = seq * TILES
                l, i = ATTN[a]
                for g in range(TILES + 1):
                    if g >= 1:
                        n, k = base + g - 1, (g - 1) % 2
                        act.wait_ge(pT_ps, n + 1)
                        a_(pT[:, k, 0:4, :], ps[:, 3, :].rearrange("p (c n) -> p c n", c=4), ACT.Copy).then_inc(pT_act, 1)
                    if g + 1 < TILES:
                        scaled(base + g + 1, f"{l}_ln{i}_scale", f"{l}_ln{i}_offset")
                    if g < TILES:
                        n, k = base + g, g % 2
                        act.wait_ge(sub_half, 8 * a + g + 1)
                        a_(prob[:, k, 0:HALF], prob[:, k, 0:HALF], ACT.Exp, scale=float(HK) ** -0.5).then_inc(e_half, 1)
                        act.wait_ge(s_used, n + 1)
                        a_(prob[:, k, HALF:H * C + H], prob[:, k, HALF:H * C + H], ACT.Exp, scale=float(HK) ** -0.5)\
                            .then_inc(e_ready, 1)

            def attend2(seq):
                base = seq * TILES
                act.wait_ge(kc_clear, 1)
                for n in range(NJ0, NJ, 2):
                    act.wait_ge(proj_ps, n + 1)
                    job_out(act, copy, n).then_inc(proj_act, 1)
                scaled(base, "L2_ln1_w", "L2_ln1_b")
                scaled(base + 1, "L2_ln1_w", "L2_ln1_b")
                for i in range(TILES + 2):
                    if 1 <= i <= TILES:
                        n, k = base + i - 1, (i - 1) % 2
                        act.wait_ge(pT_ps, n + 1)
                        for half in range(2):
                            last = a_(pT[:, k, 4 * half:4 * half + 4, :],
                                      ps[:, 5 + half, :].rearrange("p (c n) -> p c n", c=4), ACT.Copy)
                        last.then_inc(pT_act, 1)
                    if i < TILES:
                        n, k = base + i, i % 2
                        act.wait_ge(s_used, n + 1)
                        a_(prob[:, k, 0:H * C], prob[:, k, 0:H * C], ACT.Exp, scale=float(HD) ** -0.5)\
                            .then_inc(e_ready, 1)
                    if i >= 2:
                        if i + 2 < TILES:
                            act.wait_ge(zT_ps, base + i + 3)
                        turned_o(i - 2, "L2_v_b", 256)
                    if i + 2 < TILES:
                        scaled(base + i + 2, "L2_ln1_w", "L2_ln1_b")

            mlp(0, "L0_postnorm_w", "zero", "L0_mlp_b1", ACT.Gelu_apprx_tanh)
            keys(0, 0)
            tokens(0, 0)
            keys(1, 1)
            tokens(1, 1)
            mlp(1, "L1_ln_mlp_scale", "L1_ln_mlp_offset", "L1_b_fc1", ACT.Gelu)
            attend2(2)
            mlp(2, "L2_ln2_w", "L2_ln2_b", "L2_fc_b", ACT.Gelu_apprx_tanh)
            keys(2, 3)
            tokens(2, 3)
            keys(3, 4)
            tokens(3, 4)
            mlp(3, "L3_ln_mlp_scale", "L3_ln_mlp_offset", "L3_b_fc1", ACT.Gelu)

        @block.vector
        def _(dve):
            v = nc.vector
            steps = [0]

            def link(ins):
                steps[0] += 1
                ins.then_inc(dve_step, 1)
                dve.wait_ge(dve_step, steps[0])

            def copy(out, in_, bias):
                if bias is None:
                    return v.tensor_copy(out, in_)
                return v.tensor_scalar(out, in_, bias, None, ALU.add)

            dve.wait_ge(in_vec, 80)
            v.tensor_copy(copies[:, :, :, :], copies_f).then_inc(copies_ready, 1)
            link(v.tensor_copy(mask[:, 0, :], mask_i[:, :]))
            link(v.tensor_scalar(mask[:, 0, :], mask[:, 0, :], 0.0, MASKED, ALU.is_equal, ALU.mult))
            link(v.tensor_copy(mask[0:1, 1, :], mask_u[:, :]))
            v.tensor_scalar(mask[0:1, 1, :], mask[0:1, 1, :], 0.0, MASKED, ALU.is_equal, ALU.mult).then_inc(mask_ready, 1)

            def split0(t):
                b, m, w = t // 4, t // 2 % 2, t % 2
                width = S if w else KEYS0
                at = slice(KEYS0, KEYS0 + S) if w else slice(0, KEYS0)
                dve.wait_ge(base_copied, t + 1)
                if b >= 1:
                    dve.wait_ge(kq_ps, 2 * (PAIRS * (b - 1) + 4 * m + 3) + w + 1)
                full = kq_full[:, t % 2, 0:width]
                v.tensor_copy(HL[:, m, 0, at], full).then_inc(hl_step, 1)
                dve.wait_ge(hl_step, t + 1)
                v.tensor_tensor(HL[:, m, 1, at], full, HL[:, m, 0, at].bitcast(F32), ALU.subtract).then_inc(hl_ready, 1)

            def job0(n):
                dve.wait_ge(proj_ps, n + 1)
                job_out(dve, copy, n).then_inc(proj_dve, 1)

            split0(0)
            dve.wait_ge(consts_ready, 1)
            v.tensor_copy(ones_r[:, :], ones[:, :]).then_inc(ones_ready, 1)
            split0(1)
            job0(1)

            def max0(n):
                dve.wait_ge(s0_ps, n + 1)
                if n >= 2:
                    dve.wait_ge(p0_ready, n - 1)
                j = 2 * (n % 2)
                link(v.tensor_reduce(nb[:, n % 2, 0, :], ps[:, j:j + 2, 0:KEYS0], AX.X, ALU.max))
                v.tensor_scalar(nb[:, n % 2, 1, :], nb[:, n % 2, 0, :], -1.0 / HD, None, ALU.mult).then_inc(nb_ready, 1)

            def copy0(n):
                dve.wait_ge(t0_ps, n + 1)
                if n >= 2:
                    dve.wait_ge(pv0_ps, n - 1)
                v.tensor_copy(pT[:, n % 2, 0:5, :].rearrange("p c n -> p (c n)"),
                              ps[:, 4:6, :].rearrange("p q n -> p (q n)")[:, 0:5 * P]).then_inc(pt0_ready, 1)

            def invert0(n):
                k = n % 2
                dve.wait_ge(p0_ready, n + 1)
                if n >= 2:
                    dve.wait_ge(w0_pool, n - 1)
                v.reciprocal(rinv[:, k, 0:2], sm[:, k, 0:2]).then_inc(rinv0_ready, 1)

            def rows0(g):
                dve.wait_ge(o_ps, g + 1)
                dve.wait_ge(xb_ready, g + 1)
                v.tensor_tensor(x0[:, g, :], ps[:, 7, 256:512], x0[:, g, :], ALU.add).then_inc(rows_done, 1)

            N = TILES * PAIRS
            for i in range(N + 4):
                if OUT0 <= i < N and i % (2 * PAIRS) in (5, 6):
                    rows0(2 * ((i - OUT0) // (2 * PAIRS)) + i % (2 * PAIRS) - 5)
                step, b = (i - 1) % (2 * PAIRS), (i - 1) // (2 * PAIRS) + 1
                if 12 <= step < 15 and b < B and (3 * b + step - 12) % 2 == 1:
                    job0(3 * b + step - 12)
                if i < N:
                    max0(i)
                if 8 <= step < 12 and b < B:
                    split0(4 * b + step - 8)
                if 1 <= i < 3:
                    split0(i + 1)
                if 1 <= i <= N:
                    invert0(i - 1)
                if 2 <= i < N + 2:
                    copy0(i - 2)
            def spread(src, k, u, rms):
                if rms:
                    link(v.tensor_tensor_reduce(sq[:, :], src, src, 1.0 / D, 0.0, ALU.mult, ALU.add, mv[:, k, u, 1:2]))
                else:
                    link(v.bn_stats(stat[:, k, u, :], src))
                    link(v.bn_aggr(mv[:, k, u, :], stat[:, k, u, :]))
                return v.tensor_scalar(var[:, k, u:u + 1], mv[:, k, u, 1:2], 1e-6 if rms else 1e-5, None, ALU.add)

            def normalise(dst, src, k, u, rms):
                if rms:
                    return v.tensor_scalar(dst, src, rstd[:, k, u:u + 1], None, ALU.mult)
                return v.tensor_scalar(dst, src, mv[:, k, u, 0:1], rstd[:, k, u:u + 1], ALU.subtract, ALU.mult)

            def mlp_spread(l, b):
                src, rms = (x0, True) if l == 0 else (x, False)
                for u in range(2):
                    last = spread(src[:, 2 * b + u, :], b % 2, u, rms)
                last.then_inc(var_ready, 1)

            def mlp_z(l, b):
                src, rms = (x0, True) if l == 0 else (x, False)
                k = b % 2
                if b >= 2:
                    dve.wait_ge(zmT_ps, l * B + b - 1)
                dve.wait_ge(rstd_ready, norms_before(f"M{l}") + b + 1)
                for u in range(2):
                    last = normalise(z[:, k, u, :], src[:, 2 * b + u, :], k, u, rms)
                last.then_inc(zm_ready, 1)

            def values_rest(a, h):
                l, i = ATTN[a]
                n = a * H + h
                dve.wait_ge(v_ready, n + 1)
                v.scalar_tensor_tensor(KT[:, n % 2, 1, 0:B * C], ps[:, n % 2, 0:B * C], col(f"{l}_bk{i}", h),
                                       KT[:, n % 2, 0, 0:B * C].bitcast(F32), ALU.add, ALU.subtract).then_inc(k_rest, 1)
                v.scalar_tensor_tensor(VT[:, n % 2, 1, :], ps[:, n % 2, 256:512], col(f"{l}_bv{i}", h),
                                       VT[:, n % 2, 0, :].bitcast(F32), ALU.add, ALU.subtract).then_inc(v_rest, 1)

            def mlp(l):
                base = l * B
                dve.wait_ge(rows_done, rows_before(f"M{l}"))
                mlp_spread(l, 1)
                mlp_z(l, 1)
                for b in range(B):
                    if b + 2 < B:
                        mlp_spread(l, b + 2)
                        mlp_z(l, b + 2)
                    if l == 1 and b == B - 1:
                        dve.wait_ge(zmT_ps, base + B)
                        dve.wait_ge(rows_done, rows_before("M1") + B // 2 + 1)
                        first_z2()
                    if l % 2 == 0 and b == B - 1:
                        values_rest(l, 0)
                    dve.wait_ge(f2_ps, base + b + 1)
                    dve.wait_ge(xb_ready, TILES * XB_AT[f"M{l}"] + 2 * b + 2)
                    v.tensor_tensor(x[:, 2 * b:2 * b + 2, :], ps[:, 5:7, 0:D], x[:, 2 * b:2 * b + 2, :], ALU.add)\
                        .then_inc(rows_done, 1)

            def first_z2():
                tile_spread(0)
                tile_spread(1)
                for g in range(2):
                    tile_z("L2", 2 * TILES + g, g)
                    tile_spread(g + 2)

            CBP = COLS["cb_parts"][0]

            def keys(a, seq):
                dve.wait_ge(rows_done, rows_before(f"T{a}"))
                tile_spread(0)
                tile_spread(1)
                tile_z(f"T{a}", seq * TILES, 0)
                for h in range(H):
                    n = a * H + h
                    k, par = n % 2, h % 2
                    if h + 1 < H:
                        values_rest(a, h + 1)
                    dve.wait_ge(a_ps, n + 1)
                    slots = slice(0, 4, 3) if par == 0 else slice(1, 3)
                    v.tensor_copy(A[:, 0, :, h // 2, slots, :],
                                  ps[:, 2, 0:B * C].rearrange("p (g s k) -> p g s k", g=2, s=2))
                    link(v.tensor_scalar(cb_round[:, :], ps[0:2, 4, 0:KW], cols[0:2, CBP + 1:CBP + 2], None,
                                         ALU.mult))

                    def parts(dst, lo, hi, fold):
                        return v.scalar_tensor_tensor(dst, fold(ps[0:2, 4, lo:hi]), cols[0:2, CBP:CBP + 1],
                                                      fold(cb_round[:, lo:hi].bitcast(F32)), ALU.mult, ALU.add)

                    for g in range(2):
                        parts(cb[:, g, h // 2, slots, :], 2 * g * C, 2 * (g + 1) * C,
                              lambda ap: ap.rearrange("p (s k) -> p s k", s=2))
                    v.tensor_copy(Ab[:, 0, both_orders(h)], ps[:, 2, B * C:KW])
                    last = parts(cbb[:, both_orders(h)], B * C, KW, lambda ap: ap)
                    last.then_inc(a_ready, 1)
                    dve.wait_ge(vw_ps, n + 1)
                    v.tensor_copy(VW[0:C, par:B:2, h // 2, :], ps[0:C, 5 + k, :].rearrange("p (g n) -> p g n", g=2))\
                        .then_inc(vw_dve, 1)
                dve.wait_ge(vwb_ps, 2 * a + 1)
                v.tensor_copy(VWb[:, 0, :], ps[0:VO, 7, 0:D]).then_inc(vwb_ready, 1)

            def tile_spread(g):
                spread(x[:, g, :], g % 2, 0, False).then_inc(var_ready, 1)

            def tile_z(phase, n, g):
                k = g % 2
                if n >= 2:
                    dve.wait_ge(zT_ps, n - 1)
                dve.wait_ge(rstd_ready, norms_before(phase) + g + 1)
                normalise(z[:, k, 0, :], x[:, g, :], k, 0, False).then_inc(z_ready, 1)

            def tokens(a, seq):
                base = seq * TILES
                for g in range(TILES + 1):
                    if g + 2 < TILES:
                        tile_spread(g + 2)
                    if g + 1 < TILES:
                        tile_z(f"T{a}", base + g + 1, g + 1)
                    if g == TILES and a % 2 == 1:
                        dve.wait_ge(rows_done, rows_before(f"T{a}") + 2)
                        mlp_spread(a, 0)
                    n, k = base + g, g % 2
                    if g < TILES:
                        main = [ps[:, half, :].rearrange("p (h c) -> p h c", c=C) for half in range(2)]
                        dve.wait_ge(s_half, 8 * a + g + 1)
                        v.tensor_reduce(mx[:, k, 0:H // 2], main[0], AX.X, ALU.max)
                    if g >= 1:
                        dve.wait_ge(pT_ps, n)
                        v.tensor_copy(pT[:, 1 - k, 4:8, :], ps[:, 4, :].rearrange("p (c n) -> p c n", c=4))
                        v.tensor_copy(pT[0:VO, 1 - k, 8, :], ps[0:VO, 5, 0:P]).then_inc(pT_dve, 1)
                    if g == TILES and a % 2 == 1:
                        mlp_z(a, 0)
                    if g < TILES:
                        pm = [prob[:, k, half * HALF:(half + 1) * HALF].rearrange("p (h c) -> p h c", c=C)
                              for half in range(2)]
                        pb = prob[:, k, H * C:H * C + H]

                        def of(stats, half):
                            return stats[:, k, half * H // 2:(half + 1) * H // 2].unsqueeze(2)\
                                .broadcast_to([P, H // 2, C])

                        dve.wait_ge(s_ps, n + 1)
                        link(v.tensor_reduce(mx[:, k, H // 2:H], main[1], AX.X, ALU.max))
                        link(v.tensor_tensor(mx2[:, k, :], mx[:, k, :], ps[:, 2, 0:H], ALU.max))
                        v.tensor_tensor(pm[0], main[0], of(mx2, 0), ALU.subtract).then_inc(sub_half, 1)
                        v.tensor_tensor(pm[1], main[1], of(mx2, 1), ALU.subtract)
                        v.tensor_tensor(pb, ps[:, 2, 0:H], mx2[:, k, :], ALU.subtract).then_inc(s_used, 1)
                        if g == 0:
                            dve.wait_ge(vwb_ps, 2 * a + 2)
                            v.tensor_copy(VWb[:, 1, :], ps[0:VO, 6, 0:D]).then_inc(vwb_ready, 1)
                        dve.wait_ge(e_half, 8 * a + g + 1)
                        v.tensor_reduce(sm[:, k, 0:H // 2], pm[0], AX.X, ALU.add)
                        dve.wait_ge(e_ready, n + 1)
                        link(v.tensor_reduce(sm[:, k, H // 2:H], pm[1], AX.X, ALU.add))
                        link(v.tensor_tensor(sm[:, k, :], sm[:, k, :], pb, ALU.add))
                        v.reciprocal(rinv[:, k, :], sm[:, k, :]).then_inc(rinv_ready, 1)
                        dve.wait_ge(rinv_ready, 8 * a + g + 1)
                        v.tensor_tensor(pm[1], pm[1], of(rinv, 1), ALU.mult).then_inc(p_half, 1)
                    if g == TILES and a % 2 == 0:
                        values_rest(a + 1, 0)
                    if g >= 1:
                        dve.wait_ge(o_ps, TILES + base + g)
                        v.tensor_tensor(x[:, g - 1, :], ps[:, 6, 0:D], x[:, g - 1, :], ALU.add).then_inc(rows_done, 1)

            def attend2(seq):
                base = seq * TILES
                dve.wait_ge(rows_done, rows_before("L2"))
                dve.wait_ge(kc_clear, 1)
                for n in range(NJ0 + 1, NJ, 2):
                    dve.wait_ge(proj_ps, n + 1)
                    job_out(dve, copy, n).then_inc(proj_dve, 1)

                def queries(g):
                    dve.wait_ge(q_ps, g + 1)
                    v.tensor_tensor(qT2[:, g % 2, :, :], ps[:, 4, :].rearrange("p (m n) -> p m n", m=4),
                                    col("L2_q_b", 0, 4).unsqueeze(2).broadcast_to([P, 4, P]), ALU.add)\
                        .then_inc(q_ready, 1)

                def values(g):
                    k = g % 2
                    dve.wait_ge(pv_ps, g + 1)
                    o = ps[:, 0:2, 256:256 + PAIRS * VO].rearrange("p q (h c) -> p q h c", h=PAIRS)
                    rk = rinv[:, k, :].rearrange("p (q h) -> p q h", q=2)
                    link(v.reciprocal(rk, o[:, :, :, HD]))
                    v.tensor_tensor(on[:, k, :].rearrange("p (q h c) -> p q h c", q=2, h=PAIRS), o[:, :, :, 0:HD],
                                    rk.unsqueeze(3).broadcast_to([P, 2, PAIRS, HD]), ALU.mult).then_inc(on_ready, 1)

                tile_z("L2", base + 2, 2)
                queries(0)
                for i in range(TILES + 3):
                    if i < TILES:
                        dve.wait_ge(s_ps, base + i + 1)
                    if 2 <= i < TILES + 2:
                        values(i - 2)
                    if i < TILES:
                        k = i % 2
                        main = ps[:, 0:4, 0:4 * C].rearrange("p m (j c) -> p m j c", c=C)
                        mj = mx[:, k, :].rearrange("p (m j) -> p m j", m=4)
                        pm = prob[:, k, 0:H * C].rearrange("p (m j c) -> p m j c", m=4, j=4)
                        link(v.tensor_reduce(mj, main, AX.X, ALU.max))
                        v.tensor_tensor(pm, main, mj.unsqueeze(3).broadcast_to([P, 4, 4, C]), ALU.subtract)\
                            .then_inc(s_used, 1)
                    if i == TILES:
                        dve.wait_ge(rows_done, rows_before("L2") + 2)
                        mlp_spread(2, 0)
                    if i == TILES + 1:
                        mlp_z(2, 0)
                    if i >= 3:
                        g = i - 3
                        dve.wait_ge(o_ps, TILES + base + g + 1)
                        dve.wait_ge(xb_ready, TILES * XB_AT["L2"] + g + 1)
                        v.tensor_tensor(x[:, g, :], ps[:, 3, 256:512], x[:, g, :], ALU.add).then_inc(rows_done, 1)
                    if i + 1 < TILES:
                        queries(i + 1)
                    if i + 4 < TILES:
                        tile_spread(i + 4)
                    if i + 3 < TILES:
                        tile_z("L2", base + i + 3, i + 3)

            XB_AT = {"M0": 1, "M1": 2, "L2": 3, "M2": 4, "M3": 5}
            dve.wait_ge(rows_done, 2)
            mlp_spread(0, 0)
            rows0(TILES - 2)
            mlp_z(0, 0)
            rows0(TILES - 1)
            mlp(0)
            keys(0, 0)
            tokens(0, 0)
            keys(1, 1)
            tokens(1, 1)
            mlp(1)
            attend2(2)
            mlp(2)
            keys(2, 3)
            tokens(2, 3)
            keys(3, 4)
            tokens(3, 4)
            mlp(3)


def _halves(w):
    return np.ascontiguousarray(np.asarray(w).reshape(-1, P, w.shape[-1]).transpose(1, 0, 2))


def _padded(w):
    out = np.zeros((w.shape[0], H, 32), w.dtype)
    out[:, :, :HD] = w.reshape(w.shape[0], H, HD)
    return out.reshape(w.shape[0], H * 32)


def _copies():
    out = np.zeros((4, 2, HD, 2, 2, 2, 4, HD), np.float32)
    for w, blocks in enumerate(("HLH", "HHL")):
        for j, part in enumerate(blocks):
            for e in range(2):
                for c in range(HD):
                    out[:, e, c, w, "HL".index(part), e, j, c] = 1.0
    return out.reshape(P, 2, 2, P)


def _padded_bias(v, row16):
    out = np.zeros((H, 32), v.dtype)
    out[:, :HD] = v.reshape(H, HD)
    out[:, HD] = row16
    return out.reshape(4, P).T


def _layout(i):
    i = {k.replace("_xattn_", "_"): np.asarray(v) for k, v in i.items()}
    f = np.float32
    kvw = i["L0_kv_w"].reshape(D, D, 2)
    kvb = i["L0_kv_b"].reshape(D, 2)
    kin = np.concatenate([i["ctx_2048"], i["x"]], axis=1)
    kinT = _halves(np.ascontiguousarray(kin.reshape(B * KEYS0, D).T)).reshape(P, DH, B, KEYS0)
    cT = np.ascontiguousarray(i["ctx_2048"].reshape(B * C, D).T)
    cTs = np.ascontiguousarray(cT.reshape(D, 2, 2, C)[:, :, ::-1].reshape(D, B * C))
    cD = np.repeat(cT.reshape(D, B, 1, C), 2, axis=2).reshape(D, B * 2 * C)
    cols = np.zeros((P, NCOLS), f)
    for name, (at, n) in COLS.items():
        if name == "zero":
            continue
        if name == "cb_parts":
            v = np.zeros((P, 2), f)
            v[0:2] = ((0.0, 1.0), (1.0, -1.0))
        elif name == "row48":
            v = np.zeros((P, 1), f)
            v[48::C] = 1.0
        elif "_bq" in name:
            v = np.repeat(i[name].reshape(H, P), 2, axis=0).T
        elif name == "L0_k_b":
            v = kvb[:, 0].reshape(n, P).T
        elif name == "L0_v_b":
            v = kvb[:, 1].reshape(n, P).T
        elif name == "L2_q_b":
            v = _padded_bias(i[name], 1.0)
        elif name == "L2_k_b":
            v = _padded_bias(i[name], 0.0)
        else:
            v = i[name].reshape(n, P).T
        cols[:, at:at + n] = v
    brow = np.stack([i[r] for r in ROWS])
    heads = np.zeros((4, H, P, WIDTH), f)
    bvz = np.zeros((4, P, H, VO), f)
    for a, (l, k) in enumerate(ATTN):
        wk = i[f"{l}_wk{k}"].reshape(DH, P, H, HK).transpose(2, 1, 0, 3).reshape(H, P, D)
        wv = i[f"{l}_wv{k}"].reshape(DH, P, H, HK).transpose(2, 1, 0, 3).reshape(H, P, D)
        wqT = i[f"{l}_wq{k}"].T.reshape(H, HK, D)
        wo = i[f"{l}_wo{k}"].reshape(H, HK, D)
        heads[a] = np.concatenate([wk, wv, wqT, wo], axis=2)
        bv = i[f"{l}_bias_v{k}"].reshape(H, HK)
        for h in range(H):
            bvz[a, :, h, h] = bv[h]
    return {
        "ctxT": np.stack([_halves(cT), _halves(cTs)], axis=1),
        "ctxD": _halves(cD).reshape(P, DH, B, 2 * C),
        "kinT": kinT,
        "x": np.ascontiguousarray(i["x"].reshape(TILES, P, D).transpose(1, 0, 2)),
        "cols": cols,
        "mask_i": i["mask_BxS2_ik0"].reshape(1, B * C),
        "mask_u": np.ascontiguousarray(i["mask_BxS2_bf1"]).view(np.uint8).reshape(1, B * C),
        "bo": np.stack([i[f"{l}_bo{k}"] for l, k in ATTN])[None],
        "w0": np.stack([_halves(np.ascontiguousarray(kvw[:, :, 0])), _halves(i["L0_q_w"])], axis=1),
        "copies": _copies(),
        "vw0": _halves(np.ascontiguousarray(kvw[:, :, 1])),
        "ow0": _halves(i["L0_out_w"]),
        "wp2": _halves(np.concatenate([_padded(i["L2_q_w"]), _padded(i["L2_k_w"])], axis=1)),
        "vw2": np.stack([_halves(i["L2_v_w"]), _halves(i["L2_cproj_w"])], axis=1),
        "brow": brow,
        "w1": np.stack([_halves(i[k]) for k in ("L0_mlp_w1", "L1_w_fc1", "L2_fc_w", "L3_w_fc1")]),
        "w2": np.stack([_halves(i[k]) for k in ("L0_mlp_w2", "L1_w_fc2", "L2_proj_w", "L3_w_fc2")]),
        "bvz": bvz,
        "heads": heads,
    }


def kernel(**inputs):
    import concourse.bacc as bacc
    from concourse.bass_utils import run_bass_kernel_spmd

    nc = bacc.Bacc("TRN2", target_bir_lowering=False, num_devices=1)
    arrays, t = {}, {}
    for name, a in _layout(inputs).items():
        a = np.ascontiguousarray(a)
        arrays[f"in_{name}_dram"] = a
        t[name] = nc.dram_tensor(f"in_{name}_dram", a.shape, mybir.dt.from_np(a.dtype), kind="ExternalInput").ap()
    t["mask_i"] = t["mask_i"].broadcast_to([P, B * C])
    t["brow"] = t["brow"].unsqueeze(0).broadcast_to([P, len(ROWS), D])
    out = nc.dram_tensor("out_0_dram", (B, S, D), F32, kind="ExternalOutput").ap()
    t["out"] = [out[b].rearrange("(u p) n -> p u n", p=P) for b in range(B)]
    build(nc, t)
    r = run_bass_kernel_spmd(nc, [arrays], core_ids=[0])
    return r.results[0]["out_0_dram"]
```
